# Optimizing a Trainium2 kernel written in Bass

```python
import numpy as np
import jax
import jax.numpy as jnp

def _softmax(x, axis=-1):
    return jax.nn.softmax(x, axis=axis)

def _gelu(x):
    return jax.nn.gelu(x, approximate=True)

def _silu(x):
    return jax.nn.silu(x)

def _sigmoid(x):
    return jax.nn.sigmoid(x)

def _layernorm(x, axis=-1, eps=1e-05):
    m = jnp.mean(x, axis=axis, keepdims=True)
    v = jnp.var(x, axis=axis, keepdims=True)
    return (x - m) / jnp.sqrt(v + eps)

def _scatter_add(tgt, idx, src, axis=0):
    return tgt.at[idx].add(src)

def _segment_sum(src, seg, n):
    return jax.ops.segment_sum(src, seg, n)
kernel_name = 'mk_xattn_ffn_d2_seqx_r8_53117a'

def setup_inputs(seed: int=0):
    np.random.seed(seed)
    _w = jnp.asarray

    def _rec_inputs():
        import jax
        import jax.numpy as jnp
        _rk = jax.random.key(seed)
        x = 7.22e-05 + 1 * jax.random.normal(jax.random.fold_in(_rk, 1), (8, 256, 256), jnp.float32)
        _lenS = 256 - jax.random.randint(jax.random.fold_in(_rk, 7), (8,), 0, max(1, 256 // 4) + 1, jnp.int32)
        _lenS2 = 1601 - jax.random.randint(jax.random.fold_in(_rk, 8), (8,), 0, max(1, 1601 // 4) + 1, jnp.int32)
        _ctx_2048P = jax.random.normal(jax.random.fold_in(_rk, 11), (8, 16, 256), jnp.float32)
        _ctx_2048c = jax.random.dirichlet(jax.random.fold_in(_rk, 511), 0.3 * jnp.ones((16,), jnp.float32), (8, 1601))
        _ctx_2048t = jnp.einsum('bsk,bkd->bsd', _ctx_2048c, _ctx_2048P)
        _ctx_2048t = _ctx_2048t * jax.lax.rsqrt(jnp.mean(jnp.square(_ctx_2048t)) + 1e-12) * 0.953939
        ctx_2048 = -0.000514642 + 1.00011 * (_ctx_2048t + 0.3 * jax.random.normal(jax.random.fold_in(_rk, 611), (8, 1601, 256), jnp.float32))
        _validS = jnp.arange(256)[None, :] < _lenS[:, None]
        _validS2 = jnp.arange(1601)[None, :] < _lenS2[:, None]
        _causal = jnp.tril(jnp.ones((256, 256), dtype=bool))
        mask_BxS2_bk0 = jnp.logical_not(jnp.broadcast_to(_validS2[:, :], (8, 1601)))
        return (x, ctx_2048, mask_BxS2_bk0)
    x, ctx_2048, mask_BxS2_bk0 = _rec_inputs()

    def _L0_xattn_setup():
        import jax, jax.numpy as jnp
        import numpy as np
        HIDDEN = 256
        NUM_HEADS = 16
        NUM_KV_HEADS = 4
        HEAD_DIM = 128
        ROPE_THETA = 10000.0
        EPS = 1e-06

        def rms_norm(x, w, eps=EPS):
            var = jnp.mean(jnp.square(x), axis=-1, keepdims=True)
            return x * jax.lax.rsqrt(var + eps) * w

        def rope_cache(L, head_dim, theta, dtype):
            inv_freq = 1.0 / theta ** (jnp.arange(0, head_dim, 2, dtype=jnp.float32) / head_dim)
            t = jnp.arange(L, dtype=jnp.float32)
            freqs = jnp.outer(t, inv_freq)
            emb = jnp.concatenate([freqs, freqs], -1)
            cos = jnp.cos(emb).astype(dtype)[None, :, None, :]
            sin = jnp.sin(emb).astype(dtype)[None, :, None, :]
            return (cos, sin)

        def rotate_half(x):
            x1, x2 = jnp.split(x, 2, axis=-1)
            return jnp.concatenate([-x2, x1], axis=-1)
        key = jax.random.key(seed)
        ks = jax.random.split(key, 10)
        B, L, T = (2, 256, 64)
        q_out = NUM_HEADS * HEAD_DIM
        kv_out = NUM_KV_HEADS * HEAD_DIM
        s = lambda fan_in: 1.0 / np.sqrt(fan_in)
        return {'x': jax.random.normal(ks[0], (B, L, HIDDEN), jnp.float32), 'h_ctx_kv': jax.random.normal(ks[1], (B, T, HIDDEN), jnp.float32), 'wq': jax.random.normal(ks[2], (HIDDEN, q_out), jnp.float32) * s(HIDDEN), 'wk': jax.random.normal(ks[3], (HIDDEN, kv_out), jnp.float32) * s(HIDDEN), 'wv': jax.random.normal(ks[4], (HIDDEN, kv_out), jnp.float32) * s(HIDDEN), 'wo': jax.random.normal(ks[5], (q_out, HIDDEN), jnp.float32) * s(q_out), 'wk_ctx': jax.random.normal(ks[6], (HIDDEN, kv_out), jnp.float32) * s(HIDDEN), 'wv_ctx': jax.random.normal(ks[7], (HIDDEN, kv_out), jnp.float32) * s(HIDDEN), 'q_norm_w': jnp.ones((HEAD_DIM,), jnp.float32), 'k_norm_w': jnp.ones((HEAD_DIM,), jnp.float32)}
    _L0_xattn_all = _L0_xattn_setup()
    _L0_xattn_in = {k: v for k, v in _L0_xattn_all.items() if k in ('wq', 'wk', 'wv', 'wo', 'wk_ctx', 'wv_ctx', 'q_norm_w', 'k_norm_w')}
    del _L0_xattn_all

    def _L0_ffn_setup():
        import jax, jax.numpy as jnp
        import numpy as np
        NUM_EXPERTS = 8
        TOP_K = 2
        ROUTE_SCALE = 1.0
        DIM = 256
        HIDDEN = 128
        BATCH, SEQ = (4, 64)

        def _moe(x, gate, expert_bias, w1, w2, w3, shared_w1, shared_w2, shared_w3):
            bs, slen, dim = x.shape
            xt = x.reshape(-1, dim)
            scores = jax.nn.sigmoid((xt @ gate.T).astype(jnp.float32))
            _, sel = jax.lax.top_k(scores + expert_bias[None, :], TOP_K)
            top_scores = jnp.take_along_axis(scores, sel, axis=1) * ROUTE_SCALE
            flat_sel = sel.reshape(-1)
            order = jnp.argsort(flat_sel, stable=True)
            scores_sorted = top_scores.reshape(-1)[order]
            token_idx = order // TOP_K
            expert_ids = flat_sel[order]
            routed = xt[token_idx]
            routed = (routed.astype(jnp.float32) * scores_sorted[:, None]).astype(x.dtype)
            xb = routed.astype(jnp.bfloat16)
            out_r = jnp.zeros_like(routed)
            for e in range(NUM_EXPERTS):
                w1e = w1[e].astype(jnp.bfloat16)
                w2e = w2[e].astype(jnp.bfloat16)
                w3e = w3[e].astype(jnp.bfloat16)
                h = jax.nn.silu(xb @ w1e.T) * (xb @ w3e.T)
                oe = (h @ w2e.T).astype(routed.dtype)
                out_r = out_r + jnp.where((expert_ids == e)[:, None], oe, 0.0)
            hs = jax.nn.silu(xt @ shared_w1.T) * (xt @ shared_w3.T)
            out = hs @ shared_w2.T
            out = out.at[token_idx].add(out_r)
            return out.reshape(bs, slen, dim)
        key = jax.random.key(seed)
        ks = jax.random.split(key, 9)
        s = 0.02
        return {'x': jax.random.normal(ks[0], (BATCH, SEQ, DIM), jnp.float32), 'gate': jax.random.normal(ks[1], (NUM_EXPERTS, DIM), jnp.float32) * s, 'expert_bias': jnp.zeros((NUM_EXPERTS,), jnp.float32), 'w1': jax.random.normal(ks[2], (NUM_EXPERTS, HIDDEN, DIM), jnp.float32) * s, 'w2': jax.random.normal(ks[3], (NUM_EXPERTS, DIM, HIDDEN), jnp.float32) * s, 'w3': jax.random.normal(ks[4], (NUM_EXPERTS, HIDDEN, DIM), jnp.float32) * s, 'shared_w1': jax.random.normal(ks[5], (HIDDEN, DIM), jnp.float32) * s, 'shared_w2': jax.random.normal(ks[6], (DIM, HIDDEN), jnp.float32) * s, 'shared_w3': jax.random.normal(ks[7], (HIDDEN, DIM), jnp.float32) * s}
    _L0_ffn_all = _L0_ffn_setup()
    _L0_ffn_in = {k: v for k, v in _L0_ffn_all.items() if k in ('gate', 'expert_bias', 'w1', 'w2', 'w3', 'shared_w1', 'shared_w2', 'shared_w3')}
    del _L0_ffn_all

    def _L1_xattn_setup():
        import jax, jax.numpy as jnp
        import numpy as np
        key = jax.random.key(seed)
        k1, k2, k3 = jax.random.split(key, 3)
        B, S, D, M = (8, 256, 256, 128)
        hidden_states = jax.random.normal(k1, (B, S, D), dtype=jnp.float32)
        memory_tokens = jax.random.normal(k2, (B, M, D), dtype=jnp.float32)
        memory_mask = jax.random.randint(k3, (B, M), 0, 2).astype(jnp.bool_)
        return {'hidden_states': hidden_states, 'memory_tokens': memory_tokens, 'memory_mask': memory_mask}
    _L1_xattn_all = _L1_xattn_setup()
    _L1_xattn_in = {k: v for k, v in _L1_xattn_all.items() if k in ()}
    del _L1_xattn_all

    def _L1_ffn_setup():
        import jax, jax.numpy as jnp
        import numpy as np
        H, I, E = (256, 512, 8)
        B, S = (2, 256)
        key = jax.random.key(seed)
        ks = jax.random.split(key, 5)
        scale = 0.02
        return {'hidden_states': jax.random.normal(ks[0], (B, S, H), dtype=jnp.float32), 'router_w': jax.random.normal(ks[1], (H, E), dtype=jnp.float32) * scale, 'gate_w': jax.random.normal(ks[2], (E, H, I), dtype=jnp.float32) * scale, 'up_w': jax.random.normal(ks[3], (E, H, I), dtype=jnp.float32) * scale, 'down_w': jax.random.normal(ks[4], (E, I, H), dtype=jnp.float32) * scale}
    _L1_ffn_all = _L1_ffn_setup()
    _L1_ffn_in = {k: v for k, v in _L1_ffn_all.items() if k in ('router_w', 'gate_w', 'up_w', 'down_w')}
    del _L1_ffn_all
    return {'x': x, 'ctx_2048': ctx_2048, 'mask_BxS2_bk0': mask_BxS2_bk0, 'L0_xattn_wq': _L0_xattn_in['wq'], 'L0_xattn_wk': _L0_xattn_in['wk'], 'L0_xattn_wv': _L0_xattn_in['wv'], 'L0_xattn_wo': _L0_xattn_in['wo'], 'L0_xattn_wk_ctx': _L0_xattn_in['wk_ctx'], 'L0_xattn_wv_ctx': _L0_xattn_in['wv_ctx'], 'L0_xattn_q_norm_w': _L0_xattn_in['q_norm_w'], 'L0_xattn_k_norm_w': _L0_xattn_in['k_norm_w'], 'L0_ffn_gate': _L0_ffn_in['gate'], 'L0_ffn_expert_bias': _L0_ffn_in['expert_bias'], 'L0_ffn_w1': _L0_ffn_in['w1'], 'L0_ffn_w2': _L0_ffn_in['w2'], 'L0_ffn_w3': _L0_ffn_in['w3'], 'L0_ffn_shared_w1': _L0_ffn_in['shared_w1'], 'L0_ffn_shared_w2': _L0_ffn_in['shared_w2'], 'L0_ffn_shared_w3': _L0_ffn_in['shared_w3'], 'L1_ffn_router_w': _L1_ffn_in['router_w'], 'L1_ffn_gate_w': _L1_ffn_in['gate_w'], 'L1_ffn_up_w': _L1_ffn_in['up_w'], 'L1_ffn_down_w': _L1_ffn_in['down_w']}

def reference(x, ctx_2048, mask_BxS2_bk0, L0_xattn_wq, L0_xattn_wk, L0_xattn_wv, L0_xattn_wo, L0_xattn_wk_ctx, L0_xattn_wv_ctx, L0_xattn_q_norm_w, L0_xattn_k_norm_w, L0_ffn_gate, L0_ffn_expert_bias, L0_ffn_w1, L0_ffn_w2, L0_ffn_w3, L0_ffn_shared_w1, L0_ffn_shared_w2, L0_ffn_shared_w3, L1_ffn_router_w, L1_ffn_gate_w, L1_ffn_up_w, L1_ffn_down_w):
    import jax
    import jax.numpy as jnp

    def _L0_xattn_ref(x, h_ctx_kv, wq, wk, wv, wo, wk_ctx, wv_ctx, q_norm_w, k_norm_w):
        import jax, jax.numpy as jnp
        import numpy as np
        HIDDEN = 256
        NUM_HEADS = 16
        NUM_KV_HEADS = 4
        HEAD_DIM = 128
        ROPE_THETA = 10000.0
        EPS = 1e-06

        def rms_norm(x, w, eps=EPS):
            var = jnp.mean(jnp.square(x), axis=-1, keepdims=True)
            return x * jax.lax.rsqrt(var + eps) * w

        def rope_cache(L, head_dim, theta, dtype):
            inv_freq = 1.0 / theta ** (jnp.arange(0, head_dim, 2, dtype=jnp.float32) / head_dim)
            t = jnp.arange(L, dtype=jnp.float32)
            freqs = jnp.outer(t, inv_freq)
            emb = jnp.concatenate([freqs, freqs], -1)
            cos = jnp.cos(emb).astype(dtype)[None, :, None, :]
            sin = jnp.sin(emb).astype(dtype)[None, :, None, :]
            return (cos, sin)

        def rotate_half(x):
            x1, x2 = jnp.split(x, 2, axis=-1)
            return jnp.concatenate([-x2, x1], axis=-1)
        B, L, _ = x.shape
        T = h_ctx_kv.shape[1]
        rep = NUM_HEADS // NUM_KV_HEADS
        q = (x @ wq).reshape(B, L, NUM_HEADS, HEAD_DIM)
        k = (x @ wk).reshape(B, L, NUM_KV_HEADS, HEAD_DIM)
        v = (x @ wv).reshape(B, L, NUM_KV_HEADS, HEAD_DIM)
        q = rms_norm(q, q_norm_w)
        k = rms_norm(k, k_norm_w)
        k_ctx = (h_ctx_kv @ wk_ctx).reshape(B, T, NUM_KV_HEADS, HEAD_DIM)
        v_ctx = (h_ctx_kv @ wv_ctx).reshape(B, T, NUM_KV_HEADS, HEAD_DIM)
        k_ctx = rms_norm(k_ctx, k_norm_w)
        cos, sin = rope_cache(L, HEAD_DIM, ROPE_THETA, x.dtype)
        q = q * cos + rotate_half(q) * sin
        k = k * cos + rotate_half(k) * sin
        k_full = jnp.concatenate([k_ctx, k], axis=1)
        v_full = jnp.concatenate([v_ctx, v], axis=1)
        k_full = jnp.repeat(k_full, rep, axis=2)
        v_full = jnpp_repeat = jnp.repeat(v_full, rep, axis=2)
        i = jnp.arange(L)[:, None]
        j = jnp.arange(L)[None, :]
        causal = jnp.where(j > i, -jnp.inf, 0.0).astype(x.dtype)
        mask = jnp.concatenate([jnp.zeros((L, T), x.dtype), causal], axis=1)
        scale = 1.0 / np.sqrt(HEAD_DIM)
        scores = jnp.einsum('blhd,bmhd->bhlm', q, k_full) * scale + mask
        probs = jax.nn.softmax(scores, axis=-1)
        out = jnp.einsum('bhlm,bmhd->blhd', probs, v_full)
        out = out.reshape(B, L, NUM_HEADS * HEAD_DIM)
        return out @ wo

    def _L0_ffn_ref(x, gate, expert_bias, w1, w2, w3, shared_w1, shared_w2, shared_w3):
        import jax, jax.numpy as jnp
        import numpy as np
        NUM_EXPERTS = 8
        TOP_K = 2
        ROUTE_SCALE = 1.0
        DIM = 256
        HIDDEN = 128
        BATCH, SEQ = (4, 64)

        def _moe(x, gate, expert_bias, w1, w2, w3, shared_w1, shared_w2, shared_w3):
            bs, slen, dim = x.shape
            xt = x.reshape(-1, dim)
            scores = jax.nn.sigmoid((xt @ gate.T).astype(jnp.float32))
            _, sel = jax.lax.top_k(scores + expert_bias[None, :], TOP_K)
            top_scores = jnp.take_along_axis(scores, sel, axis=1) * ROUTE_SCALE
            flat_sel = sel.reshape(-1)
            order = jnp.argsort(flat_sel, stable=True)
            scores_sorted = top_scores.reshape(-1)[order]
            token_idx = order // TOP_K
            expert_ids = flat_sel[order]
            routed = xt[token_idx]
            routed = (routed.astype(jnp.float32) * scores_sorted[:, None]).astype(x.dtype)
            xb = routed.astype(jnp.bfloat16)
            out_r = jnp.zeros_like(routed)
            for e in range(NUM_EXPERTS):
                w1e = w1[e].astype(jnp.bfloat16)
                w2e = w2[e].astype(jnp.bfloat16)
                w3e = w3[e].astype(jnp.bfloat16)
                h = jax.nn.silu(xb @ w1e.T) * (xb @ w3e.T)
                oe = (h @ w2e.T).astype(routed.dtype)
                out_r = out_r + jnp.where((expert_ids == e)[:, None], oe, 0.0)
            hs = jax.nn.silu(xt @ shared_w1.T) * (xt @ shared_w3.T)
            out = hs @ shared_w2.T
            out = out.at[token_idx].add(out_r)
            return out.reshape(bs, slen, dim)
        return _moe(x, gate, expert_bias, w1, w2, w3, shared_w1, shared_w2, shared_w3)

    def _L1_xattn_ref(hidden_states, memory_tokens, memory_mask):
        import jax, jax.numpy as jnp
        import numpy as np
        B, S, D = hidden_states.shape
        scale = 1.0 / jnp.sqrt(jnp.asarray(D, hidden_states.dtype))
        scores = jnp.einsum('bsd,bmd->bsm', hidden_states, memory_tokens) * scale
        neg_inf = jnp.asarray(-1e+30, scores.dtype)
        scores = jnp.where(memory_mask[:, None, :], scores, neg_inf)
        attn = jax.nn.softmax(scores, axis=-1)
        readout = jnp.einsum('bsm,bmd->bsd', attn, memory_tokens)
        valid_b = jnp.any(memory_mask, axis=-1)
        out = jnp.where(valid_b[:, None, None], readout, jnp.zeros_like(readout))
        return out

    def _L1_ffn_ref(hidden_states, router_w, gate_w, up_w, down_w):
        import jax, jax.numpy as jnp
        import numpy as np
        H, I, E = (256, 512, 8)
        B, S = (2, 256)
        hidden_shape = hidden_states.shape
        x = hidden_states.reshape(-1, hidden_shape[-1])
        route = jax.nn.sigmoid(x @ router_w)
        max_ind = jnp.argmax(route, axis=1)
        max_prob = jnp.take_along_axis(route, max_ind[:, None], axis=1)
        out = jnp.zeros_like(x)
        num_experts = gate_w.shape[0]
        for e in range(num_experts):
            mask = (max_ind == e)[:, None]
            h = jax.nn.silu(x @ gate_w[e]) * (x @ up_w[e])
            out = out + jnp.where(mask, h @ down_w[e], 0.0)
        out = out * max_prob
        return out.reshape(hidden_shape)
    x = x + _L0_xattn_ref(_layernorm(x, axis=-1), ctx_2048, L0_xattn_wq, L0_xattn_wk, L0_xattn_wv, L0_xattn_wo, L0_xattn_wk_ctx, L0_xattn_wv_ctx, L0_xattn_q_norm_w, L0_xattn_k_norm_w)
    x = x + _L0_ffn_ref(_layernorm(x, axis=-1), L0_ffn_gate, L0_ffn_expert_bias, L0_ffn_w1, L0_ffn_w2, L0_ffn_w3, L0_ffn_shared_w1, L0_ffn_shared_w2, L0_ffn_shared_w3)
    x = x + _L1_xattn_ref(_layernorm(x, axis=-1), ctx_2048, mask_BxS2_bk0)
    x = x + _L1_ffn_ref(_layernorm(x, axis=-1), L1_ffn_router_w, L1_ffn_gate_w, L1_ffn_up_w, L1_ffn_down_w)
    return x

_drawn_inputs = setup_inputs


def setup_inputs(seed=0):
    import zlib

    import numpy as np

    out = dict(_drawn_inputs(seed))
    spreads = {'L0_xattn_q_norm_w': (1.0, 0.2),
     'L0_xattn_k_norm_w': (1.0, 0.538),
     'L0_ffn_expert_bias': (0.0, 0.8)}
    factors = {'L0_xattn_wk': 4.159,
     'L0_xattn_wv': 3.873,
     'L0_ffn_gate': 8.0,
     'L0_ffn_w1': 8.0,
     'L0_ffn_w2': 8.0,
     'L0_ffn_w3': 8.0,
     'L0_ffn_shared_w1': 5.718,
     'L0_ffn_shared_w2': 5.568,
     'L0_ffn_shared_w3': 5.557,
     'L1_ffn_router_w': 5.303,
     'L1_ffn_gate_w': 4.944,
     'L1_ffn_up_w': 4.913,
     'L1_ffn_down_w': 4.912}
    for name, (base, spread) in spreads.items():
        noise = np.random.default_rng([zlib.crc32(name.encode()), seed]).standard_normal(out[name].shape)
        drawn = base * np.exp(spread * noise) if base else spread * noise
        out[name] = jnp.asarray(drawn.astype(out[name].dtype))
    for name, factor in factors.items():
        out[name] = (out[name] * factor).astype(out[name].dtype)
    return out
```

```python
from contextlib import ExitStack

import concourse.bass as bass
from concourse import mybir

F32 = mybir.dt.float32
F32R = mybir.dt.float32r
BF16 = mybir.dt.bfloat16
U32 = mybir.dt.uint32
U8 = mybir.dt.uint8
ALU = mybir.AluOpType
ACT = mybir.ActivationFunctionType
AX = mybir.AxisListType

P = 128
B, L, D = 8, 256, 256
T = 1601
NH, NKV, HD = 16, 4, 128
GRP = NH // NKV
DC = D // P
TOK = B * L
NT = TOK // P
QT = L // P
CT = -(-T // P)
TP = CT * P
KB = QT + CT
NK = KB * P
NKV_USED = QT * P + T
BG = B * NKV
NEG = -1.0e30
ROW = 1.0 / HD
E0, H0 = 8, 128
E1, H1 = 8, 512
HC1 = H1 // P


def scope(ctx, nc):
    sems = []

    def sb(name, shape, dt=F32):
        return ctx.enter_context(nc.sbuf_tensor(name, shape, dt))

    def psum(name, shape, dt=F32):
        return ctx.enter_context(nc.psum_tensor(name, shape, dt))

    def sem(name):
        sems.append(ctx.enter_context(nc.semaphore(name)))
        return sems[-1]

    def clear(error, *_):
        if error:
            return
        nums = sorted(s.num for s in sems)
        with nc.Block() as block:
            @block.gpsimd
            def _(pool):
                first = 0
                for n in range(len(nums)):
                    if n + 1 == len(nums) or nums[n + 1] != nums[n] + 1:
                        pool.sem_clear(range(nums[first], nums[n] + 1))
                        first = n + 1

    ctx.push(clear)
    return sb, psum, sem


def positive(count):
    return not (isinstance(count, int) and count <= 0)


def norm_memory(sb, sem, name):
    return (sb(name + "_stats", [P, NT, 6]), sb(name + "_var_eps", [P, NT]),
            sem(name + "_stats_ready"), sem(name + "_var_ready"), sem(name + "_eps_added"), sem(name + "_rstd_ready"))


def norm_mean_var(nc, dve, x_sb, mean_var, memory):
    stats, _, stats_ready, var_ready, _, _ = memory
    for t in range(NT):
        nc.vector.bn_stats(stats[:, t, :], x_sb[:, t, :]).then_inc(stats_ready, 1)
    for t in range(NT):
        dve.wait_ge(stats_ready, t + 1)
        nc.vector.bn_aggr(mean_var[:, t, :], stats[:, t, :]).then_inc(var_ready, 1)


def norm_rstd(nc, pool, mean_var, rstd, half, memory):
    _, var_eps, _, var_ready, eps_added, rstd_ready = memory
    pool.wait_ge(var_ready, NT)
    nc.gpsimd.tensor_scalar(var_eps[:, :], mean_var[:, :, 1], LN_EPS, 1.0, ALU.add, ALU.mult).then_inc(eps_added, 1)
    pool.wait_ge(eps_added, 1)
    nc.gpsimd.tensor_tensor(rstd[:, :], var_eps[:, :], half[:, 0:NT], ALU.pow).then_inc(rstd_ready, 1)


GRAN = 1 + NKV
W1 = (2 * NKV + NH) * HD
LN_EPS, RMS_EPS = 1e-5, 1e-6


def self_projections(nc, x_sb, x_loaded, ident_loaded, half_made, w_dram, rope_dram, qw_dram, kw_dram, q_dram, k_dram, v_dram,
                     mean_var, rstd, half, ident):
    wq_d, wk_d, wv_d = w_dram
    with ExitStack() as ctx:
        sb, psum, sem = scope(ctx, nc)
        norm = norm_memory(sb, sem, "norm1")
        w_raw = sb("w1_raw", [P, DC, W1])
        w_hi = sb("w1_hi", [P, DC, W1], F32R)
        w_lo = sb("w1_lo", [P, DC, W1], F32R)
        rope = sb("rope", [P, 2, QT, HD])
        weight = sb("norm_w", [P, 2, 2, HD])
        table = sb("rope_w", [P, 2, 2, QT, HD])
        xn = sb("xn1", [P, 2, D])
        xt_hi = sb("xt1_hi", [P, 2, DC, P], F32R)
        xt_lo = sb("xt1_lo", [P, 2, DC, P], F32R)
        squares = sb("squares1", [P, 2, GRP * HD])
        sq_sum = sb("sq_sum1", [P, GRAN, GRP])
        sq_mean = sb("sq_mean1", [P, GRAN, GRP])
        rms = sb("rms1", [P, GRAN, GRP])
        normed = sb("normed1", [P, GRAN, GRP * HD])
        by_cos = sb("by_cos", [P, GRAN, GRP * HD])
        by_sin = sb("by_sin", [P, GRAN, GRP * HD])
        roped = sb("roped", [P, GRAN, GRP * HD])
        out_t = sb("out_t1", [P, GRAN, GRP, P])
        v_out = sb("v_out1", [P, 2, NKV * HD])
        ps_p = psum("ps_p1", [P, GRAN, 512])
        ps_v = psum("ps_v1", [P, 512])
        ps_t = psum("ps_t1", [P, 512])
        ps_x = psum("ps_x1", [P, 512])

        w_loaded, tab_loaded = sem("w1_loaded"), sem("tab_loaded")
        w_hi_done, w_lo_done = sem("w1_hi_done"), sem("w1_lo_done")
        table_ready = sem("table_ready")
        xn_ready, xt_ready = sem("xn1_ready"), sem("xt1_ready")
        xt_hi_done, xt_lo_done = sem("xt1_hi_done"), sem("xt1_lo_done")
        proj_done, v_done = sem("proj1_done"), sem("v1_done")
        square_done, mean_done, rms_done = sem("square1"), sem("mean1"), sem("rms1s")
        normed_done, cos_done, sin_done, roped_done = sem("normed1s"), sem("cos1"), sem("sin1"), sem("roped1")
        t_done, copied, sum_taken = sem("t1_done"), sem("t1_copied"), sem("sum1_taken")
        v_copied, store_begun = sem("v1_copied"), sem("store1_begun")
        out_written = [sem(f"out1_written{j}") for j in range(GRAN)]
        v_written = [sem(f"v1_written{j}") for j in range(2)]

        NB = NT // 2
        LAST = NB - 1
        WPIECES = W1 // 512

        def granule(f):
            return (f // GRAN) % 2, f % GRAN

        def w_cols(j):
            at = 0 if j == 0 else (2 * NKV + (j - 1) * GRP) * HD
            return slice(at, at + GRP * HD)

        LEAD = 3
        LASTG = 2 * GRAN

        def exists(f, last):
            return not (last and f >= LASTG)

        with nc.Block() as block:
            @block.sync
            def _(sp):
                for dram, at in ((wk_d, 0), (wv_d, NKV * HD), (wq_d, 2 * NKV * HD)):
                    sp.dma_start(w_raw[:, :, at:at + dram.shape[1]], dram.rearrange("(c p) n -> p c n", p=P)).then_inc(w_loaded, 16)
                for n in range(2):
                    sp.dma_start(rope[:, n, :, :], rope_dram[n].rearrange("(t p) d -> p t d", p=P)).then_inc(tab_loaded, 16)
                half_w = HD // 2
                for n, w in enumerate((kw_dram, qw_dram)):
                    row = w.rearrange("(a d) -> a d", a=1)
                    sp.dma_start(weight[:, n, 0, :], row.to_broadcast([P, HD])).then_inc(tab_loaded, 16)
                    sp.dma_start(weight[:, n, 1, 0:half_w], row[:, half_w:HD].to_broadcast([P, half_w])).then_inc(tab_loaded, 16)
                    sp.dma_start(weight[:, n, 1, half_w:HD], row[:, 0:half_w].to_broadcast([P, half_w])).then_inc(tab_loaded, 16)
                for j in range(GRAN):
                    sp.sem_inc(out_written[j], 16)
                for j in range(2):
                    sp.sem_inc(v_written[j], 16)
                with sp.Fori(0, NB) as i:
                    heads = [sp.snap(i * NKV + g) for g in range(NKV)]
                    for tt in range(2):
                        sp.wait_ge(v_copied, i * 2 + tt + 1)
                        sp.sem_inc(store_begun, 1)
                        sp.dma_start(v_dram[bass.ds(heads[0], NKV), :, 1 - tt, :].rearrange("g p d -> p g d"),
                                     v_out[:, tt, :].rearrange("p (g d) -> p g d", g=NKV)).then_inc(v_written[tt], 16)
                        for j in range(GRAN):
                            sp.wait_ge(copied, i * LASTG + tt * GRAN + j + 1)
                            sp.sem_inc(store_begun, 1)
                            if j == 0:
                                dst = k_dram[bass.ds(heads[0], NKV), :, (1 - tt) * P:(2 - tt) * P].rearrange("g p n -> p g n")
                            else:
                                dst = q_dram[bass.ds(heads[j - 1], 1), :, :, tt * P:tt * P + P].rearrange("a p h n -> p (a h) n")
                            sp.dma_start(dst, out_t[:, j, :, :]).then_inc(out_written[j], 16)
                for j in range(GRAN):
                    sp.wait_ge(out_written[j], 16 * (NT + 1))
                for j in range(2):
                    sp.wait_ge(v_written[j], 16 * (NB + 1))

            @block.scalar
            def _(act):
                act.wait_ge(w_loaded, 16 * 3)
                for j in range(WPIECES):
                    cols = slice(j * 512, j * 512 + 512)
                    nc.scalar.activation(w_hi[:, :, cols], w_raw[:, :, cols], ACT.Copy).then_inc(w_hi_done, 1)

                def high(i, tt):
                    act.wait_ge(xt_ready, i * 2 + tt + 1)
                    if positive((i * 2 + tt - 1) * GRAN):
                        act.wait_ge(proj_done, (i * 2 + tt - 1) * GRAN)
                    nc.scalar.activation(xt_hi[:, tt % 2, :, :], ps_x[:, 0:D].rearrange("p (c n) -> p c n", c=DC),
                                         ACT.Copy).then_inc(xt_hi_done, 1)

                def square(i, f):
                    tt, j = granule(f)
                    act.wait_ge(proj_done, i * LASTG + f + 1)
                    if positive(i * LASTG + f - GRAN + 1):
                        act.wait_ge(mean_done, i * LASTG + f - GRAN + 1)
                    if positive(i * LASTG + f - 1):
                        act.wait_ge(square_done, (i * LASTG + f - 1) * GRP)
                    for h in range(GRP):
                        d = slice(h * HD, h * HD + HD)
                        nc.scalar.activation(squares[:, f % 2, d], ps_p[:, j, d], ACT.Square, accum_out=sq_sum[:, j, h:h + 1]).then_inc(square_done, 1)
                    if j == 0:
                        act.wait_ge(v_done, i * 2 + f // GRAN + 1)
                        act.wait_ge(v_written[tt], 16 * (i + f // LASTG + 1))
                        nc.scalar.activation(v_out[:, tt, :], ps_v[:, :], ACT.Copy).then_inc(v_copied, 1)

                def copy_out(i, f):
                    tt, j = granule(f)
                    act.wait_ge(t_done, i * LASTG + f + 1)
                    act.wait_ge(out_written[j], 16 * (i * 2 + tt + 1))
                    nc.scalar.activation(out_t[:, j, :, :], ps_t[:, :].rearrange("p (h n) -> p h n", h=GRP), ACT.Copy).then_inc(copied, 1)

                high(0, 0)
                for f in range(LEAD):
                    square(0, f)

                def body(i, last):
                    for f in range(LASTG):
                        tt, j = granule(f)
                        if j == 0 and exists(f + GRAN, last):
                            high(i, tt + 1)
                        if exists(f + LEAD, last):
                            square(i, f + LEAD)
                        copy_out(i, f)

                body(0, False)
                with act.Fori(1, LAST) as i:
                    body(i, False)
                body(LAST, True)

            @block.vector
            def _(dve):
                def normalise(t, slot):
                    tile = bass.ds(t, 1)
                    nc.vector.tensor_scalar(xn[:, slot, :], x_sb[:, tile, :].rearrange("p a n -> p (a n)"),
                                            mean_var[:, tile, 0], rstd[:, tile], ALU.subtract, ALU.mult).then_inc(xn_ready, 1)

                def low(i, tt):
                    dve.wait_ge(xt_hi_done, i * 2 + tt + 1)
                    if positive((i * 2 + tt - 1) * GRAN):
                        dve.wait_ge(proj_done, (i * 2 + tt - 1) * GRAN)
                    nc.vector.tensor_tensor(xt_lo[:, tt % 2, :, :], ps_x[:, 0:D].rearrange("p (c n) -> p c n", c=DC),
                                            xt_hi[:, tt % 2, :, :].bitcast(F32), ALU.subtract).then_inc(xt_lo_done, 1)

                def rotate(i, f):
                    tt, j = granule(f)
                    which = 0 if j == 0 else 1
                    dve.wait_ge(rms_done, i * LASTG + f + 1)
                    if positive(i * LASTG + f - GRAN + 1):
                        dve.wait_ge(cos_done, i * LASTG + f - GRAN + 1)
                    nc.vector.tensor_tensor(normed[:, j, :].rearrange("p (h d) -> p h d", h=GRP),
                                            ps_p[:, j, :].rearrange("p (h d) -> p h d", h=GRP),
                                            rms[:, j, :].unsqueeze(2).to_broadcast([P, GRP, HD]), ALU.mult).then_inc(normed_done, 1)
                    dve.wait_ge(normed_done, i * LASTG + f + 1)
                    src = normed[:, j, :].rearrange("p (h s d) -> p h s d", h=GRP, s=2)
                    dst = by_sin[:, j, :].rearrange("p (h s d) -> p h s d", h=GRP, s=2)
                    for s in range(2):
                        sines = table[:, which, 1, tt, s * (HD // 2):(s + 1) * (HD // 2)]
                        nc.vector.tensor_tensor(dst[:, :, s, :], src[:, :, 1 - s, :],
                                                sines.unsqueeze(1).to_broadcast([P, GRP, HD // 2]), ALU.mult).then_inc(sin_done, 1)

                def add_parts(i, f):
                    j = f % GRAN
                    dve.wait_ge(sin_done, (i * LASTG + f + 1) * 2)
                    dve.wait_ge(cos_done, i * LASTG + f + 1)
                    if positive(i * LASTG + f - GRAN + 1):
                        dve.wait_ge(t_done, i * LASTG + f - GRAN + 1)
                    nc.vector.tensor_tensor(roped[:, j, :], by_cos[:, j, :], by_sin[:, j, :], ALU.add).then_inc(roped_done, 1)

                dve.wait_ge(x_loaded, 16)
                norm_mean_var(nc, dve, x_sb, mean_var, norm)
                dve.wait_ge(norm[-1], 1)
                normalise(0, 0)
                normalise(1, 1)
                for j in range(WPIECES):
                    cols = slice(j * 512, j * 512 + 512)
                    dve.wait_ge(w_hi_done, j + 1)
                    nc.vector.tensor_tensor(w_lo[:, :, cols], w_raw[:, :, cols], w_hi[:, :, cols].bitcast(F32),
                                            ALU.subtract).then_inc(w_lo_done, 1)
                dve.wait_ge(tab_loaded, 16 * 8)
                for n in range(2):
                    for m in range(2):
                        nc.vector.tensor_tensor(table[:, n, m, :, :], rope[:, m, :, :],
                                                weight[:, n, m, :].unsqueeze(1).to_broadcast([P, QT, HD]), ALU.mult).then_inc(table_ready, 1)
                dve.wait_ge(table_ready, 4)
                nc.vector.tensor_scalar(table[:, 1, :, :, :], table[:, 1, :, :, :], float(HD) ** -0.5, None, ALU.mult).then_inc(table_ready, 1)
                dve.wait_ge(table_ready, 5)
                low(0, 0)
                rotate(0, 0)
                rotate(0, 1)
                add_parts(0, 0)

                def body(i, last):
                    for f in range(LASTG):
                        tt, j = granule(f)
                        if j == 0 and exists(f + GRAN, last):
                            low(i, tt + 1)
                            if exists(f + 2 * GRAN, last):
                                dve.wait_ge(xt_ready, i * 2 + tt + 1)
                                normalise(i * 2 + tt + 2, tt)
                        if exists(f + 2, last):
                            rotate(i, f + 2)
                        if exists(f + 1, last):
                            add_parts(i, f + 1)

                body(0, False)
                with dve.Fori(1, LAST) as i:
                    body(i, False)
                body(LAST, True)

            @block.gpsimd
            def _(pool):
                def root(i, f):
                    j = f % GRAN
                    pool.wait_ge(square_done, (i * LASTG + f + 1) * GRP)
                    pool.sem_inc(sum_taken, 1)
                    nc.gpsimd.tensor_scalar(sq_mean[:, j, :], sq_sum[:, j, :], 1.0 / HD, RMS_EPS, ALU.mult, ALU.add).then_inc(mean_done, 1)
                    pool.wait_ge(mean_done, i * LASTG + f + 1)
                    if positive(i * LASTG + f - GRAN + 1):
                        pool.wait_ge(normed_done, i * LASTG + f - GRAN + 1)
                    nc.gpsimd.tensor_tensor(rms[:, j, :], sq_mean[:, j, :], half[:, 0:GRP], ALU.pow).then_inc(rms_done, 1)

                def cosines(i, f):
                    tt, j = granule(f)
                    pool.wait_ge(normed_done, i * LASTG + f + 1)
                    if positive(i * LASTG + f - GRAN + 1):
                        pool.wait_ge(roped_done, i * LASTG + f - GRAN + 1)
                    nc.gpsimd.tensor_tensor(by_cos[:, j, :].rearrange("p (h d) -> p h d", h=GRP),
                                            normed[:, j, :].rearrange("p (h d) -> p h d", h=GRP),
                                            table[:, 0 if j == 0 else 1, 0, tt, :].unsqueeze(1).to_broadcast([P, GRP, HD]),
                                            ALU.mult).then_inc(cos_done, 1)

                pool.wait_ge(half_made, 1)
                norm_rstd(nc, pool, mean_var, rstd, half, norm)
                for f in range(LEAD):
                    root(0, f)
                pool.wait_ge(table_ready, 5)
                cosines(0, 0)
                cosines(0, 1)

                def body(i, last):
                    for f in range(LASTG):
                        if exists(f + LEAD, last):
                            root(i, f + LEAD)
                        if exists(f + 2, last):
                            cosines(i, f + 2)

                body(0, False)
                with pool.Fori(1, LAST) as i:
                    body(i, False)
                body(LAST, True)

            @block.tensor
            def _(pe):
                def transpose_x(i, tt):
                    pe.wait_ge(xn_ready, i * 2 + tt + 1)
                    if positive(i * 2 + tt):
                        pe.wait_ge(xt_lo_done, i * 2 + tt)
                    for c in range(DC):
                        last = nc.tensor.transpose(ps_x[:, c * P:c * P + P], xn[:, tt % 2, c * P:c * P + P], ident[:, :])
                    last.then_inc(xt_ready, 1)

                def three(out, slot, cols):
                    for c in range(DC):
                        a_hi, a_lo = xt_hi[:, slot, c, :], xt_lo[:, slot, c, :]
                        nc.tensor.matmul(out, a_hi, w_hi[:, c, cols], start=c == 0, stop=False)
                        nc.tensor.matmul(out, a_hi, w_lo[:, c, cols], start=False, stop=False)
                        last = nc.tensor.matmul(out, a_lo, w_hi[:, c, cols], start=False, stop=c == DC - 1)
                    return last

                def project(i, f):
                    tt, j = granule(f)
                    if j == 0:
                        pe.wait_ge(xt_lo_done, i * 2 + f // GRAN + 1)
                    if positive(i * LASTG + f - GRAN + 1):
                        pe.wait_ge(normed_done, i * LASTG + f - GRAN + 1)
                        pe.wait_ge(square_done, (i * LASTG + f - GRAN + 1) * GRP)
                    if j == 0:
                        three(ps_p[:, j, :], tt, w_cols(j)).then_inc(proj_done, 1)
                        if positive(i * 2 + f // GRAN):
                            pe.wait_ge(v_copied, i * 2 + f // GRAN)
                        three(ps_v[:, :], tt, slice(NKV * HD, 2 * NKV * HD)).then_inc(v_done, 1)
                    else:
                        three(ps_p[:, j, :], tt, w_cols(j)).then_inc(proj_done, 1)

                def transposes(i, f):
                    j = f % GRAN
                    pe.wait_ge(roped_done, i * LASTG + f + 1)
                    if positive(i * LASTG + f):
                        pe.wait_ge(copied, i * LASTG + f)
                    for h in range(GRP):
                        last = nc.tensor.transpose(ps_t[:, h * P:h * P + P], roped[:, j, h * P:h * P + P], ident[:, :])
                    last.then_inc(t_done, 1)

                pe.wait_ge(ident_loaded, 16)
                transpose_x(0, 0)
                pe.wait_ge(w_lo_done, WPIECES)
                for f in range(LEAD):
                    project(0, f)

                def body(i, last):
                    for f in range(LASTG):
                        tt, j = granule(f)
                        if j == 0 and exists(f + GRAN, last):
                            transpose_x(i, tt + 1)
                        if exists(f + LEAD, last):
                            project(i, f + LEAD)
                        transposes(i, f)

                body(0, False)
                with pe.Fori(1, LAST) as i:
                    body(i, False)
                body(LAST, True)
def context_projections(nc, ctx_dram, wk_dram, wv_dram, kw_dram, k_dram, v_dram, half, ident):
    NTILE = B * CT
    TB = 4
    NB = NTILE // TB
    LAST = NB - 1
    LEAD = 2
    W = NKV * HD
    with ExitStack() as ctx:
        sb, psum, sem = scope(ctx, nc)
        w_raw = sb("w2_raw", [P, DC, 2 * W])
        w_hi = sb("w2_hi", [P, DC, 2 * W], F32R)
        w_lo = sb("w2_lo", [P, DC, 2 * W], F32R)
        kw_col = sb("kw_col", [P, 1])
        c_raw = sb("c_raw", [P, 2, 2, DC * P])
        c_hi = sb("c_hi", [P, 2, 2, DC, P], F32R)
        c_lo = sb("c_lo", [P, 2, 2, DC, P], F32R)
        squares = sb("squares2", [P, 2, W])
        sq_sum = sb("sq_sum2", [P, TB, NKV])
        sq_mean = sb("sq_mean2", [P, TB, NKV])
        rms = sb("rms2", [P, TB, NKV])
        normed = sb("normed2", [P, TB, W])
        k_out = sb("k_out2", [P, TB, NKV, P])
        v_out = sb("v_out2", [P, TB, W])
        ps_k = psum("ps_k2", [P, 4, 512])
        ps_v = psum("ps_v2", [P, 2, 512])
        ps_t = psum("ps_t2", [P, 2, 512])

        w_loaded, kw_loaded = sem("w2_loaded"), sem("kw_loaded")
        c_loaded = [sem(f"c_loaded{j}") for j in range(2)]
        w_hi_done, w_lo_done = sem("w2_hi_done"), sem("w2_lo_done")
        c_hi_done, c_lo_done = sem("c_hi_done"), sem("c_lo_done")
        k_done, v_done = sem("k2_done"), sem("v2_done")
        square_done, sum_done, sum_taken = sem("square2"), sem("sum2"), sem("sum2_taken")
        mean_done, rms_done, normed_done = sem("mean2"), sem("rms2s"), sem("normed2s")
        t_done, k_copied, v_copied, store_begun = sem("t2_done"), sem("k2_copied"), sem("v2_copied"), sem("store2_begun")
        load_begun = sem("load2_begun")
        k_written = [sem(f"k2_written{j}") for j in range(TB)]
        v_written = [sem(f"v2_written{j}") for j in range(TB)]

        def exists(t, last):
            return not (last and t >= TB)

        with nc.Block() as block:
            @block.sync
            def _(sp):
                sp.dma_start(w_raw[:, :, 0:W], wk_dram.rearrange("(c p) n -> p c n", p=P)).then_inc(w_loaded, 16)
                sp.dma_start(w_raw[:, :, W:2 * W], wv_dram.rearrange("(c p) n -> p c n", p=P)).then_inc(w_loaded, 16)
                sp.dma_start(kw_col[:, :], kw_dram.rearrange("(p a) -> p a", a=1)).then_inc(kw_loaded, 16)

                for j in range(TB):
                    sp.sem_inc(k_written[j], 16)
                    sp.sem_inc(v_written[j], 16)

                def body(i):
                    for t in range(TB):
                        tile = i * TB + t
                        g0, at = (tile // CT) * NKV, (tile % CT)
                        sp.wait_ge(v_copied, tile + 1)
                        sp.sem_inc(store_begun, 1)
                        sp.dma_start(v_dram[bass.ds(g0, NKV), :, bass.ds(at + QT, 1), :].rearrange("g p a d -> p g (a d)"),
                                     v_out[:, t, :].rearrange("p (g d) -> p g d", g=NKV)).then_inc(v_written[t], 16)
                        sp.wait_ge(k_copied, tile + 1)
                        sp.sem_inc(store_begun, 1)
                        sp.dma_start(k_dram[bass.ds(g0, NKV), :, bass.ds(at * P + QT * P, P)].rearrange("g p n -> p g n"),
                                     k_out[:, t, :, :]).then_inc(k_written[t], 16)

                with sp.Fori(0, NB) as i:
                    body(i)
                for j in range(TB):
                    sp.wait_ge(k_written[j], 16 * (NB + 1))
                    sp.wait_ge(v_written[j], 16 * (NB + 1))

            def pair_place(i, p):
                return p % 2, i + p // 2

            @block.scalar
            def _(act):
                def load(i, p):
                    act.sem_inc(load_begun, 1)
                    act.dma_start(c_raw[:, p % 2, :, :], ctx_dram[bass.ds((i * 2 + p) * 2, 2)].rearrange("t p c n -> p t (c n)")).then_inc(c_loaded[p % 2], 16)

                load(0, 0)
                load(0, 1)
                act.wait_ge(w_loaded, 32)
                for h in range(4):
                    cols = slice(h * 256, h * 256 + 256)
                    nc.scalar.activation(w_hi[:, :, cols], w_raw[:, :, cols], ACT.Copy).then_inc(w_hi_done, 1)
                act.wait_ge(kw_loaded, 16)

                def high(i, p):
                    j, before = pair_place(i, p)
                    act.wait_ge(c_loaded[j], 16 * (before + 1))
                    if positive((i * 2 + p - 1) * 2):
                        act.wait_ge(v_done, (i * 2 + p - 1) * 2)
                    nc.scalar.activation(c_hi[:, j, :, :, :], c_raw[:, j, :, :].rearrange("p t (c n) -> p t c n", c=DC), ACT.Copy).then_inc(c_hi_done, 1)

                def square_and_v(i, t):
                    act.wait_ge(k_done, i * TB + t + 1)
                    if positive(i * TB + t - 1):
                        act.wait_ge(sum_done, i * TB + t - 1)
                    nc.scalar.activation(squares[:, t % 2, :], ps_k[:, t % TB, :], ACT.Square).then_inc(square_done, 1)
                    act.wait_ge(v_done, i * TB + t + 1)
                    act.wait_ge(v_written[t % TB], 16 * (i + t // TB + 1))
                    nc.scalar.activation(v_out[:, t % TB, :], ps_v[:, t % 2, :], ACT.Copy).then_inc(v_copied, 1)

                def copy_k(i, t):
                    act.wait_ge(t_done, i * TB + t + 1)
                    act.wait_ge(k_written[t % TB], 16 * (i + 1))
                    nc.scalar.activation(k_out[:, t, :, :], ps_t[:, t % 2, :].rearrange("p (h n) -> p h n", h=NKV),
                                         ACT.Copy, scale=kw_col[:, :]).then_inc(k_copied, 1)

                for p in range(2):
                    high(0, p)
                for p in range(2):
                    act.wait_ge(c_lo_done, p + 1)
                    load(0, p + 2)
                for t in range(LEAD):
                    square_and_v(0, t)

                def body(i, last, loads):
                    for t in range(TB):
                        if t % 2 == 0 and not last:
                            high(i, t // 2 + 2)
                        if t % 2 == 1 and loads:
                            act.wait_ge(c_lo_done, i * 2 + t // 2 + 3)
                            load(i, t // 2 + 4)
                        if exists(t + LEAD, last):
                            square_and_v(i, t + LEAD)
                        copy_k(i, t)

                body(0, False, True)
                with act.Fori(1, LAST - 1) as i:
                    body(i, False, True)
                body(LAST - 1, False, False)
                body(LAST, True, False)

            @block.vector
            def _(dve):
                def low(i, p):
                    j, _ = pair_place(i, p)
                    dve.wait_ge(c_hi_done, i * 2 + p + 1)
                    if positive((i * 2 + p - 1) * 2):
                        dve.wait_ge(v_done, (i * 2 + p - 1) * 2)
                    nc.vector.tensor_tensor(c_lo[:, j, :, :, :], c_raw[:, j, :, :].rearrange("p t (c n) -> p t c n", c=DC),
                                            c_hi[:, j, :, :, :].bitcast(F32), ALU.subtract).then_inc(c_lo_done, 1)

                def sum_squares(i, t):
                    dve.wait_ge(square_done, i * TB + t + 1)
                    if positive(i * TB + t - TB + 1):
                        dve.wait_ge(mean_done, i * TB + t - TB + 1)
                    nc.vector.tensor_reduce(sq_sum[:, t % TB, :], squares[:, t % 2, :].rearrange("p (h d) -> p h d", h=NKV),
                                            AX.X, ALU.add).then_inc(sum_done, 1)

                def normalise(i, t):
                    dve.wait_ge(rms_done, i * TB + t + 1)
                    if positive(i * TB + t - TB + 1):
                        dve.wait_ge(t_done, i * TB + t - TB + 1)
                    nc.vector.tensor_tensor(normed[:, t % TB, :].rearrange("p (h d) -> p h d", h=NKV),
                                            ps_k[:, t % TB, :].rearrange("p (h d) -> p h d", h=NKV),
                                            rms[:, t % TB, :].unsqueeze(2).to_broadcast([P, NKV, HD]), ALU.mult).then_inc(normed_done, 1)

                for h in range(4):
                    cols = slice(h * 256, h * 256 + 256)
                    dve.wait_ge(w_hi_done, h + 1)
                    nc.vector.tensor_tensor(w_lo[:, :, cols], w_raw[:, :, cols], w_hi[:, :, cols].bitcast(F32),
                                            ALU.subtract).then_inc(w_lo_done, 1)
                low(0, 0)
                low(0, 1)
                for t in range(LEAD):
                    sum_squares(0, t)
                normalise(0, 0)

                def body(i, last):
                    for t in range(TB):
                        if t % 2 == 0 and not last:
                            low(i, t // 2 + 2)
                        if exists(t + 1, last):
                            normalise(i, t + 1)
                        if exists(t + LEAD, last):
                            sum_squares(i, t + LEAD)

                body(0, False)
                with dve.Fori(1, LAST) as i:
                    body(i, False)
                body(LAST, True)

            @block.gpsimd
            def _(pool):
                def root(i, t):
                    pool.wait_ge(sum_done, i * TB + t + 1)
                    pool.sem_inc(sum_taken, 1)
                    nc.gpsimd.tensor_scalar(sq_mean[:, t, :], sq_sum[:, t, :], 1.0 / HD, RMS_EPS, ALU.mult, ALU.add).then_inc(mean_done, 1)
                    pool.wait_ge(mean_done, i * TB + t + 1)
                    if positive(i * TB + t - TB + 1):
                        pool.wait_ge(normed_done, i * TB + t - TB + 1)
                    nc.gpsimd.tensor_tensor(rms[:, t, :], sq_mean[:, t, :], half[:, 0:NKV], ALU.pow).then_inc(rms_done, 1)

                for t in range(TB):
                    root(0, t)
                with pool.Fori(1, NB) as i:
                    for t in range(TB):
                        root(i, t)

            @block.tensor
            def _(pe):
                def three(out, j, tt, cols):
                    for c in range(DC):
                        a_hi, a_lo = c_hi[:, j, tt, c, :], c_lo[:, j, tt, c, :]
                        nc.tensor.matmul(out, a_hi, w_hi[:, c, cols], start=c == 0, stop=False)
                        nc.tensor.matmul(out, a_hi, w_lo[:, c, cols], start=False, stop=False)
                        last = nc.tensor.matmul(out, a_lo, w_hi[:, c, cols], start=False, stop=c == DC - 1)
                    return last

                def project(i, t):
                    j, tt = (t // 2) % 2, t % 2
                    if tt == 0:
                        pe.wait_ge(c_lo_done, i * 2 + t // 2 + 1)
                    if positive(i * TB + t - TB + 1):
                        pe.wait_ge(normed_done, i * TB + t - TB + 1)
                    three(ps_k[:, t % TB, :], j, tt, slice(0, W)).then_inc(k_done, 1)
                    if positive(i * TB + t - 1):
                        pe.wait_ge(v_copied, i * TB + t - 1)
                    three(ps_v[:, t % 2, :], j, tt, slice(W, 2 * W)).then_inc(v_done, 1)

                def transposes(i, t):
                    pe.wait_ge(normed_done, i * TB + t + 1)
                    if positive(i * TB + t - 1):
                        pe.wait_ge(k_copied, i * TB + t - 1)
                    for h in range(NKV):
                        last = nc.tensor.transpose(ps_t[:, t % 2, h * P:h * P + P], normed[:, t, h * HD:h * HD + HD], ident[:, :])
                    last.then_inc(t_done, 1)

                pe.wait_ge(w_lo_done, 4)
                for t in range(LEAD):
                    project(0, t)

                def body(i, last):
                    for t in range(TB):
                        if exists(t + LEAD, last):
                            project(i, t + LEAD)
                        transposes(i, t)

                body(0, False)
                with pe.Fori(1, LAST) as i:
                    body(i, False)
                body(LAST, True)


UNITS = 2 * QT
BODY_IT = 2
BODY_U = BODY_IT * UNITS
SLOTS = 8
PC = 512
PB = 4
RING = 4
KQ_PIECES, V_PIECES = 6, 4
KPIECE = NK // 4


def blocks_of(qt, c):
    return [k for k in (2 * c, 2 * c + 1) if (0 if qt else 1) <= k < KB]


def attention(nc, q_dram, k_dram, v_dram, wo_dram, x_sb, ident, ident_bf, mask_bf):
    with ExitStack() as ctx:
        sb, psum, sem = scope(ctx, nc)
        raw_q = sb("raw_q", [P, GRP, L])
        raw_k = sb("raw_k", [P, NK])
        raw_v = sb("raw_v", [P, KB * HD])
        q_hi = sb("q_hi", [P, BODY_IT, GRP, L], F32R)
        q_lo = sb("q_lo", [P, BODY_IT, GRP, L], F32R)
        k_hi = sb("k_hi", [P, BODY_IT, NK], F32R)
        k_lo = sb("k_lo", [P, BODY_IT, NK], F32R)
        v_hi = sb("v_hi", [P, BODY_IT, KB * HD], F32R)
        v_lo = sb("v_lo", [P, BODY_IT, KB * HD], F32R)
        prob = sb("prob", [P, PB, NK])
        pt_hi = sb("pt_hi", [P, RING, PC], F32R)
        pt_lo = sb("pt_lo", [P, RING, PC], F32R)
        wo = sb("wo", [P, NH, D])
        o_t = sb("o_t", [P, 2, GRP, P])
        piece_max = sb("piece_max", [P, 2, 4])
        neg_max = sb("neg_max", [P, PB])
        piece_sum = sb("piece_sum", [P, 2, 4])
        row_sum = sb("row_sum", [P, 2])
        inv_sum = sb("inv_sum", [P, PB])
        ps_s = psum("ps_s", [P, 4, PC])
        ps_t = psum("ps_t", [P, 2, PC])
        ps_o = psum("ps_o", [P, 2, PC])

        kq_loaded, v_loaded, wo_loaded = sem("kq_loaded"), sem("v_loaded"), sem("wo_loaded")
        kq_hi, kq_lo = sem("kq_hi_split"), sem("kq_lo_split")
        vv_hi, vv_lo = sem("v_hi_split"), sem("v_lo_split")
        scores_ready = sem("scores_ready")
        max_ready = sem("max_ready")
        neg_max_ready = sem("neg_max_ready")
        exp_done = sem("exp_done")
        sum_ready = sem("sum_ready")
        inv_ready = sem("inv_ready")
        norm_begun, norm_done = sem("norm_begun"), sem("norm_done")
        t_ready = sem("t_ready")
        hi_done, lo_done = sem("pt_hi_done"), sem("pt_lo_done")
        pv_done = sem("pv_done")
        o_copied = sem("o_copied")
        y_ready, y_added = sem("y_ready"), sem("y_added")
        prob_zeroed = sem("prob_zeroed")

        T_CREDIT, PV_CREDIT, O_CREDIT, YR_CREDIT, YA_CREDIT, N_CREDIT = 16, 8, 2, 2, 1, 8
        LAST = BG // BODY_IT - 1

        def head(i, n):
            return (n // 8) % BODY_IT, (n // 4) % QT, n % 4

        def score_cols(qt, p):
            return max(p * PC, 0 if qt else P), min((p + 1) * PC, NKV_USED + 1)

        with nc.Block() as block:
            @block.sync
            def _(sp):
                sp.dma_start(wo[:, :, :], wo_dram.rearrange("(h p) n -> p h n", p=P)).then_inc(wo_loaded, 16)

                def load(it):
                    sp.dma_start(raw_q[:, :, :], q_dram[bass.ds(it, 1)].rearrange("a p h q -> p (a h) q")).then_inc(kq_loaded, 16)
                    sp.dma_start(raw_k[:, :], k_dram[bass.ds(it, 1)].rearrange("a p n -> p (a n)")).then_inc(kq_loaded, 16)

                def load_v(it):
                    sp.dma_start(raw_v[:, :], v_dram[bass.ds(it, 1)].rearrange("a p k n -> p (a k n)")).then_inc(v_loaded, 16)

                load(0)
                load_v(0)
                with sp.Fori(1, BG) as it:
                    sp.wait_ge(kq_hi, it * KQ_PIECES)
                    sp.wait_ge(kq_lo, it * KQ_PIECES)
                    load(it)
                    sp.wait_ge(vv_hi, it * V_PIECES)
                    sp.wait_ge(vv_lo, it * V_PIECES)
                    load_v(it)

            def kq_piece(gi, x):
                if x < 2:
                    h = slice(2 * x, 2 * x + 2)
                    return raw_q[:, h, :], q_hi[:, gi, h, :], q_lo[:, gi, h, :]
                k = slice((x - 2) * KPIECE, (x - 1) * KPIECE)
                return raw_k[:, k], k_hi[:, gi, k], k_lo[:, gi, k]

            def v_piece(gi, x):
                k = slice(x * PC, min((x + 1) * PC, KB * HD))
                return raw_v[:, k], v_hi[:, gi, k], v_lo[:, gi, k]

            KQ_PLAN = {0: [(1, 4)], 1: [(1, 5)], 2: [(2, 0), (2, 1)], 3: [(2, 2), (2, 3)], 4: [(2, 4)],
                       5: [(2, 5)], 6: [(3, 0), (3, 1)], 7: [(3, 2), (3, 3)]}
            V_PLAN = {0: [(1, 0)], 1: [(1, 1)], 2: [(1, 2), (1, 3)], 3: [],
                      4: [(2, 0)], 5: [(2, 1)], 6: [(2, 2), (2, 3)], 7: []}

            @block.scalar
            def _(act):
                def exp(i, n, p):
                    _, qt, _ = head(i, n)
                    lo, hi = score_cols(qt, p)
                    hi = min(hi, NKV_USED)
                    if p == 0:
                        act.wait_ge(neg_max_ready, i * 16 + n + 1)
                    act.wait_ge(t_ready, T_CREDIT + i * 64 + 8 * (n // 2 - 2) + 2 * p + 2)
                    if p == 0:
                        act.wait_ge(sum_ready, i * 16 + n - 1 + 2)
                    nc.scalar.activation(prob[:, n % PB, lo:hi], ps_s[:, p, lo - p * PC:hi - p * PC], ACT.Exp,
                                         bias=neg_max[:, n % PB:n % PB + 1],
                                         accum_out=piece_sum[:, n % 2, p:p + 1]).then_inc(exp_done, 1)

                def high(i, u, c):
                    k = 8 * u + c
                    qt = (u // 2) % QT
                    bs = [x % 2 for x in blocks_of(qt, c)]
                    cols = slice(bs[0] * 256, bs[-1] * 256 + 256)
                    act.wait_ge(t_ready, T_CREDIT + i * 64 + k + 1)
                    act.wait_ge(pv_done, PV_CREDIT + i * 64 + k + 1 - RING)
                    nc.scalar.activation(pt_hi[:, k % RING, cols], ps_t[:, k % 2, cols], ACT.Copy).then_inc(hi_done, 1)

                def split_kq(i, it, x):
                    raw, hi, _ = kq_piece(it % BODY_IT, x)
                    act.wait_ge(kq_loaded, (i * BODY_IT + it + 1) * 32)
                    if it >= BODY_IT:
                        act.wait_ge(scores_ready, i * 64 + 32 * (it - 1))
                    nc.scalar.activation(hi, raw, ACT.Copy).then_inc(kq_hi, 1)

                def split_v(i, it, x):
                    raw, hi, _ = v_piece(it % BODY_IT, x)
                    act.wait_ge(v_loaded, (i * BODY_IT + it + 1) * 16)
                    if it >= 1:
                        act.wait_ge(pv_done, PV_CREDIT + i * 64 + 32 * (it - 1))
                    nc.scalar.activation(hi, raw, ACT.Copy).then_inc(vv_hi, 1)

                def copy_o(i, u):
                    act.wait_ge(pv_done, PV_CREDIT + i * 64 + 8 * u + 8)
                    if u % 2 == 0:
                        act.wait_ge(y_ready, YR_CREDIT + i * (BODY_U // 2) + u // 2 + 1 - 2)
                    pp = u % 2
                    nc.scalar.activation(o_t[:, (u // 2) % 2, 2 * pp:2 * pp + 2, :],
                                         ps_o[:, u % 2, 0:2 * P].rearrange("p (h q) -> p h q", h=2),
                                         ACT.Copy).then_inc(o_copied, 1)

                for x in range(KQ_PIECES):
                    split_kq(0, 0, x)
                for x in range(V_PIECES):
                    split_v(0, 0, x)
                act.wait_ge(prob_zeroed, 1)
                for n in range(3):
                    for p in range(4):
                        exp(0, n, p)
                for x in range(4):
                    split_kq(0, 1, x)
                high(0, 0, 0)

                def body(i, last):
                    for u in range(BODY_U):
                        more = not (last and u >= BODY_U - 2)
                        for s in range(SLOTS):
                            if s < 7 or not (last and u == BODY_U - 1):
                                high(i, u + (s + 1) // 8, (s + 1) % 8)
                            if s < 4 and not (last and u == BODY_U - 1):
                                exp(i, 2 * u + 3, s)
                            elif s >= 4 and more:
                                exp(i, 2 * u + 4, s - 4)
                            if s == 1:
                                for it, x in KQ_PLAN[u]:
                                    if not (last and it >= BODY_IT):
                                        split_kq(i, it, x)
                            if s == 5:
                                for it, x in V_PLAN[u]:
                                    if not (last and it >= BODY_IT):
                                        split_v(i, it, x)
                        copy_o(i, u)

                with act.Fori(0, LAST) as i:
                    body(i, False)
                body(LAST, True)

            @block.vector
            def _(dve):
                def piece_maximum(i, n, p):
                    _, qt, _ = head(i, n)
                    lo, hi = score_cols(qt, p)
                    hi = min(hi, NKV_USED)
                    dve.wait_ge(scores_ready, i * 64 + 4 * n + p + 1)
                    nc.vector.tensor_reduce(piece_max[:, n % 2, p:p + 1], ps_s[:, p, lo - p * PC:hi - p * PC],
                                            AX.X, ALU.max).then_inc(max_ready, 1)

                def negative_maximum(i, n):
                    dve.wait_ge(max_ready, i * 64 + 4 * n + 4)
                    if not (isinstance(i, int) and 4 * n - 12 <= 0):
                        dve.wait_ge(exp_done, i * 64 + 4 * n - 12)
                    nc.vector.tensor_reduce(neg_max[:, n % PB:n % PB + 1], piece_max[:, n % 2, :], AX.X, ALU.max,
                                            negate=True).then_inc(neg_max_ready, 1)

                def inverse_sum(i, n):
                    dve.wait_ge(exp_done, i * 64 + 4 * n + 4)
                    nc.vector.tensor_reduce(row_sum[:, n % 2:n % 2 + 1], piece_sum[:, n % 2, :], AX.X, ALU.add).then_inc(sum_ready, 1)
                    dve.wait_ge(sum_ready, i * 16 + n + 1 + 2)
                    if not (isinstance(i, int) and 4 * n - 12 <= 0):
                        dve.wait_ge(norm_done, N_CREDIT + i * 64 + 4 * n - 12)
                    nc.vector.reciprocal(inv_sum[:, n % PB:n % PB + 1], row_sum[:, n % 2:n % 2 + 1]).then_inc(inv_ready, 1)

                def low(i, u, c):
                    k = 8 * u + c
                    qt = (u // 2) % QT
                    bs = [x % 2 for x in blocks_of(qt, c)]
                    cols = slice(bs[0] * 256, bs[-1] * 256 + 256)
                    dve.wait_ge(hi_done, i * 64 + k + 1)
                    dve.wait_ge(pv_done, PV_CREDIT + i * 64 + k + 1 - RING)
                    nc.vector.tensor_tensor(pt_lo[:, k % RING, cols], ps_t[:, k % 2, cols],
                                            pt_hi[:, k % RING, cols].bitcast(F32), ALU.subtract).then_inc(lo_done, 1)

                def add_y(i, u):
                    tile = bass.ds(2 * (i // 2) + (u // 2) % QT, 1)
                    dve.wait_ge(y_ready, YR_CREDIT + i * (BODY_U // 2) + u // 2 + 1)
                    x_t = x_sb[:, tile, :].rearrange("p a n -> p (a n)")
                    nc.vector.tensor_tensor(x_t, ps_o[:, u % 2, 256:512], x_t, ALU.add).then_inc(y_added, 1)

                nc.vector.memset(prob[:, :, NKV_USED:NK], 0.0).then_inc(prob_zeroed, 1)
                dve.sem_inc(sum_ready, 2)
                dve.sem_inc(y_added, YA_CREDIT)
                for n in range(4):
                    for p in range(4):
                        piece_maximum(0, n, p)
                    negative_maximum(0, n)
                    if 1 <= n <= 2:
                        inverse_sum(0, n - 1)
                low(0, 0, 0)

                def body(i, last):
                    for u in range(BODY_U):
                        more = not (last and u >= BODY_U - 2)
                        for s in range(SLOTS):
                            n, sp = 2 * u + 4 + s // 4, s % 4
                            if s < 7 or not (last and u == BODY_U - 1):
                                low(i, u + (s + 1) // 8, (s + 1) % 8)
                            if s % 4 == 0 and not (last and u == BODY_U - 1):
                                inverse_sum(i, 2 * u + 2 + s // 4)
                            if more:
                                piece_maximum(i, n, sp)
                                if sp == 3:
                                    negative_maximum(i, n)
                            if s == 5 and u % 2 == 0 and u > 0:
                                add_y(i, u - 1)
                    add_y(i, BODY_U - 1)

                with dve.Fori(0, LAST) as i:
                    body(i, False)
                body(LAST, True)

            @block.gpsimd
            def _(pool):
                def normalise(i, n):
                    _, qt, _ = head(i, n)
                    pool.wait_ge(inv_ready, i * 16 + n + 1)
                    pool.sem_inc(norm_begun, 1)
                    for p in range(4):
                        lo, hi = score_cols(qt, p)
                        hi = min(hi, NKV_USED)
                        nc.gpsimd.tensor_scalar(prob[:, n % PB, lo:hi], prob[:, n % PB, lo:hi],
                                                inv_sum[:, n % PB:n % PB + 1], 1.0, ALU.mult, ALU.mult).then_inc(norm_done, 1)

                def split_kq(i, it, x):
                    raw, hi, lo = kq_piece(it % BODY_IT, x)
                    pool.wait_ge(kq_hi, (i * BODY_IT + it) * KQ_PIECES + x + 1)
                    if it >= BODY_IT:
                        pool.wait_ge(scores_ready, i * 64 + 32 * (it - 1))
                    nc.gpsimd.tensor_tensor(lo, raw, hi.bitcast(F32), ALU.subtract).then_inc(kq_lo, 1)

                def split_v(i, it, x):
                    raw, hi, lo = v_piece(it % BODY_IT, x)
                    pool.wait_ge(vv_hi, (i * BODY_IT + it) * V_PIECES + x + 1)
                    if it >= 1:
                        pool.wait_ge(pv_done, PV_CREDIT + i * 64 + 32 * (it - 1))
                    nc.gpsimd.tensor_tensor(lo, raw, hi.bitcast(F32), ALU.subtract).then_inc(vv_lo, 1)

                pool.sem_inc(norm_done, N_CREDIT)
                for x in range(KQ_PIECES):
                    split_kq(0, 0, x)
                for x in range(V_PIECES):
                    split_v(0, 0, x)
                for n in range(2):
                    normalise(0, n)
                for x in range(4):
                    split_kq(0, 1, x)

                def body(i, last):
                    for u in range(BODY_U):
                        if not (last and u == BODY_U - 1):
                            normalise(i, 2 * u + 2)
                        for it, x in KQ_PLAN[u]:
                            if not (last and it >= BODY_IT):
                                split_kq(i, it, x)
                        if not (last and u == BODY_U - 1):
                            normalise(i, 2 * u + 3)
                        for it, x in V_PLAN[u]:
                            if not (last and it >= BODY_IT):
                                split_v(i, it, x)

                with pool.Fori(0, LAST) as i:
                    body(i, False)
                body(LAST, True)

            @block.tensor
            def _(pe):
                def scores(i, n, p):
                    gi, qt, h = head(i, n)
                    lo, hi = score_cols(qt, p)
                    if n % 8 == 0 and p == 0:
                        pe.wait_ge(kq_hi, (i * BODY_IT + n // 8 + 1) * KQ_PIECES)
                        pe.wait_ge(kq_lo, (i * BODY_IT + n // 8 + 1) * KQ_PIECES)
                    if not (isinstance(i, int) and 4 * n + p - 3 <= 0):
                        pe.wait_ge(exp_done, i * 64 + 4 * n + p - 3)
                    out = ps_s[:, p, lo - p * PC:hi - p * PC]
                    qs = slice(qt * P, qt * P + P)
                    nc.tensor.matmul(out, q_hi[:, gi, h, qs], k_hi[:, gi, lo:hi], start=True, stop=False)
                    nc.tensor.matmul(out, q_hi[:, gi, h, qs], k_lo[:, gi, lo:hi], start=False, stop=False)
                    if p == 0:
                        nc.tensor.matmul(ps_s[:, 0, lo:lo + P], ident_bf[:, :], mask_bf[:, :], start=False, stop=False,
                                         skip_group_check=True)
                    nc.tensor.matmul(out, q_lo[:, gi, h, qs], k_hi[:, gi, lo:hi], start=False, stop=True).then_inc(scores_ready, 1)

                def transposes(i, u, c):
                    k = 8 * u + c
                    qt = (u // 2) % QT
                    if c % 2 == 0:
                        pe.wait_ge(norm_done, N_CREDIT + i * 64 + 4 * (2 * u + 1) + c // 2 + 1)
                    if not (isinstance(i, int) and k - 1 <= 0):
                        pe.wait_ge(lo_done, i * 64 + k - 1)
                    for blk in blocks_of(qt, c):
                        for j in range(2):
                            at = (blk % 2) * 256 + j * P
                            last = nc.tensor.transpose(ps_t[:, k % 2, at:at + P],
                                                       prob[:, (2 * u + j) % PB, blk * P:blk * P + P], ident[:, :])
                    last.then_inc(t_ready, 1)

                def products(i, u, c):
                    k = 8 * u + c
                    gi, qt = (u // 4) % BODY_IT, (u // 2) % QT
                    if u % 4 == 0 and c == 0:
                        pe.wait_ge(vv_hi, (i * BODY_IT + u // 4 + 1) * V_PIECES)
                        pe.wait_ge(vv_lo, (i * BODY_IT + u // 4 + 1) * V_PIECES)
                    if c == 0:
                        pe.wait_ge(o_copied, O_CREDIT + i * BODY_U + u - 1)
                        if u % 2 == 1:
                            pe.wait_ge(y_added, YA_CREDIT + i * (BODY_U // 2) + u // 2)
                    pe.wait_ge(lo_done, i * 64 + k + 1)
                    out = ps_o[:, u % 2, 0:256]
                    for blk in blocks_of(qt, c):
                        vs = slice(blk * HD, blk * HD + HD)
                        cols = slice((blk % 2) * 256, (blk % 2) * 256 + 256)
                        nc.tensor.matmul(out, v_hi[:, gi, vs], pt_hi[:, k % RING, cols], start=blk == (0 if qt else 1), stop=False)
                        nc.tensor.matmul(out, v_hi[:, gi, vs], pt_lo[:, k % RING, cols], start=False, stop=False)
                        last = nc.tensor.matmul(out, v_lo[:, gi, vs], pt_hi[:, k % RING, cols], start=False, stop=blk == KB - 1)
                    last.then_inc(pv_done, 1)

                def project(i, u):
                    gi = (u // 4) % BODY_IT
                    pe.wait_ge(o_copied, O_CREDIT + i * BODY_U + u + 1)
                    for h in range(GRP):
                        hh = (i % 2) * (BODY_IT * GRP) + gi * GRP + h
                        last = nc.tensor.matmul(ps_o[:, u % 2, 256:512], o_t[:, (u // 2) % 2, h, :],
                                                wo[:, bass.ds(hh, 1), :].rearrange("p a n -> p (a n)"),
                                                start=h == 0, stop=h == GRP - 1)
                    last.then_inc(y_ready, 1)

                pe.sem_inc(t_ready, T_CREDIT)
                pe.sem_inc(pv_done, PV_CREDIT)
                pe.sem_inc(o_copied, O_CREDIT)
                pe.sem_inc(y_ready, YR_CREDIT)
                pe.wait_ge(wo_loaded, 16)
                for n in range(4):
                    for p in range(4):
                        scores(0, n, p)
                transposes(0, 0, 0)
                transposes(0, 0, 1)

                def body(i, last):
                    for u in range(BODY_U):
                        for s in range(SLOTS):
                            n, sp = 2 * u + 4 + s // 4, s % 4
                            if not (last and u == BODY_U - 1 and s >= 6):
                                transposes(i, u + (s + 2) // 8, (s + 2) % 8)
                            products(i, u, s)
                            if not (last and u >= BODY_U - 2):
                                scores(i, n, sp)
                            if s == 3 and u % 2 == 0 and u > 0:
                                project(i, u - 1)
                    project(i, BODY_U - 1)

                with pe.Fori(0, LAST) as i:
                    body(i, False)
                body(LAST, True)
GT = 4
NG = NT // GT


def moe_two_of_eight(nc, x_sb, gate_dram, bias_dram, w1_dram, w3_dram, w2_dram, sw1_dram, sw3_dram, sw2_dram,
                     mean_var, rstd, half, ident, ident_bf, iota):
    with ExitStack() as ctx:
        sb, psum, sem = scope(ctx, nc)
        N = GT * P
        norm = norm_memory(sb, sem, "norm2")
        w_raw = sb("w4_raw", [P, 3, E0, D])
        w_bf = sb("w4_bf", [P, 3, E0, D], BF16)
        sw = sb("w4_shared", [P, 3, D])
        gate = sb("gate4", [P, DC, E0])
        bias = sb("bias4", [P, E0])
        xn = sb("xn4", [P, GT, D])
        xt = sb("xt4", [P, DC, N])
        score = sb("score4", [P, GT, E0])
        biased = sb("biased4", [P, GT, E0])
        best = sb("best4", [P, GT, 8])
        best_at = sb("best_at4", [P, GT, 8], U32)
        chosen_at = sb("chosen_at4", [P, GT, 2])
        first = sb("first4", [P, GT, E0])
        second = sb("second4", [P, GT, E0])
        chosen = sb("chosen4", [P, GT, E0])
        weight = sb("weight4", [P, GT, E0])
        xb = sb("xb4", [P, 2, GT, D], BF16)
        xbt = sb("xbt4", [P, 2, DC, N], BF16)
        h1_bf = sb("h1_4_bf", [P, 2, N], BF16)
        h3_bf = sb("h3_4_bf", [P, 2, N], BF16)
        exp_bf = sb("exp4_bf", [P, 2, N], BF16)
        den_bf = sb("den4_bf", [P, 2, N], BF16)
        inv_bf = sb("inv4_bf", [P, 2, N], BF16)
        silu_bf = sb("silu4_bf", [P, 2, N], BF16)
        exp_f = sb("exp4_f", [P, N])
        den_f = sb("den4_f", [P, N])
        inv_f = sb("inv4_f", [P, N])
        silu_f = sb("silu4_f", [P, N])
        y_bf = sb("y4_bf", [P, 2, 2 * D], BF16)
        score_exp = sb("score_exp4", [P, GT, E0])
        score_den = sb("score_den4", [P, GT, E0])
        act_bf = sb("act4_bf", [P, 2, N], BF16)
        act_f = sb("act4_f", [P, N])
        ps_acc = psum("ps_acc4", [P, 2, 512])
        ps_h = psum("ps_h4", [P, 4, 512])
        ps_b = psum("ps_b4", [P, 1024], BF16)
        ps_y = psum("ps_y4", [P, 512])

        w_loaded = [sem(f"w4_loaded{e}") for e in range(E0)]
        sw_loaded, gate_loaded = sem("sw4_loaded"), sem("gate4_loaded")
        w_cast = sem("w4_cast")
        xn_ready, xt_ready, xt_copied = sem("xn4"), sem("xt4s"), sem("xt4_copied")
        logits, scored, added, maxed, indexed, idx_f = sem("logits4"), sem("scored4"), sem("biased4s"), sem("best4s"), sem("best4_at"), sem("chosen4_at")
        is_first, is_second, chosen_s, weighted = sem("first4s"), sem("second4s"), sem("chosen4s"), sem("weight4s")
        choice_begun = sem("choice4_begun")
        scale_begun = sem("scale4_begun")
        xb_ready, xbt_ready, xbt_copied = sem("xb4s"), sem("xbt4s"), sem("xbt4_copied")
        h1_ready, h3_ready, h1_copied, h3_copied = sem("h1_4"), sem("h3_4"), sem("h1_4_copied"), sem("h3_4_copied")
        exp_ready, den_ready, inv_ready, silu_ready, act_ready = sem("exp4s"), sem("den4s"), sem("inv4s"), sem("silu4s"), sem("act4s")
        score_exps, score_dens = sem("score_exp4s"), sem("score_den4s")
        y_done, y_copied, summed, x_added = sem("y4"), sem("y4_copied"), sem("summed4"), sem("x4_added")
        shared_done = sem("shared4")
        STEPS = E0 + 1

        with nc.Block() as block:
            @block.sync
            def _(sp):
                sp.dma_start(gate[:, :, :], gate_dram.rearrange("(c p) e -> p c e", p=P)).then_inc(gate_loaded, 16)
                sp.dma_start(bias[:, :], bias_dram.rearrange("(a e) -> a e", a=1).to_broadcast([P, E0])).then_inc(gate_loaded, 16)
                for n, w in enumerate((sw1_dram, sw3_dram)):
                    sp.dma_start(sw[:, n, :].rearrange("p (c h) -> p c h", c=DC), w.rearrange("(c p) h -> p c h", p=P)).then_inc(sw_loaded, 16)
                sp.dma_start(sw[:, 2, :], sw2_dram).then_inc(sw_loaded, 16)
                for e in range(E0):
                    for n, w in enumerate((w1_dram, w3_dram)):
                        sp.dma_start(w_raw[:, n, e, :].rearrange("p (c h) -> p c h", c=DC),
                                     w[e].rearrange("(c p) h -> p c h", p=P)).then_inc(w_loaded[e], 16)
                    sp.dma_start(w_raw[:, 2, e, :], w2_dram[e]).then_inc(w_loaded[e], 16)

            @block.gpsimd
            def _(pool):
                norm_rstd(nc, pool, mean_var, rstd, half, norm)

                def cast(e):
                    pool.wait_ge(w_loaded[e], 16 * 3)
                    for n in range(3):
                        nc.gpsimd.tensor_copy(w_bf[:, n, e, :], w_raw[:, n, e, :]).then_inc(w_cast, 1)

                def scale(i, e):
                    if e == 0:
                        pool.wait_ge(weighted, i + 1)
                    if positive(i * E0 + e - 1):
                        pool.wait_ge(xbt_ready, i * E0 + e - 1)
                    pool.sem_inc(scale_begun, 1)
                    for t in range(GT):
                        nc.gpsimd.tensor_scalar(xb[:, e % 2, t, :], xn[:, t, :], weight[:, t, e:e + 1], 1.0, ALU.mult, ALU.mult).then_inc(xb_ready, 1)

                for e in range(E0):
                    cast(e)
                    scale(0, e)
                with pool.Fori(1, NG) as i:
                    for e in range(E0):
                        scale(i, e)

            @block.scalar
            def _(act):
                def group(i):
                    act.wait_ge(xt_ready, (i + 1) * DC)
                    for c in range(DC):
                        nc.scalar.activation(xt[:, c, :], ps_h[:, 2 + c, :], ACT.Copy).then_inc(xt_copied, 1)
                    act.wait_ge(logits, i + 1)
                    nc.scalar.activation(score_exp[:, :, :], ps_y[:, 0:GT * E0].rearrange("p (t e) -> p t e", t=GT), ACT.Exp, scale=-1.0).then_inc(score_exps, 1)

                    def inputs(e):
                        act.wait_ge(xbt_ready, i * E0 + e + 1)
                        if positive(i * E0 + e - 1):
                            act.wait_ge(h3_ready, (i * STEPS + e - 1 + 1) if e >= 2 else i * STEPS - (1 - e))
                        nc.scalar.activation(xbt[:, e % 2, :, :], ps_b[:, :].rearrange("p (c n) -> p c n", c=DC), ACT.Copy).then_inc(xbt_copied, 1)

                    def outputs(s, h):
                        k = (i * E0 + s - 1) * 2 + h
                        act.wait_ge(y_done, k + 1)
                        if positive(k - 1):
                            act.wait_ge(summed, k - 1)
                        nc.scalar.activation(y_bf[:, h, :], ps_y[:, :], ACT.Copy).then_inc(y_copied, 1)

                    def hidden(s):
                        j = s % 2
                        act.wait_ge(h1_ready, i * STEPS + s + 1)
                        if s == 0:
                            if positive(i):
                                act.wait_ge(den_ready, (i - 1) * STEPS + 1)
                            nc.scalar.activation(exp_f[:, :], ps_h[:, 0, :], ACT.Exp, scale=-1.0).then_inc(exp_ready, 1)
                            return
                        if positive(i * STEPS + s - 2):
                            act.wait_ge(act_ready, i * STEPS + s - 1)
                        nc.scalar.activation(h1_bf[:, j, :], ps_h[:, 2 * j, :], ACT.Copy).then_inc(h1_copied, 1)
                        act.wait_ge(h1_copied, i * E0 + s)
                        nc.scalar.activation(exp_bf[:, j, :], h1_bf[:, j, :], ACT.Exp, scale=-1.0).then_inc(exp_ready, 1)
                        act.wait_ge(h3_ready, i * STEPS + s + 1)
                        nc.scalar.activation(h3_bf[:, j, :], ps_h[:, 2 * j + 1, :], ACT.Copy).then_inc(h3_copied, 1)

                    hidden(0)
                    inputs(0)
                    for s in range(STEPS):
                        if s + 1 < STEPS:
                            hidden(s + 1)
                        if s > 0:
                            outputs(s, 0)
                        if s + 1 < E0:
                            inputs(s + 1)
                        if s > 0:
                            outputs(s, 1)

                group(0)
                with act.Fori(1, NG) as i:
                    group(i)

            @block.vector
            def _(dve):
                def group(i):
                    for t in range(GT):
                        tile = bass.ds(i * GT + t, 1)
                        if positive(i):
                            dve.wait_ge(xb_ready, i * E0 * GT)
                        nc.vector.tensor_scalar(xn[:, t, :], x_sb[:, tile, :].rearrange("p a n -> p (a n)"),
                                                mean_var[:, tile, 0], rstd[:, tile], ALU.subtract, ALU.mult).then_inc(xn_ready, 1)
                    dve.wait_ge(score_exps, i + 1)
                    nc.vector.tensor_scalar(score_den[:, :, :], score_exp[:, :, :], 1.0, None, ALU.add).then_inc(score_dens, 1)
                    dve.wait_ge(score_dens, i + 1)
                    nc.vector.reciprocal(score[:, :, :], score_den[:, :, :]).then_inc(scored, 1)
                    dve.wait_ge(scored, i + 1)
                    nc.vector.tensor_tensor(biased[:, :, :], score[:, :, :], bias[:, :].unsqueeze(1).to_broadcast([P, GT, E0]), ALU.add).then_inc(added, 1)
                    dve.wait_ge(added, i + 1)
                    dve.sem_inc(choice_begun, 1)
                    for t in range(GT):
                        nc.vector.max(best[:, t, :], biased[:, t, :]).then_inc(maxed, 1)
                    dve.wait_ge(maxed, (i + 1) * GT)
                    dve.sem_inc(choice_begun, 1)
                    for t in range(GT):
                        nc.vector.max_index(best_at[:, t, :], best[:, t, :], biased[:, t, :]).then_inc(indexed, 1)
                    dve.wait_ge(indexed, (i + 1) * GT)
                    nc.vector.tensor_copy(chosen_at[:, :, :], best_at[:, :, 0:2]).then_inc(idx_f, 1)
                    dve.wait_ge(idx_f, i + 1)
                    places = iota[:, 0:E0].unsqueeze(1).to_broadcast([P, GT, E0])
                    for n, (out, s) in enumerate(((first, is_first), (second, is_second))):
                        nc.vector.tensor_tensor(out[:, :, :], places, chosen_at[:, :, n:n + 1].to_broadcast([P, GT, E0]), ALU.is_equal).then_inc(s, 1)
                    dve.wait_ge(is_first, i + 1)
                    dve.wait_ge(is_second, i + 1)
                    nc.vector.tensor_tensor(chosen[:, :, :], first[:, :, :], second[:, :, :], ALU.add).then_inc(chosen_s, 1)
                    dve.wait_ge(chosen_s, i + 1)
                    nc.vector.tensor_tensor(weight[:, :, :], chosen[:, :, :], score[:, :, :], ALU.mult).then_inc(weighted, 1)
                    for s in range(STEPS):
                        j = s % 2
                        exp, den, inv, silu, act, h1, h3 = ((exp_f[:, :], den_f[:, :], inv_f[:, :], silu_f[:, :], act_f[:, :],
                                                            ps_h[:, 0, :], ps_h[:, 1, :]) if s == 0 else
                                                           (exp_bf[:, j, :], den_bf[:, j, :], inv_bf[:, j, :], silu_bf[:, j, :],
                                                            act_bf[:, j, :], h1_bf[:, j, :], h3_bf[:, j, :]))
                        dve.wait_ge(exp_ready, i * STEPS + s + 1)
                        nc.vector.tensor_scalar(den, exp, 1.0, None, ALU.add).then_inc(den_ready, 1)
                        dve.wait_ge(den_ready, i * STEPS + s + 1)
                        with nc.allow_low_precision(reason="the reference divides in bfloat16"):
                            nc.vector.reciprocal(inv, den).then_inc(inv_ready, 1)
                        dve.wait_ge(inv_ready, i * STEPS + s + 1)
                        nc.vector.tensor_tensor(silu, h1, inv, ALU.mult).then_inc(silu_ready, 1)
                        if s == 0:
                            dve.wait_ge(h3_ready, i * STEPS + 1)
                        else:
                            dve.wait_ge(h3_copied, i * E0 + s)
                        dve.wait_ge(silu_ready, i * STEPS + s + 1)
                        if s == 0 and positive(i):
                            dve.wait_ge(shared_done, i)
                        if s > 0 and positive((i * E0 + s - 1) * 2 - 2):
                            dve.wait_ge(y_done, (i * E0 + s - 2) * 2)
                        nc.vector.tensor_tensor(act, h3, silu, ALU.mult).then_inc(act_ready, 1)
                    dve.wait_ge(summed, (i + 1) * E0 * 2)
                    for h in range(2):
                        x_t = x_sb[:, bass.ds(i * GT + 2 * h, 2), :].rearrange("p a n -> p (a n)")
                        nc.vector.tensor_tensor(x_t, ps_acc[:, h, :], x_t, ALU.add).then_inc(x_added, 1)

                norm_mean_var(nc, dve, x_sb, mean_var, norm)
                dve.wait_ge(gate_loaded, 32)
                dve.wait_ge(norm[-1], 1)
                group(0)
                with dve.Fori(1, NG) as i:
                    group(i)

            @block.tensor
            def _(pe):
                def group(i):
                    pe.wait_ge(xn_ready, (i + 1) * GT)
                    for c in range(DC):
                        if positive(i):
                            pe.wait_ge(h3_copied, i * E0)
                        for t in range(GT):
                            last = nc.tensor.transpose(ps_h[:, 2 + c, t * P:t * P + P], xn[:, t, c * P:c * P + P], ident[:, :])
                        last.then_inc(xt_ready, 1)
                    pe.wait_ge(xt_copied, (i + 1) * DC)
                    if positive(i):
                        pe.wait_ge(y_copied, i * E0 * 2)
                    for t in range(GT):
                        for c in range(DC):
                            last = nc.tensor.matmul(ps_y[:, t * E0:(t + 1) * E0], xt[:, c, t * P:t * P + P], gate[:, c, :],
                                                    start=c == 0, stop=c == DC - 1)
                    last.then_inc(logits, 1)

                    def inputs(e):
                        pe.wait_ge(xb_ready, (i * E0 + e + 1) * GT)
                        if positive(i * E0 + e):
                            pe.wait_ge(xbt_copied, i * E0 + e)
                        for c in range(DC):
                            for t in range(GT):
                                last = nc.tensor.transpose(ps_b[:, c * N + t * P:c * N + t * P + P], xb[:, e % 2, t, c * P:c * P + P], ident_bf[:, :])
                        last.then_inc(xbt_ready, 1)

                    def hidden(s):
                        j = s % 2
                        if s > 0:
                            pe.wait_ge(xbt_copied, i * E0 + s)
                        if s == 2:
                            pe.wait_ge(act_ready, i * STEPS + 1)
                        elif s != 1 and positive(i * E0 + s - 2):
                            pe.wait_ge(h3_copied, i * E0 + max(s - 2, 0))
                        for n, done in ((0, h1_ready), (1, h3_ready)):
                            for c in range(DC):
                                if s == 0:
                                    a, b = sw[:, n, c * H0:c * H0 + H0], xt[:, c, :]
                                else:
                                    a, b = w_bf[:, n, s - 1, c * H0:c * H0 + H0], xbt[:, (s - 1) % 2, c, :]
                                last = nc.tensor.matmul(ps_h[:, 2 * j + n, :], a, b, start=c == 0, stop=c == DC - 1)
                            last.then_inc(done, 1)

                    def add(t, a, b, first=False, last=False):
                        return nc.tensor.matmul(ps_acc[:, t // 2, (t % 2) * D:(t % 2) * D + D], a, b, start=first and t % 2 == 0,
                                                stop=last and t % 2 == 1, skip_group_check=True)

                    def shared_outputs():
                        pe.wait_ge(act_ready, i * STEPS + 1)
                        if positive(i):
                            pe.wait_ge(x_added, i * 2)
                        for t in range(GT):
                            last = add(t, act_f[:, t * P:t * P + P], sw[:, 2, :], first=True)
                        last.then_inc(shared_done, 1)

                    def outputs(s, h):
                        k = (i * E0 + s - 1) * 2 + h
                        if h == 0:
                            pe.wait_ge(act_ready, i * STEPS + s + 1)
                        if s == 1 and h == 0:
                            pe.wait_ge(score_exps, i + 1)
                        if positive(k):
                            pe.wait_ge(y_copied, k)
                        for t in range(2):
                            last = nc.tensor.matmul(ps_y[:, t * D:t * D + D], act_bf[:, s % 2, (2 * h + t) * P:(2 * h + t + 1) * P], w_bf[:, 2, s - 1, :],
                                                    start=True, stop=True)
                        last.then_inc(y_done, 1)

                    def sums(s, h):
                        pe.wait_ge(y_copied, (i * E0 + s - 1) * 2 + h + 1)
                        for t in range(2):
                            last = add(2 * h + t, ident_bf[:, :], y_bf[:, h, t * D:t * D + D], last=s == STEPS - 1)
                        last.then_inc(summed, 1)

                    hidden(0)
                    inputs(0)
                    for s in range(STEPS):
                        if s + 1 < STEPS:
                            if not positive(i):
                                pe.wait_ge(w_cast, 3 * (s + 1))
                            hidden(s + 1)
                        if s > 1:
                            sums(s - 1, 1)
                        if s > 0:
                            outputs(s, 0)
                        else:
                            shared_outputs()
                        if s + 1 < E0:
                            inputs(s + 1)
                        if s > 0:
                            outputs(s, 1)
                            sums(s, 0)
                    sums(STEPS - 1, 1)

                pe.wait_ge(gate_loaded, 32)
                pe.wait_ge(sw_loaded, 48)
                group(0)
                with pe.Fori(1, NG) as i:
                    group(i)


def memory_attention(nc, x_sb, ctx_t_dram, ctx_dram, mask_dram, mean_var, rstd, half, ident):
    UB = 2 * QT
    NB = NT // UB
    LAST = NB - 1
    KP = CT * P
    SL = 4
    RINGC = 4
    PIECES = [(0, 4), (4, 8), (8, 12), (12, CT)]
    with ExitStack() as ctx:
        sb, psum, sem = scope(ctx, nc)
        raw_t = sb("raw_t5", [P, CT, DC * P])
        raw_r = sb("raw_r5", [P, CT, D])
        mask = sb("mask5", [1, 2, T], U8)
        pen = sb("pen5", [P, 2, KP], BF16)
        row0 = sb("row0_5", [P, P], BF16)
        t_hi = sb("t_hi5", [P, 2, CT, DC, P], F32R)
        t_lo = sb("t_lo5", [P, 2, CT, DC, P], F32R)
        r_hi = sb("r_hi5", [P, 2, CT, D], F32R)
        r_lo = sb("r_lo5", [P, 2, CT, D], F32R)
        rstd_scaled = sb("rstd5", [P, NT])
        xn = sb("xn5", [P, 2, D])
        xt_hi = sb("xt5_hi", [P, 2, DC, P], F32R)
        xt_lo = sb("xt5_lo", [P, 2, DC, P], F32R)
        prob = sb("prob5", [P, 2, KP])
        pt_hi = sb("pt5_hi", [P, RINGC, 512], F32R)
        pt_lo = sb("pt5_lo", [P, RINGC, 512], F32R)
        piece_max = sb("piece_max5", [P, 2, SL])
        neg_max = sb("neg_max5", [P, 4])
        piece_sum = sb("piece_sum5", [P, 2, SL])
        row_sum = sb("row_sum5", [P, 2])
        inv_row = sb("inv_row5", [P, 2])
        inv_sum = sb("inv_sum5", [P, 2])
        ps_s = psum("ps_s5", [P, SL, 512])
        ps_t = psum("ps_t5", [P, 2, 512])
        ps_o = psum("ps_o5", [P, 2, 512])

        norm = norm_memory(sb, sem, "norm3")
        t_loaded, r_loaded, m_loaded = [sem(f"t5_loaded{x}") for x in range(4)], [sem(f"r5_loaded{x}") for x in range(4)], [sem(f"m5_loaded{j}") for j in range(2)]
        th_done, tl_done, rh_done, rl_done = sem("t5_hi"), sem("t5_lo"), sem("r5_hi"), sem("r5_lo")
        mask_begun = sem("mask5_begun")
        zeroed, row0_ready, pen_ready, scaled = sem("zeroed5"), sem("row0_5s"), sem("pen5s"), sem("rstd5s")
        xn_ready, xt_ready, xt_hi_done, xt_lo_done = sem("xn5s"), sem("xt5s"), sem("xt5_his"), sem("xt5_los")
        scores_ready, max_ready, neg_max_ready, exp_done = sem("scores5"), sem("max5"), sem("neg_max5s"), sem("exp5")
        sum_ready, recip_ready, inv_ready = sem("sum5"), sem("recip5"), sem("inv5")
        pt_ready, hi_done, lo_done, pv_done, x_added = sem("pt5"), sem("pt5_his"), sem("pt5_los"), sem("pv5"), sem("x5_added")

        def exists(n, last):
            return not (last and n >= UB)

        def cols(p):
            return p * 512, min((p + 1) * 512, T)

        def blocks(c):
            return range(4 * c, min(4 * c + 4, CT))

        with nc.Block() as block:
            @block.sync
            def _(sp):
                def load_mask(b, j):
                    sp.dma_start(mask[:, j, :], mask_dram[bass.ds(b, 1), :]).then_inc(m_loaded[j], 16)

                def load_t(b, x):
                    lo, hi = PIECES[x]
                    sp.dma_start(raw_t[:, lo:hi, :], ctx_t_dram[bass.ds(b * CT + lo, hi - lo)].rearrange("t p c n -> p t (c n)")).then_inc(t_loaded[x], 16)

                def load_r(b, x):
                    lo, hi = PIECES[x]
                    sp.dma_start(raw_r[:, lo:hi, :], ctx_dram[bass.ds(b, 1), lo * P:hi * P, :].rearrange("a (t p) d -> p (a t) d", p=P)).then_inc(r_loaded[x], 16)

                for x in range(4):
                    load_t(0, x)
                for j in range(2):
                    load_mask(j, j)
                for x in range(4):
                    load_r(0, x)
                for x in range(4):
                    sp.wait_ge(th_done, x + 1)
                    sp.wait_ge(tl_done, x + 1)
                    load_t(1, x)

                def both(i, more):
                    for j in range(2):
                        for x in range(4):
                            if more:
                                sp.wait_ge(th_done, (i * 2 + j + 1) * 4 + x + 1)
                                sp.wait_ge(tl_done, (i * 2 + j + 1) * 4 + x + 1)
                                load_t(i * 2 + j + 2, x)
                            if more or j == 0:
                                sp.wait_ge(rh_done, (i * 2 + j) * 4 + x + 1)
                                sp.wait_ge(rl_done, (i * 2 + j) * 4 + x + 1)
                                load_r(i * 2 + j + 1, x)
                        if more:
                            sp.wait_ge(pen_ready, i * 2 + j + 1)
                            sp.sem_inc(mask_begun, 1)
                            load_mask(i * 2 + j + 2, j)

                with sp.Fori(0, LAST) as i:
                    both(i, True)
                both(LAST, False)

            @block.gpsimd
            def _(pool):
                norm_rstd(nc, pool, mean_var, rstd, half, norm)
                nc.gpsimd.memset(row0[:, :], 0.0).then_inc(row0_ready, 1)
                pool.wait_ge(row0_ready, 1)
                nc.gpsimd.memset(row0[0:1, :], 1.0).then_inc(row0_ready, 1)
                nc.gpsimd.memset(prob[:, :, T:KP], 0.0).then_inc(zeroed, 1)
                nc.gpsimd.memset(pen[:, :, :], 0.0).then_inc(zeroed, 1)

                def split_t(i, b, x):
                    lo, hi = PIECES[x]
                    pool.wait_ge(th_done, (i * 2 + b) * 4 + x + 1)
                    if positive((i * 2 + b - 2) * 2 * SL + 2 * SL):
                        pool.wait_ge(scores_ready, (i * 2 + b - 1) * 2 * SL)
                    nc.gpsimd.tensor_tensor(t_lo[:, b % 2, lo:hi, :, :], raw_t[:, lo:hi, :].rearrange("p t (c n) -> p t c n", c=DC),
                                            t_hi[:, b % 2, lo:hi, :, :].bitcast(F32), ALU.subtract).then_inc(tl_done, 1)

                def split_r(i, b, x):
                    lo, hi = PIECES[x]
                    pool.wait_ge(rh_done, (i * 2 + b) * 4 + x + 1)
                    if positive((i * 2 + b - 1) * 2 * SL):
                        pool.wait_ge(pv_done, (i * 2 + b - 1) * 2 * SL)
                    nc.gpsimd.tensor_tensor(r_lo[:, b % 2, lo:hi, :], raw_r[:, lo:hi, :], r_hi[:, b % 2, lo:hi, :].bitcast(F32),
                                            ALU.subtract).then_inc(rl_done, 1)

                for x in range(4):
                    split_t(0, 0, x)
                for x in range(4):
                    split_t(0, 1, x)
                for x in range(4):
                    split_r(0, 0, x)

                def body(i, last):
                    for u in range(UB):
                        for x in (2 * (u % 2), 2 * (u % 2) + 1):
                            if not last:
                                split_t(i, u // 2 + 2, x)
                            if not (last and u >= 2):
                                split_r(i, u // 2 + 1, x)

                body(0, False)
                with pool.Fori(1, LAST) as i:
                    body(i, False)
                body(LAST, True)

            @block.scalar
            def _(act):
                def split_t(i, b, x):
                    lo, hi = PIECES[x]
                    act.wait_ge(t_loaded[x], (i * 2 + b + 1) * 16)
                    if positive((i * 2 + b - 1) * 2 * SL):
                        act.wait_ge(scores_ready, (i * 2 + b - 1) * 2 * SL)
                    nc.scalar.activation(t_hi[:, b % 2, lo:hi, :, :], raw_t[:, lo:hi, :].rearrange("p t (c n) -> p t c n", c=DC), ACT.Copy).then_inc(th_done, 1)

                def split_r(i, b, x):
                    lo, hi = PIECES[x]
                    act.wait_ge(r_loaded[x], (i * 2 + b + 1) * 16)
                    if positive((i * 2 + b - 1) * 2 * SL):
                        act.wait_ge(pv_done, (i * 2 + b - 1) * 2 * SL)
                    nc.scalar.activation(r_hi[:, b % 2, lo:hi, :], raw_r[:, lo:hi, :], ACT.Copy).then_inc(rh_done, 1)

                def exp(i, n, p):
                    lo, hi = cols(p)
                    if p == 0:
                        act.wait_ge(neg_max_ready, i * UB + n + 1)
                        if positive(i * UB + n - 1):
                            act.wait_ge(sum_ready, i * UB + n - 1)
                    if positive((i * UB + n - 2) * SL + p + 1):
                        act.wait_ge(pt_ready, (i * UB + n - 2) * SL + p + 1)
                    nc.scalar.activation(prob[:, n % 2, lo:hi], ps_s[:, p, 0:hi - lo], ACT.Exp, bias=neg_max[:, n % 4:n % 4 + 1],
                                         accum_out=piece_sum[:, n % 2, p:p + 1]).then_inc(exp_done, 1)

                def high(i, u, c):
                    k = u * SL + c
                    w = len(blocks(c)) * P
                    act.wait_ge(pt_ready, i * UB * SL + k + 1)
                    if positive(i * UB * SL + k + 1 - RINGC):
                        act.wait_ge(pv_done, i * UB * SL + k + 1 - RINGC)
                    nc.scalar.activation(pt_hi[:, k % RINGC, 0:w], ps_t[:, k % 2, 0:w], ACT.Copy).then_inc(hi_done, 1)

                def high_x(i, v):
                    act.wait_ge(xt_ready, i * UB + v + 1)
                    if positive((i * UB + v - 1) * SL):
                        act.wait_ge(scores_ready, (i * UB + v - 1) * SL)
                    nc.scalar.activation(xt_hi[:, v % 2, :, :], ps_o[:, v % 2, D:2 * D].rearrange("p (c n) -> p c n", c=DC), ACT.Copy).then_inc(xt_hi_done, 1)

                for v in range(2):
                    high_x(0, v)
                for x in range(4):
                    split_t(0, 0, x)
                for x in range(4):
                    split_t(0, 1, x)
                for x in range(4):
                    split_r(0, 0, x)
                act.wait_ge(zeroed, 2)
                for p in range(SL):
                    exp(0, 0, p)
                high_x(0, 2)
                high(0, 0, 0)

                def body(i, last):
                    for u in range(UB):
                        for s in range(SL):
                            if exists(u + (s + 1) // SL, last):
                                high(i, u + (s + 1) // SL, (s + 1) % SL)
                            if exists(u + 1, last):
                                exp(i, u + 1, s)
                            x = 2 * (u % 2) + s // 2
                            if s % 2 == 0 and not last:
                                split_t(i, u // 2 + 2, x)
                            if s % 2 == 1 and not (last and u >= 2):
                                split_r(i, u // 2 + 1, x)
                        if exists(u + 3, last):
                            high_x(i, u + 3)

                body(0, False)
                with act.Fori(1, LAST) as i:
                    body(i, False)
                body(LAST, True)

            @block.vector
            def _(dve):
                def normalise(i, v):
                    tile = bass.ds(i * UB + v, 1)
                    if positive(i * UB + v - 1):
                        dve.wait_ge(xt_ready, i * UB + v - 1)
                    nc.vector.tensor_scalar(xn[:, v % 2, :], x_sb[:, tile, :].rearrange("p a n -> p (a n)"),
                                            mean_var[:, tile, 0], rstd_scaled[:, tile], ALU.subtract, ALU.mult).then_inc(xn_ready, 1)

                def low_x(i, v):
                    dve.wait_ge(xt_hi_done, i * UB + v + 1)
                    if positive((i * UB + v - 1) * SL):
                        dve.wait_ge(scores_ready, (i * UB + v - 1) * SL)
                    nc.vector.tensor_tensor(xt_lo[:, v % 2, :, :], ps_o[:, v % 2, D:2 * D].rearrange("p (c n) -> p c n", c=DC),
                                            xt_hi[:, v % 2, :, :].bitcast(F32), ALU.subtract).then_inc(xt_lo_done, 1)

                def penalty(i, b):
                    dve.wait_ge(m_loaded[b % 2], 16 * (i + b // 2 + 1))
                    if positive((i * 2 + b - 1) * 2 * SL):
                        dve.wait_ge(scores_ready, (i * 2 + b - 1) * 2 * SL)
                    nc.vector.tensor_scalar(pen[0:1, b % 2, 0:T], mask[0:1, b % 2, :], -NEG, NEG, ALU.mult, ALU.add).then_inc(pen_ready, 1)

                def piece_maximum(i, n, p):
                    lo, hi = cols(p)
                    dve.wait_ge(scores_ready, (i * UB + n) * SL + p + 1)
                    nc.vector.tensor_reduce(piece_max[:, n % 2, p:p + 1], ps_s[:, p, 0:hi - lo], AX.X, ALU.max).then_inc(max_ready, 1)

                def negative_maximum(i, n):
                    dve.wait_ge(max_ready, (i * UB + n + 1) * SL)
                    if positive((i * UB + n - 3) * SL):
                        dve.wait_ge(exp_done, (i * UB + n - 3) * SL)
                    nc.vector.tensor_reduce(neg_max[:, n % 4:n % 4 + 1], piece_max[:, n % 2, :], AX.X, ALU.max, negate=True).then_inc(neg_max_ready, 1)

                def inverse_sum(i, n):
                    dve.wait_ge(exp_done, (i * UB + n + 1) * SL)
                    nc.vector.tensor_reduce(row_sum[:, n % 2:n % 2 + 1], piece_sum[:, n % 2, :], AX.X, ALU.add).then_inc(sum_ready, 1)
                    dve.wait_ge(sum_ready, i * UB + n + 1)
                    nc.vector.reciprocal(inv_row[:, n % 2:n % 2 + 1], row_sum[:, n % 2:n % 2 + 1]).then_inc(recip_ready, 1)
                    dve.wait_ge(recip_ready, i * UB + n + 1)
                    nc.vector.scalar_tensor_tensor(inv_sum[:, n % 2:n % 2 + 1], neg_max[:, n % 4:n % 4 + 1], -NEG / 2,
                                                   inv_row[:, n % 2:n % 2 + 1], ALU.is_lt, ALU.mult).then_inc(inv_ready, 1)

                def low(i, u, c):
                    k = u * SL + c
                    w = len(blocks(c)) * P
                    dve.wait_ge(hi_done, i * UB * SL + k + 1)
                    if positive(i * UB * SL + k + 1 - RINGC):
                        dve.wait_ge(pv_done, i * UB * SL + k + 1 - RINGC)
                    nc.vector.tensor_tensor(pt_lo[:, k % RINGC, 0:w], ps_t[:, k % 2, 0:w], pt_hi[:, k % RINGC, 0:w].bitcast(F32),
                                            ALU.subtract).then_inc(lo_done, 1)

                def add_x(i, u):
                    tile = bass.ds(i * UB + u, 1)
                    dve.wait_ge(inv_ready, i * UB + u + 1)
                    dve.wait_ge(pv_done, (i * UB + u + 1) * SL)
                    x_t = x_sb[:, tile, :].rearrange("p a n -> p (a n)")
                    nc.vector.scalar_tensor_tensor(x_t, ps_o[:, u % 2, 0:D], inv_sum[:, u % 2:u % 2 + 1], x_t, ALU.mult, ALU.add).then_inc(x_added, 1)

                norm_mean_var(nc, dve, x_sb, mean_var, norm)
                dve.wait_ge(norm[-1], 1)
                nc.vector.tensor_scalar(rstd_scaled[:, :], rstd[:, :], float(D) ** -0.5, None, ALU.mult).then_inc(scaled, 1)
                dve.wait_ge(scaled, 1)
                normalise(0, 0)
                normalise(0, 1)
                dve.wait_ge(zeroed, 2)
                penalty(0, 0)
                penalty(0, 1)
                low_x(0, 0)
                low_x(0, 1)
                normalise(0, 2)
                for n in range(2):
                    for p in range(SL):
                        piece_maximum(0, n, p)
                    negative_maximum(0, n)
                low_x(0, 2)
                normalise(0, 3)
                low(0, 0, 0)

                def body(i, last):
                    for u in range(UB):
                        for s in range(SL):
                            if exists(u + (s + 1) // SL, last):
                                low(i, u + (s + 1) // SL, (s + 1) % SL)
                            if exists(u + 2, last):
                                piece_maximum(i, u + 2, s)
                            if s == 0:
                                inverse_sum(i, u)
                            if s == 1:
                                if positive(i * UB + u):
                                    add_x(i, u - 1) if u else add_x(i - 1, UB - 1)
                                if exists(u + 4, last):
                                    normalise(i, u + 4)
                            if s == 2 and u % 2 == 0 and not last:
                                penalty(i, u // 2 + 2)
                        if exists(u + 2, last):
                            negative_maximum(i, u + 2)
                        if exists(u + 3, last):
                            low_x(i, u + 3)

                body(0, False)
                with dve.Fori(1, LAST) as i:
                    body(i, False)
                body(LAST, True)
                add_x(LAST, UB - 1)

            @block.tensor
            def _(pe):
                def transpose_x(i, v):
                    pe.wait_ge(xn_ready, i * UB + v + 1)
                    if positive(i * UB + v - 3):
                        pe.wait_ge(x_added, i * UB + v - 3)
                    if positive(i * UB + v - 1):
                        pe.wait_ge(xt_lo_done, i * UB + v - 1)
                    for c in range(DC):
                        last = nc.tensor.transpose(ps_o[:, v % 2, D + c * P:D + c * P + P], xn[:, v % 2, c * P:c * P + P], ident[:, :])
                    last.then_inc(xt_ready, 1)

                def scores(i, n, p):
                    b = (n // 2) % 2
                    t0, t1 = 4 * p, min(4 * p + 4, CT)
                    if p == 0:
                        pe.wait_ge(xt_lo_done, i * UB + n + 1)
                        if n % 2 == 0:
                            pe.wait_ge(tl_done, (i * 2 + n // 2 + 1) * 4)
                            pe.wait_ge(pen_ready, i * 2 + n // 2 + 1)
                    if positive((i * UB + n - 1) * SL + p + 1):
                        pe.wait_ge(exp_done, (i * UB + n - 1) * SL + p + 1)
                    out = ps_s[:, p, 0:(t1 - t0) * P]
                    for c in range(DC):
                        a_hi, a_lo = xt_hi[:, n % 2, c, :], xt_lo[:, n % 2, c, :]
                        k_hi, k_lo = t_hi[:, b, t0:t1, c, :], t_lo[:, b, t0:t1, c, :]
                        nc.tensor.matmul(out, a_hi, k_hi, start=c == 0, stop=False)
                        nc.tensor.matmul(out, a_hi, k_lo, start=False, stop=False)
                        if c == 0:
                            nc.tensor.matmul(out, row0[:, :], pen[:, b, t0 * P:t1 * P], start=False, stop=False)
                        last = nc.tensor.matmul(out, a_lo, k_hi, start=False, stop=c == DC - 1)
                    last.then_inc(scores_ready, 1)

                def transposes(i, u, c):
                    k = u * SL + c
                    pe.wait_ge(exp_done, (i * UB + u) * SL + c + 1)
                    if positive(i * UB * SL + k - 1):
                        pe.wait_ge(lo_done, i * UB * SL + k - 1)
                    for n, blk in enumerate(blocks(c)):
                        last = nc.tensor.transpose(ps_t[:, k % 2, n * P:n * P + P], prob[:, u % 2, blk * P:blk * P + P], ident[:, :])
                    last.then_inc(pt_ready, 1)

                def products(i, u, c):
                    k = u * SL + c
                    b = (u // 2) % 2
                    if c == 0:
                        if u % 2 == 0:
                            pe.wait_ge(rl_done, (i * 2 + u // 2 + 1) * 4)
                        if not (isinstance(i, int) and i * UB + u + 3 > NT):
                            pe.wait_ge(xt_lo_done, i * UB + u + 3)
                        if positive(i * UB + u - 1):
                            pe.wait_ge(x_added, i * UB + u - 1)
                    pe.wait_ge(lo_done, i * UB * SL + k + 1)
                    out = ps_o[:, u % 2, 0:D]
                    for n, blk in enumerate(blocks(c)):
                        p_hi, p_lo = pt_hi[:, k % RINGC, n * P:n * P + P], pt_lo[:, k % RINGC, n * P:n * P + P]
                        nc.tensor.matmul(out, p_hi, r_hi[:, b, blk, :], start=blk == 0, stop=False)
                        nc.tensor.matmul(out, p_hi, r_lo[:, b, blk, :], start=False, stop=False)
                        last = nc.tensor.matmul(out, p_lo, r_hi[:, b, blk, :], start=False, stop=blk == CT - 1)
                    last.then_inc(pv_done, 1)

                for v in range(2):
                    transpose_x(0, v)
                pe.wait_ge(row0_ready, 2)
                for p in range(SL):
                    scores(0, 0, p)
                for p in range(SL):
                    scores(0, 1, p)
                transpose_x(0, 2)
                transposes(0, 0, 0)

                def body(i, last):
                    for u in range(UB):
                        for s in range(SL):
                            if exists(u + (s + 1) // SL, last):
                                transposes(i, u + (s + 1) // SL, (s + 1) % SL)
                            products(i, u, s)
                            if exists(u + 2, last):
                                scores(i, u + 2, s)
                            if s == 2 and exists(u + 3, last):
                                transpose_x(i, u + 3)

                body(0, False)
                with pe.Fori(1, LAST) as i:
                    body(i, False)
                body(LAST, True)


ESLOTS = NT + E1 - 1
TO_INT = 1.5 * 2.0 ** 23


def route_to_slots(nc, x_sb, router_dram, sorted_dram, mean_var, rstd, half, ident, upper_bf, ones_bf, iota,
                   place, expert_of, max_prob):
    with ExitStack() as ctx:
        sb, psum, sem = scope(ctx, nc)
        norm = norm_memory(sb, sem, "norm4")
        router = sb("router6", [P, DC, E1])
        zeros = sb("zeros6", [P, D])
        xn = sb("xn6", [P, NT, D])
        xt = sb("xt6", [P, 2, 2 * DC * P])
        score = sb("score6", [P, NT, E1])
        best = sb("best6", [P, NT, 8])
        best_at = sb("best_at6", [P, NT, 8], U32)
        best_f = sb("best_f6", [P, NT])
        onehot = sb("onehot6", [P, NT, E1])
        onehot_bf = sb("onehot6_bf", [P, NT, E1], BF16)
        upto = sb("upto6", [P, E1, E1])
        share = sb("share6", [P, E1])
        share_int = sb("share6_int", [P, E1])
        slots = sb("slots6", [P, E1])
        slots_upto = sb("slots_upto6", [P, E1, E1])
        end = sb("end6", [P, E1])
        first_slot = sb("first_slot6", [P, E1])
        first_row = sb("first_row6", [P, E1])
        row = sb("row6", [P, NT, E1])
        own_row = sb("own_row6", [P, NT, E1])
        place_f = sb("place_f6", [P, NT])
        passed = sb("passed6", [P, ESLOTS, E1])
        passed_n = sb("passed_n6", [P, ESLOTS])
        passed_min = sb("passed_min6", [P, ESLOTS])
        ps_t = psum("ps_t6", [P, 2, 512])
        ps_l = psum("ps_l6", [P, NT * E1])
        ps_n = psum("ps_n6", [P, (NT + 1) * E1])

        router_loaded, zeros_ready, zeroed, upto_ready = sem("router6_loaded"), sem("zeros6s"), sem("zeroed6"), sem("upto6s")
        xn_ready, xt_ready, xt_copied, logits, scored = sem("xn6s"), sem("xt6s"), sem("xt6_copied"), sem("logits6"), sem("scored6")
        choice_begun, maxed, indexed, idx_f = sem("choice6_begun"), sem("best6s"), sem("best6_at"), sem("best6_f")
        prob_copied, is_own, is_own_bf, counted = sem("prob6"), sem("onehot6s"), sem("onehot6_bfs"), sem("counted6")
        shared, share_rounded, slots_ready, upto_slots, ends = sem("share6s"), sem("share6_ints"), sem("slots6s"), sem("slots_upto6s"), sem("end6s")
        first_slots, first_rows, rows, own_rows, places = sem("first_slot6s"), sem("first_row6s"), sem("row6s"), sem("own_row6s"), sem("place_f6s")
        place_ready, compared, passed_s, passed_max, table_ready = sem("place6"), sem("passed6s"), sem("passed_n6s"), sem("passed_min6s"), sem("expert_of6")
        scattered = sem("scattered6")

        with nc.Block() as block:
            @block.sync
            def _(sp):
                sp.dma_start(router[:, :, :], router_dram.rearrange("(c p) e -> p c e", p=P)).then_inc(router_loaded, 16)
                sp.wait_ge(zeros_ready, 1)
                sp.dma_start(sorted_dram.rearrange("(s p) d -> p s d", p=P), zeros[:, :].unsqueeze(1).to_broadcast([P, ESLOTS, D])).then_inc(zeroed, 16)

            @block.vector
            def _(dve):
                nc.vector.memset(zeros[:, :], 0.0).then_inc(zeros_ready, 1)
                by_row = iota[:, 0:E1].unsqueeze(2).to_broadcast([P, E1, E1])
                by_col = iota[:, 0:E1].unsqueeze(1).to_broadcast([P, E1, E1])
                nc.vector.tensor_tensor(upto[:, :, :], by_col, by_row, ALU.is_le).then_inc(upto_ready, 1)
                norm_mean_var(nc, dve, x_sb, mean_var, norm)
                dve.wait_ge(norm[-1], 1)
                for t in range(NT):
                    nc.vector.tensor_scalar(xn[:, t, :], x_sb[:, t, :], mean_var[:, t, 0:1], rstd[:, t:t + 1], ALU.subtract, ALU.mult).then_inc(xn_ready, 1)
                dve.wait_ge(scored, 1)
                dve.sem_inc(choice_begun, 1)
                for t in range(NT):
                    nc.vector.max(best[:, t, :], score[:, t, :]).then_inc(maxed, 1)
                dve.wait_ge(maxed, NT)
                dve.sem_inc(choice_begun, 1)
                for t in range(NT):
                    nc.vector.max_index(best_at[:, t, :], best[:, t, :], score[:, t, :]).then_inc(indexed, 1)
                nc.vector.tensor_copy(max_prob[:, :], best[:, :, 0]).then_inc(prob_copied, 1)
                dve.wait_ge(indexed, NT)
                nc.vector.tensor_copy(best_f[:, :], best_at[:, :, 0]).then_inc(idx_f, 1)
                dve.wait_ge(idx_f, 1)
                nc.vector.tensor_tensor(onehot[:, :, :], iota[:, 0:E1].unsqueeze(1).to_broadcast([P, NT, E1]),
                                        best_f[:, :].unsqueeze(2).to_broadcast([P, NT, E1]), ALU.is_equal).then_inc(is_own, 1)
                dve.wait_ge(is_own, 1)
                nc.vector.tensor_copy(onehot_bf[:, :, :], onehot[:, :, :]).then_inc(is_own_bf, 1)

                dve.wait_ge(counted, 1)
                nc.vector.tensor_scalar(share[:, :], ps_n[:, NT * E1:], 1.0 / P, (P - 1) / (2 * P), ALU.mult, ALU.add).then_inc(shared, 1)
                dve.wait_ge(shared, 1)
                nc.vector.tensor_scalar(share_int[:, :], share[:, :], TO_INT, None, ALU.add).then_inc(share_rounded, 1)
                dve.wait_ge(share_rounded, 1)
                nc.vector.tensor_scalar(slots[:, :], share_int[:, :], TO_INT, None, ALU.subtract).then_inc(slots_ready, 1)
                dve.wait_ge(slots_ready, 1)
                dve.wait_ge(upto_ready, 1)
                nc.vector.tensor_tensor(slots_upto[:, :, :], upto[:, :, :], slots[:, :].unsqueeze(1).to_broadcast([P, E1, E1]), ALU.mult).then_inc(upto_slots, 1)
                dve.wait_ge(upto_slots, 1)
                nc.vector.tensor_reduce(end[:, :], slots_upto[:, :, :], AX.X, ALU.add).then_inc(ends, 1)
                dve.wait_ge(ends, 1)
                nc.vector.tensor_tensor(first_slot[:, :], end[:, :], slots[:, :], ALU.subtract).then_inc(first_slots, 1)
                dve.wait_ge(first_slots, 1)
                nc.vector.tensor_scalar(first_row[:, :], first_slot[:, :], float(P), None, ALU.mult).then_inc(first_rows, 1)
                dve.wait_ge(first_rows, 1)
                nc.vector.tensor_tensor(row[:, :, :], ps_n[:, 0:NT * E1].rearrange("p (t e) -> p t e", t=NT),
                                        first_row[:, :].unsqueeze(1).to_broadcast([P, NT, E1]), ALU.add).then_inc(rows, 1)
                dve.wait_ge(rows, 1)
                nc.vector.tensor_tensor(own_row[:, :, :], row[:, :, :], onehot[:, :, :], ALU.mult).then_inc(own_rows, 1)
                dve.wait_ge(own_rows, 1)
                nc.vector.tensor_reduce(place_f[:, :], own_row[:, :, :], AX.X, ALU.add).then_inc(places, 1)
                dve.wait_ge(places, 1)
                nc.vector.tensor_copy(place[:, :], place_f[:, :]).then_inc(place_ready, 1)
                nc.vector.tensor_tensor(passed[:, :, :], iota[:, 0:ESLOTS].unsqueeze(2).to_broadcast([P, ESLOTS, E1]),
                                        end[:, :].unsqueeze(1).to_broadcast([P, ESLOTS, E1]), ALU.is_ge).then_inc(compared, 1)
                dve.wait_ge(compared, 1)
                nc.vector.tensor_reduce(passed_n[:, :], passed[:, :, :], AX.X, ALU.add).then_inc(passed_s, 1)
                dve.wait_ge(passed_s, 1)
                nc.vector.tensor_scalar(passed_min[:, :], passed_n[:, :], float(E1 - 1), None, ALU.min).then_inc(passed_max, 1)
                dve.wait_ge(passed_max, 1)
                nc.vector.tensor_copy(expert_of[:, :], passed_min[:, :]).then_inc(table_ready, 1)
                dve.wait_ge(table_ready, 1)
                dve.wait_ge(prob_copied, 1)

            @block.tensor
            def _(pe):
                pe.wait_ge(router_loaded, 16)

                def turn(g):
                    pe.wait_ge(xn_ready, 2 * g + 2)
                    if g >= 2:
                        pe.wait_ge(xt_copied, g - 1)
                    for t in range(2):
                        for c in range(DC):
                            last = nc.tensor.transpose(ps_t[:, g % 2, (t * DC + c) * P:(t * DC + c + 1) * P], xn[:, 2 * g + t, c * P:c * P + P], ident[:, :])
                    last.then_inc(xt_ready, 1)

                turn(0)
                for g in range(NT // 2):
                    if g + 1 < NT // 2:
                        turn(g + 1)
                    pe.wait_ge(xt_copied, g + 1)
                    for t in range(2):
                        for c in range(DC):
                            last = nc.tensor.matmul(ps_l[:, (2 * g + t) * E1:(2 * g + t + 1) * E1], xt[:, g % 2, (t * DC + c) * P:(t * DC + c + 1) * P],
                                                    router[:, c, :], start=c == 0, stop=c == DC - 1)
                    last.then_inc(logits, 1)
                pe.wait_ge(is_own_bf, 1)
                nc.tensor.matmul(ps_n[:, 0:NT * E1], upper_bf[:, :], onehot_bf[:, :, :].rearrange("p t e -> p (t e)"), start=True, stop=False, skip_group_check=True)
                for t in range(NT):
                    last = nc.tensor.matmul(ps_n[:, (t + 1) * E1:].rearrange("p (n e) -> p n e", e=E1), ones_bf[:, :],
                                            onehot_bf[:, t:t + 1, :].to_broadcast([P, NT - t, E1]), start=False, stop=t == NT - 1, skip_group_check=True)
                last.then_inc(counted, 1)

            @block.scalar
            def _(act):
                for g in range(NT // 2):
                    act.wait_ge(xt_ready, g + 1)
                    if g >= 2:
                        act.wait_ge(logits, g - 1)
                    nc.scalar.activation(xt[:, g % 2, :], ps_t[:, g % 2, :], ACT.Copy).then_inc(xt_copied, 1)
                act.wait_ge(logits, NT // 2)
                nc.scalar.activation(score[:, :, :], ps_l[:, :].rearrange("p (t e) -> p t e", t=NT), ACT.Sigmoid).then_inc(scored, 1)

            @block.gpsimd
            def _(pool):
                norm_rstd(nc, pool, mean_var, rstd, half, norm)
                pool.wait_ge(zeroed, 16)
                pool.wait_ge(xn_ready, NT)
                pool.wait_ge(place_ready, 1)
                for t in range(NT):
                    nc.gpsimd.indirect_dma_start(sorted_dram, bass.IndirectOffsetOnAxis(ap=place[:, t:t + 1], axis=0), xn[:, t, :], None).then_inc(scattered, 16)
                pool.wait_ge(scattered, 16 * NT)


def moe_slots(nc, x_sb, weights, sorted_dram, y_dram, out_dram, ident, place, expert_of, max_prob, w_loaded):
    gate_w, up_w, down_w = weights
    with ExitStack() as ctx:
        sb, psum, sem = scope(ctx, nc)
        xs = sb("xs7", [P, 2, D])
        xt = sb("xt7", [P, 2, DC, P])
        sig = sb("sig7", [P, H1])
        silu = sb("silu7", [P, H1])
        hid = sb("hid7", [P, H1])
        ht = sb("ht7", [P, HC1, P])
        y = sb("y7", [P, 2, D])
        back = sb("back7", [P, NT, D])
        ps_x = psum("ps_x7", [P, 512])
        ps_g = psum("ps_g7", [P, 512])
        ps_u = psum("ps_u7", [P, 512])
        ps_h = psum("ps_h7", [P, 512])
        ps_y = psum("ps_y7", [P, 2, 512])

        xs_loaded = [sem(f"xs7_loaded{j}") for j in range(2)]
        y_written = [sem(f"y7_written{j}") for j in range(2)]
        io_begun = sem("io7_begun")
        xt_ready, xt_copied, gate_done, up_done = sem("xt7s"), sem("xt7_copied"), sem("gate7"), sem("up7")
        sig_ready, silu_ready, hid_ready, ht_ready, ht_copied = sem("sig7s"), sem("silu7s"), sem("hid7s"), sem("ht7s"), sem("ht7_copied")
        y_done, y_copied = sem("y7s"), sem("y7_copied")
        returned = [sem(f"returned7_{q}") for q in range(4)]
        x_added, out_written = sem("x7_added"), sem("out_written")
        Q = NT // 4
        PAIRS = (ESLOTS - 3) // 2

        def all_slots(engine, step):
            for s in range(2):
                step(s, s)
            with engine.Fori(1, PAIRS) as i:
                for j in range(2):
                    step(i * 2 + j, j)
            for s in range(2 * PAIRS, ESLOTS):
                step(s, s % 2)

        def exists(s):
            return not isinstance(s, int) or s < ESLOTS

        with nc.Block() as block:
            @block.sync
            def _(sp):
                def load(s, j, n):
                    if positive(n):
                        sp.wait_ge(xt_ready, s - 1)
                        sp.sem_inc(io_begun, 1)
                    sp.dma_start(xs[:, j, :], sorted_dram[bass.ds(s * P, P), :]).then_inc(xs_loaded[j], 16)

                def step(s, j):
                    if exists(s + 2):
                        load(s + 2, j, 1)
                    sp.wait_ge(y_copied, s + 1)
                    sp.sem_inc(io_begun, 1)
                    sp.dma_start(y_dram[bass.ds(s * P, P), :], y[:, j, :]).then_inc(y_written[j], 16)

                load(0, 0, 0)
                load(1, 1, 0)
                all_slots(sp, step)
                for q in range(4):
                    sp.wait_ge(x_added, (q + 1) * Q)
                    sp.dma_start(out_dram[:, q * Q:(q + 1) * Q, :], x_sb[:, q * Q:(q + 1) * Q, :]).then_inc(out_written, 16)
                sp.wait_ge(out_written, 16 * 4)

            @block.tensor
            def _(pe):
                def turn_x(s, j):
                    pe.wait_ge(xs_loaded[j], 16 * (s // 2 + 1))
                    if positive(s):
                        pe.wait_ge(xt_copied, s)
                    for c in range(DC):
                        last = nc.tensor.transpose(ps_x[:, c * P:c * P + P], xs[:, j, c * P:c * P + P], ident[:, :])
                    last.then_inc(xt_ready, 1)

                def hidden(s, j):
                    e = pe.value_load(expert_of[0:1, bass.ds(s, 1)], min_val=0, max_val=E1 - 1)
                    pe.wait_ge(xt_copied, s + 1)
                    if positive(s):
                        pe.wait_ge(hid_ready, s)
                    for ps, w, done in ((ps_g, gate_w, gate_done), (ps_u, up_w, up_done)):
                        for c in range(DC):
                            last = nc.tensor.matmul(ps[:, :], xt[:, j, c, :], w[:, bass.ds(e, 1), c, :].rearrange("p a n -> p (a n)"),
                                                    start=c == 0, stop=c == DC - 1)
                        last.then_inc(done, 1)

                def turn_h(s):
                    pe.wait_ge(hid_ready, s + 1)
                    if positive(s):
                        pe.wait_ge(ht_copied, s)
                    for c in range(HC1):
                        last = nc.tensor.transpose(ps_h[:, c * P:c * P + P], hid[:, c * P:c * P + P], ident[:, :])
                    last.then_inc(ht_ready, 1)

                def output(s, j):
                    e = pe.value_load(expert_of[0:1, bass.ds(s, 1)], min_val=0, max_val=E1 - 1)
                    pe.wait_ge(ht_copied, s + 1)
                    if positive(s - 1):
                        pe.wait_ge(y_copied, s - 1)
                    for c in range(HC1):
                        last = nc.tensor.matmul(ps_y[:, j, 0:D], ht[:, c, :], down_w[:, bass.ds(e, 1), c, :].rearrange("p a n -> p (a n)"),
                                                start=c == 0, stop=c == HC1 - 1)
                    last.then_inc(y_done, 1)

                def step(s, j):
                    if exists(s + 1):
                        hidden(s + 1, 1 - j)
                    output(s, j)
                    if exists(s + 2):
                        turn_x(s + 2, j)
                    if exists(s + 1):
                        turn_h(s + 1)

                turn_x(0, 0)
                turn_x(1, 1)
                pe.wait_ge(w_loaded[0], w_loaded[1])
                hidden(0, 0)
                turn_h(0)
                all_slots(pe, step)

            @block.scalar
            def _(act):
                def copy_x(s, j):
                    act.wait_ge(xt_ready, s + 1)
                    if positive(s - 1):
                        act.wait_ge(up_done, s - 1)
                    nc.scalar.activation(xt[:, j, :, :], ps_x[:, 0:D].rearrange("p (c n) -> p c n", c=DC), ACT.Copy).then_inc(xt_copied, 1)

                def squash(s):
                    act.wait_ge(gate_done, s + 1)
                    if positive(s):
                        act.wait_ge(silu_ready, s)
                    nc.scalar.activation(sig[:, :], ps_g[:, :], ACT.Sigmoid).then_inc(sig_ready, 1)

                def step(s, j):
                    if exists(s + 1):
                        squash(s + 1)
                    act.wait_ge(y_done, s + 1)
                    if positive(s - 1):
                        act.wait_ge(y_written[j], 16 * (s // 2))
                        act.sem_inc(io_begun, 1)
                    nc.scalar.activation(y[:, j, :], ps_y[:, j, 0:D], ACT.Copy).then_inc(y_copied, 1)
                    if exists(s + 2):
                        copy_x(s + 2, j)

                copy_x(0, 0)
                copy_x(1, 1)
                squash(0)
                all_slots(act, step)

            @block.vector
            def _(dve):
                def step(s, j):
                    dve.wait_ge(sig_ready, s + 1)
                    nc.vector.tensor_tensor(silu[:, :], ps_g[:, :], sig[:, :], ALU.mult).then_inc(silu_ready, 1)
                    dve.wait_ge(silu_ready, s + 1)
                    dve.wait_ge(up_done, s + 1)
                    if positive(s):
                        dve.wait_ge(ht_ready, s)
                    nc.vector.tensor_tensor(hid[:, :], ps_u[:, :], silu[:, :], ALU.mult).then_inc(hid_ready, 1)
                    dve.wait_ge(ht_ready, s + 1)
                    if positive(s):
                        dve.wait_ge(y_done, s)
                    nc.vector.tensor_copy(ht[:, :, :], ps_h[:, :].rearrange("p (c n) -> p c n", c=HC1)).then_inc(ht_copied, 1)

                all_slots(dve, step)
                for t in range(NT):
                    dve.wait_ge(returned[t // Q], 16 * Q)
                    nc.vector.scalar_tensor_tensor(x_sb[:, t, :], back[:, t, :], max_prob[:, t:t + 1], x_sb[:, t, :], ALU.mult, ALU.add).then_inc(x_added, 1)

            @block.gpsimd
            def _(pool):
                for j in range(2):
                    pool.wait_ge(y_written[j], 16 * ((ESLOTS + 1 - j) // 2))
                for t in range(NT):
                    nc.gpsimd.indirect_dma_start(back[:, t, :], None, y_dram, bass.IndirectOffsetOnAxis(ap=place[:, t:t + 1], axis=0)).then_inc(returned[t // Q], 16)
def program(nc, x_dram, ctx_dram, ctx_t_dram, mask_dram, wq, wk, wv, wo, wk_ctx, wv_ctx, q_norm_w, k_norm_w,
            gate, expert_bias, w1, w3, w2, sw1, sw3, sw2, router_w, gate_w, up_w, down_w,
            ident_dram, iota_dram, upper_dram, causal_dram, rope_dram, out_dram):
    q_dram = nc.dram_tensor("q_scratch", (BG, P, GRP, L), F32).ap()
    k_dram = nc.dram_tensor("k_scratch", (BG, P, NK), F32).ap()
    v_dram = nc.dram_tensor("v_scratch", (BG, P, KB, HD), F32).ap()
    sorted_dram = nc.dram_tensor("sorted_scratch", (ESLOTS * P, D), F32).ap()
    y_dram = nc.dram_tensor("y_scratch", (ESLOTS * P, D), F32).ap()
    with ExitStack() as ctx:
        sb, psum, sem = scope(ctx, nc)
        x_sb = sb("x_sb", [P, NT, D])
        ident = sb("ident", [P, P])
        ident_bf = sb("ident_bf", [P, P], BF16)
        iota = sb("iota", [P, P])
        upper_bf = sb("upper_bf", [P, P], BF16)
        ones_bf = sb("ones_bf", [P, P], BF16)
        causal_bf = sb("causal_bf", [P, P], BF16)
        half = sb("half", [P, 64])
        mean_var = sb("mean_var", [P, NT, 2])
        rstd = sb("rstd", [P, NT])
        upper = sb("upper", [P, P])
        causal = sb("causal", [P, P])
        ident_loaded, x_loaded, consts_loaded, half_made, made = sem("ident_loaded"), sem("x_loaded"), sem("consts_loaded"), sem("half_made"), sem("consts_made")
        with nc.Block() as block:
            @block.sync
            def _(sp):
                sp.dma_start(ident[:, :], ident_dram).then_inc(ident_loaded, 16)
                sp.dma_start(x_sb[:, :, :], x_dram.rearrange("b (t p) d -> p (b t) d", p=P)).then_inc(x_loaded, 16)
                for dst, src in ((iota, iota_dram), (upper, upper_dram), (causal, causal_dram)):
                    sp.dma_start(dst[:, :], src).then_inc(consts_loaded, 16)

            @block.vector
            def _(dve):
                nc.vector.memset(half[:, :], -0.5).then_inc(half_made, 1)

        self_projections(nc, x_sb, x_loaded, ident_loaded, half_made, (wq, wk, wv), rope_dram, q_norm_w, k_norm_w, q_dram, k_dram, v_dram, mean_var, rstd, half, ident)
        with nc.Block() as block:
            @block.vector
            def _(dve):
                nc.vector.memset(ones_bf[:, :], 1.0).then_inc(made, 1)
                dve.wait_ge(consts_loaded, 48)
                dve.wait_ge(ident_loaded, 16)
                for dst, src in ((ident_bf, ident), (upper_bf, upper), (causal_bf, causal)):
                    nc.vector.tensor_copy(dst[:, :], src[:, :]).then_inc(made, 1)
                dve.wait_ge(made, 4)

        context_projections(nc, ctx_t_dram, wk_ctx, wv_ctx, k_norm_w, k_dram, v_dram, half, ident)
        attention(nc, q_dram, k_dram, v_dram, wo, x_sb, ident, ident_bf, causal_bf)

        moe_two_of_eight(nc, x_sb, gate, expert_bias, w1, w3, w2, sw1, sw3, sw2, mean_var, rstd, half, ident, ident_bf, iota)

        memory_attention(nc, x_sb, ctx_t_dram, ctx_dram, mask_dram, mean_var, rstd, half, ident)

        gate_sb = sb("gate_w", [P, E1, DC, H1])
        up_sb = sb("up_w", [P, E1, DC, H1])
        down_sb = sb("down_w", [P, E1, HC1, D])
        place = sb("place", [P, NT], U32)
        expert_of = sb("expert_of", [P, ESLOTS], U32)
        max_prob = sb("max_prob", [P, NT])
        w_loaded = sem("w6_loaded")
        with nc.Block() as block:
            @block.sync
            def _(sp):
                for dst, src in ((gate_sb, gate_w), (up_sb, up_w), (down_sb, down_w)):
                    sp.dma_start(dst[:, :, :, :], src.rearrange("e (c p) n -> p e c n", p=P)).then_inc(w_loaded, 16)
        route_to_slots(nc, x_sb, router_w, sorted_dram, mean_var, rstd, half, ident, upper_bf, ones_bf, iota, place, expert_of, max_prob)
        moe_slots(nc, x_sb, (gate_sb, up_sb, down_sb), sorted_dram, y_dram, out_dram.rearrange("b (t p) d -> p (b t) d", p=P),
                  ident, place, expert_of, max_prob, (w_loaded, 3 * 16))


def kernel(x, ctx_2048, mask_BxS2_bk0, L0_xattn_wq, L0_xattn_wk, L0_xattn_wv, L0_xattn_wo, L0_xattn_wk_ctx, L0_xattn_wv_ctx,
           L0_xattn_q_norm_w, L0_xattn_k_norm_w, L0_ffn_gate, L0_ffn_expert_bias, L0_ffn_w1, L0_ffn_w2, L0_ffn_w3,
           L0_ffn_shared_w1, L0_ffn_shared_w2, L0_ffn_shared_w3, L1_ffn_router_w, L1_ffn_gate_w, L1_ffn_up_w, L1_ffn_down_w):
    import numpy as np
    import concourse.bacc as bacc
    from concourse.bass_utils import run_bass_kernel_spmd

    context = np.zeros((B, TP, D), np.float32)
    context[:, :T] = np.asarray(ctx_2048)
    context_t = context.reshape(B * CT, P, DC, P).transpose(0, 3, 2, 1)
    inv_freq = np.float32(1) / np.float32(10000) ** (np.arange(0, HD, 2, dtype=np.float32) / np.float32(HD))
    angle = np.outer(np.arange(L, dtype=np.float32), inv_freq)
    rope = np.stack([np.concatenate([np.cos(angle), np.cos(angle)], 1), np.concatenate([-np.sin(angle), np.sin(angle)], 1)])
    arrays = [
        ("x", x), ("ctx", context), ("ctx_t", context_t), ("mask", mask_BxS2_bk0),
        ("wq", L0_xattn_wq), ("wk", L0_xattn_wk), ("wv", L0_xattn_wv), ("wo", L0_xattn_wo),
        ("wk_ctx", L0_xattn_wk_ctx), ("wv_ctx", L0_xattn_wv_ctx), ("q_norm_w", L0_xattn_q_norm_w), ("k_norm_w", L0_xattn_k_norm_w),
        ("gate", np.asarray(L0_ffn_gate).T), ("expert_bias", L0_ffn_expert_bias),
        ("w1", np.asarray(L0_ffn_w1).transpose(0, 2, 1)), ("w3", np.asarray(L0_ffn_w3).transpose(0, 2, 1)),
        ("w2", np.asarray(L0_ffn_w2).transpose(0, 2, 1)), ("sw1", np.asarray(L0_ffn_shared_w1).T),
        ("sw3", np.asarray(L0_ffn_shared_w3).T), ("sw2", np.asarray(L0_ffn_shared_w2).T),
        ("router_w", L1_ffn_router_w), ("gate_w", L1_ffn_gate_w), ("up_w", L1_ffn_up_w), ("down_w", L1_ffn_down_w),
        ("ident", np.eye(P, dtype=np.float32)), ("iota", np.tile(np.arange(P, dtype=np.float32), (P, 1))),
        ("upper", np.triu(np.ones((P, P), np.float32), 1)), ("causal", np.triu(np.full((P, P), NEG, np.float32), 1)),
        ("rope", rope.astype(np.float32))]
    nc = bacc.Bacc("TRN2", target_bir_lowering=False, num_devices=1)
    inputs, aps = {}, []
    for name, a in arrays:
        a = np.ascontiguousarray(a)
        inputs["in_" + name] = a
        aps.append(nc.dram_tensor("in_" + name, a.shape, mybir.dt.from_np(a.dtype), kind="ExternalInput").ap())
    out = nc.dram_tensor("out", (B, L, D), F32, kind="ExternalOutput").ap()
    program(nc, *aps, out)
    return run_bass_kernel_spmd(nc, [inputs], core_ids=[0]).results[0]["out"]
```

```python
from contextlib import ExitStack

import concourse.bass as bass
from concourse import mybir

F32 = mybir.dt.float32
F32R = mybir.dt.float32r
BF16 = mybir.dt.bfloat16
U32 = mybir.dt.uint32
U8 = mybir.dt.uint8
ALU = mybir.AluOpType
ACT = mybir.ActivationFunctionType
AX = mybir.AxisListType

P = 128
B, L, D = 8, 256, 256
T = 1601
NH, NKV, HD = 16, 4, 128
GRP = NH // NKV
DC = D // P
TOK = B * L
NT = TOK // P
QT = L // P
CT = -(-T // P)
TP = CT * P
KB = QT + CT
NK = KB * P
NKV_USED = QT * P + T
BG = B * NKV
NEG = -1.0e30
ROW = 1.0 / HD
E0, H0 = 8, 128
E1, H1 = 8, 512
HC1 = H1 // P
ESLOTS = NT + E1 - 1


def scope(ctx, nc):
    sems = []

    def sb(name, shape, dt=F32):
        return ctx.enter_context(nc.sbuf_tensor(name, shape, dt))

    def psum(name, shape, dt=F32):
        return ctx.enter_context(nc.psum_tensor(name, shape, dt))

    def sem(name):
        sems.append(ctx.enter_context(nc.semaphore(name)))
        return sems[-1]

    def clear(error, *_):
        if error:
            return
        nums = sorted(s.num for s in sems)
        with nc.Block() as block:
            @block.gpsimd
            def _(pool):
                first = 0
                for n in range(len(nums)):
                    if n + 1 == len(nums) or nums[n + 1] != nums[n] + 1:
                        pool.sem_clear(range(nums[first], nums[n] + 1))
                        first = n + 1

    ctx.push(clear)
    return sb, psum, sem


def positive(count):
    return not (isinstance(count, int) and count <= 0)


NORM_TILES = 4
NORM_PARTS = NT // NORM_TILES


def norm_memory(sb, sem, name):
    return (sb(name + "_stats", [P, NT, 6]), sb(name + "_var_eps", [P, NT]),
            sem(name + "_stats_ready"), sem(name + "_var_ready"), sem(name + "_eps_added"), sem(name + "_rstd_ready"))


def norm_mean_var(nc, dve, x_sb, mean_var, memory, part):
    stats, _, stats_ready, var_ready, _, _ = memory
    tiles = range(part * NORM_TILES, (part + 1) * NORM_TILES)
    for t in tiles:
        nc.vector.bn_stats(stats[:, t, :], x_sb[:, t, :]).then_inc(stats_ready, 1)
    for t in tiles:
        dve.wait_ge(stats_ready, t + 1)
        nc.vector.bn_aggr(mean_var[:, t, :], stats[:, t, :]).then_inc(var_ready, 1)


def norm_rstd(nc, pool, mean_var, rstd, half, memory, part):
    _, var_eps, _, var_ready, eps_added, rstd_ready = memory
    tiles = slice(part * NORM_TILES, (part + 1) * NORM_TILES)
    pool.wait_ge(var_ready, (part + 1) * NORM_TILES)
    nc.gpsimd.tensor_scalar(var_eps[:, tiles], mean_var[:, tiles, 1], LN_EPS, 1.0, ALU.add, ALU.mult).then_inc(eps_added, 1)
    pool.wait_ge(eps_added, part + 1)
    nc.gpsimd.tensor_tensor(rstd[:, tiles], var_eps[:, tiles], half[:, 0:NORM_TILES], ALU.pow).then_inc(rstd_ready, 1)


GRAN = 1 + NKV
W1 = (2 * NKV + NH) * HD
LN_EPS, RMS_EPS = 1e-5, 1e-6


def self_projections(nc, x_sb, x_loaded, ident_loaded, half_made, w_dram, rope_dram, qw_dram, kw_dram, q_dram, k_dram, v_dram,
                     mean_var, rstd, half, ident):
    wq_d, wk_d, wv_d = w_dram
    with ExitStack() as ctx:
        sb, psum, sem = scope(ctx, nc)
        norm = norm_memory(sb, sem, "norm1")
        w_raw = sb("w1_raw", [P, DC, W1])
        w_hi = sb("w1_hi", [P, DC, W1], F32R)
        w_lo = sb("w1_lo", [P, DC, W1], F32R)
        rope = sb("rope", [P, 2, QT, HD])
        weight = sb("norm_w", [P, 2, 2, HD])
        table = sb("rope_w", [P, 2, 2, QT, HD])
        xn = sb("xn1", [P, 2, D])
        xt_hi = sb("xt1_hi", [P, 2, DC, P], F32R)
        xt_lo = sb("xt1_lo", [P, 2, DC, P], F32R)
        squares = sb("squares1", [P, 2, GRP * HD])
        sq_sum = sb("sq_sum1", [P, GRAN, GRP])
        sq_mean = sb("sq_mean1", [P, GRAN, GRP])
        rms = sb("rms1", [P, GRAN, GRP])
        normed = sb("normed1", [P, GRAN, GRP * HD])
        by_cos = sb("by_cos", [P, GRAN, GRP * HD])
        by_sin = sb("by_sin", [P, GRAN, GRP * HD])
        roped = sb("roped", [P, GRAN, GRP * HD])
        out_t = sb("out_t1", [P, GRAN, GRP, P])
        v_out = sb("v_out1", [P, 2, NKV * HD])
        ps_p = psum("ps_p1", [P, GRAN, 512])
        ps_v = psum("ps_v1", [P, 512])
        ps_t = psum("ps_t1", [P, 512])
        ps_x = psum("ps_x1", [P, 512])

        tab_loaded = sem("tab_loaded")
        w_hi_done, w_lo_done = sem("w1_hi_done"), sem("w1_lo_done")
        table_ready = sem("table_ready")
        xn_ready, xt_ready = sem("xn1_ready"), sem("xt1_ready")
        xt_hi_done, xt_lo_done = sem("xt1_hi_done"), sem("xt1_lo_done")
        proj_done, v_done = sem("proj1_done"), sem("v1_done")
        square_done, mean_done, rms_done = sem("square1"), sem("mean1"), sem("rms1s")
        normed_done, cos_done, sin_done, roped_done = sem("normed1s"), sem("cos1"), sem("sin1"), sem("roped1")
        t_done, copied, sum_taken = sem("t1_done"), sem("t1_copied"), sem("sum1_taken")
        v_copied, store_begun = sem("v1_copied"), sem("store1_begun")
        out_written = [sem(f"out1_written{j}") for j in range(GRAN)]
        v_written = [sem(f"v1_written{j}") for j in range(2)]

        NB = NT // 2
        LAST = NB - 1
        WPIECES = W1 // 512
        w_loaded = [sem(f"w1_loaded{j}") for j in range(WPIECES)]

        def granule(f):
            return (f // GRAN) % 2, f % GRAN

        def w_cols(j):
            at = 0 if j == 0 else (2 * NKV + (j - 1) * GRP) * HD
            return slice(at, at + GRP * HD)

        LEAD = 4
        LASTG = 2 * GRAN
        CH = 3

        def exists(f, last):
            return not (last and f >= LASTG)

        with nc.Block() as block:
            @block.sync
            def _(sp):
                w_rows = [w.rearrange("(c p) n -> p c n", p=P) for w in (wk_d, wv_d, wq_d)]
                for j in range(WPIECES):
                    src = w_rows[j] if j < 2 else w_rows[2][:, :, (j - 2) * 512:(j - 1) * 512]
                    sp.dma_start(w_raw[:, :, j * 512:j * 512 + 512], src).then_inc(w_loaded[j], 16)
                for n in range(2):
                    sp.dma_start(rope[:, n, :, :], rope_dram[n].rearrange("(t p) d -> p t d", p=P)).then_inc(tab_loaded, 16)
                half_w = HD // 2
                for n, w in enumerate((kw_dram, qw_dram)):
                    row = w.rearrange("(a d) -> a d", a=1)
                    sp.dma_start(weight[:, n, 0, :], row.to_broadcast([P, HD])).then_inc(tab_loaded, 16)
                    sp.dma_start(weight[:, n, 1, 0:half_w], row[:, half_w:HD].to_broadcast([P, half_w])).then_inc(tab_loaded, 16)
                    sp.dma_start(weight[:, n, 1, half_w:HD], row[:, 0:half_w].to_broadcast([P, half_w])).then_inc(tab_loaded, 16)
                for j in range(GRAN):
                    sp.sem_inc(out_written[j], 16)
                for j in range(2):
                    sp.sem_inc(v_written[j], 16)
                with sp.Fori(0, NB) as i:
                    heads = [sp.snap(i * NKV + g) for g in range(NKV)]
                    for tt in range(2):
                        sp.wait_ge(v_copied, i * 2 + tt + 1)
                        sp.sem_inc(store_begun, 1)
                        sp.dma_start(v_dram[bass.ds(heads[0], NKV), :, 1 - tt, :].rearrange("g p d -> p g d"),
                                     v_out[:, tt, :].rearrange("p (g d) -> p g d", g=NKV)).then_inc(v_written[tt], 16)
                        for j in range(GRAN):
                            sp.wait_ge(copied, i * LASTG + tt * GRAN + j + 1)
                            sp.sem_inc(store_begun, 1)
                            if j == 0:
                                dst = k_dram[bass.ds(heads[0], NKV), :, (1 - tt) * P:(2 - tt) * P].rearrange("g p n -> p g n")
                            else:
                                dst = q_dram[bass.ds(heads[j - 1], 1), :, :, tt * P:tt * P + P].rearrange("a p h n -> p (a h) n")
                            sp.dma_start(dst, out_t[:, j, :, :]).then_inc(out_written[j], 16)
                for j in range(GRAN):
                    sp.wait_ge(out_written[j], 16 * (NT + 1))
                for j in range(2):
                    sp.wait_ge(v_written[j], 16 * (NB + 1))

            @block.scalar
            def _(act):
                def split_w(j):
                    act.wait_ge(w_loaded[j], 16)
                    cols = slice(j * 512, j * 512 + 512)
                    nc.scalar.activation(w_hi[:, :, cols], w_raw[:, :, cols], ACT.Copy).then_inc(w_hi_done, 1)

                def high(i, tt):
                    act.wait_ge(xt_ready, i * 2 + tt + 1)
                    if positive((i * 2 + tt - 1) * GRAN):
                        act.wait_ge(proj_done, (i * 2 + tt - 1) * GRAN)
                    nc.scalar.activation(xt_hi[:, tt % 2, :, :], ps_x[:, 0:D].rearrange("p (c n) -> p c n", c=DC),
                                         ACT.Copy).then_inc(xt_hi_done, 1)

                def square(i, f):
                    tt, j = granule(f)
                    act.wait_ge(proj_done, i * LASTG + f + 1)
                    if positive(i * LASTG + f - GRAN + 1):
                        act.wait_ge(mean_done, i * LASTG + f - GRAN + 1)
                    if positive(i * LASTG + f - 1):
                        act.wait_ge(square_done, (i * LASTG + f - 1) * GRP)
                    for h in range(GRP):
                        d = slice(h * HD, h * HD + HD)
                        nc.scalar.activation(squares[:, f % 2, d], ps_p[:, j, d], ACT.Square, accum_out=sq_sum[:, j, h:h + 1]).then_inc(square_done, 1)
                    if j == 0:
                        act.wait_ge(v_done, i * 2 + f // GRAN + 1)
                        act.wait_ge(v_written[tt], 16 * (i + f // LASTG + 1))
                        nc.scalar.activation(v_out[:, tt, :], ps_v[:, :], ACT.Copy).then_inc(v_copied, 1)

                def copy_out(i, f):
                    tt, j = granule(f)
                    act.wait_ge(t_done, i * LASTG + f + 1)
                    act.wait_ge(out_written[j], 16 * (i * 2 + tt + 1))
                    nc.scalar.activation(out_t[:, j, :, :], ps_t[:, :].rearrange("p (h n) -> p h n", h=GRP), ACT.Copy).then_inc(copied, 1)

                for j in range(2):
                    split_w(j)
                high(0, 0)
                for j in range(2, WPIECES):
                    split_w(j)
                for f in range(LEAD):
                    square(0, f)

                def body(i, last):
                    for f in range(LASTG):
                        tt, j = granule(f)
                        if j == 0 and exists(f + GRAN, last):
                            high(i, tt + 1)
                        if exists(f + LEAD, last):
                            square(i, f + LEAD)
                        copy_out(i, f)

                body(0, False)
                with act.Fori(1, LAST) as i:
                    body(i, False)
                body(LAST, True)

            @block.vector
            def _(dve):
                def normalise(t, slot):
                    tile = bass.ds(t, 1)
                    nc.vector.tensor_scalar(xn[:, slot, :], x_sb[:, tile, :].rearrange("p a n -> p (a n)"),
                                            mean_var[:, tile, 0], rstd[:, tile], ALU.subtract, ALU.mult).then_inc(xn_ready, 1)

                def low(i, tt):
                    dve.wait_ge(xt_hi_done, i * 2 + tt + 1)
                    if positive((i * 2 + tt - 1) * GRAN):
                        dve.wait_ge(proj_done, (i * 2 + tt - 1) * GRAN)
                    nc.vector.tensor_tensor(xt_lo[:, tt % 2, :, :], ps_x[:, 0:D].rearrange("p (c n) -> p c n", c=DC),
                                            xt_hi[:, tt % 2, :, :].bitcast(F32), ALU.subtract).then_inc(xt_lo_done, 1)

                def rotate(i, f):
                    tt, j = granule(f)
                    which = 0 if j == 0 else 1
                    dve.wait_ge(rms_done, i * LASTG + f + 1)
                    if positive(i * LASTG + f - GRAN + 1):
                        dve.wait_ge(cos_done, i * LASTG + f - GRAN + 1)
                    nc.vector.tensor_tensor(normed[:, j, :].rearrange("p (h d) -> p h d", h=GRP),
                                            ps_p[:, j, :].rearrange("p (h d) -> p h d", h=GRP),
                                            rms[:, j, :].unsqueeze(2).to_broadcast([P, GRP, HD]), ALU.mult).then_inc(normed_done, 1)
                    dve.wait_ge(normed_done, i * LASTG + f + 1)
                    src = normed[:, j, :].rearrange("p (h s d) -> p h s d", h=GRP, s=2)
                    dst = by_sin[:, j, :].rearrange("p (h s d) -> p h s d", h=GRP, s=2)
                    for s in range(2):
                        sines = table[:, which, 1, tt, s * (HD // 2):(s + 1) * (HD // 2)]
                        nc.vector.tensor_tensor(dst[:, :, s, :], src[:, :, 1 - s, :],
                                                sines.unsqueeze(1).to_broadcast([P, GRP, HD // 2]), ALU.mult).then_inc(sin_done, 1)
                    if positive(i * LASTG + f - GRAN + 1):
                        dve.wait_ge(roped_done, i * LASTG + f - GRAN + 1)
                    d = slice(CH * HD, GRP * HD)
                    nc.vector.tensor_tensor(by_cos[:, j, d].rearrange("p (h d) -> p h d", d=HD), normed[:, j, d].rearrange("p (h d) -> p h d", d=HD),
                                            table[:, which, 0, tt, :].unsqueeze(1).to_broadcast([P, GRP - CH, HD]), ALU.mult).then_inc(sin_done, 1)

                def add_parts(i, f):
                    j = f % GRAN
                    dve.wait_ge(sin_done, (i * LASTG + f + 1) * 3)
                    dve.wait_ge(cos_done, i * LASTG + f + 1)
                    if positive(i * LASTG + f - GRAN + 1):
                        dve.wait_ge(t_done, i * LASTG + f - GRAN + 1)
                    nc.vector.tensor_tensor(roped[:, j, :], by_cos[:, j, :], by_sin[:, j, :], ALU.add).then_inc(roped_done, 1)

                dve.wait_ge(x_loaded, 16)
                norm_mean_var(nc, dve, x_sb, mean_var, norm, 0)
                dve.wait_ge(norm[-1], 1)
                normalise(0, 0)
                normalise(1, 1)
                for part in range(1, NORM_PARTS):
                    norm_mean_var(nc, dve, x_sb, mean_var, norm, part)
                dve.wait_ge(norm[-1], NORM_PARTS)
                for j in range(WPIECES):
                    if j == 2:
                        low(0, 0)
                    cols = slice(j * 512, j * 512 + 512)
                    dve.wait_ge(w_hi_done, j + 1)
                    nc.vector.tensor_tensor(w_lo[:, :, cols], w_raw[:, :, cols], w_hi[:, :, cols].bitcast(F32),
                                            ALU.subtract).then_inc(w_lo_done, 1)
                dve.wait_ge(tab_loaded, 16 * 8)
                for n in range(2):
                    for m in range(2):
                        nc.vector.tensor_tensor(table[:, n, m, :, :], rope[:, m, :, :],
                                                weight[:, n, m, :].unsqueeze(1).to_broadcast([P, QT, HD]), ALU.mult).then_inc(table_ready, 1)
                dve.wait_ge(table_ready, 4)
                nc.vector.tensor_scalar(table[:, 1, :, :, :], table[:, 1, :, :, :], float(HD) ** -0.5, None, ALU.mult).then_inc(table_ready, 1)
                dve.wait_ge(table_ready, 5)
                rotate(0, 0)
                rotate(0, 1)
                add_parts(0, 0)

                def body(i, last):
                    for f in range(LASTG):
                        tt, j = granule(f)
                        if j == 0 and exists(f + GRAN, last):
                            low(i, tt + 1)
                            if exists(f + 2 * GRAN, last):
                                dve.wait_ge(xt_ready, i * 2 + tt + 1)
                                normalise(i * 2 + tt + 2, tt)
                        if exists(f + 2, last):
                            rotate(i, f + 2)
                        if exists(f + 1, last):
                            add_parts(i, f + 1)

                body(0, False)
                with dve.Fori(1, LAST) as i:
                    body(i, False)
                body(LAST, True)

            @block.gpsimd
            def _(pool):
                def root(i, f):
                    j = f % GRAN
                    pool.wait_ge(square_done, (i * LASTG + f + 1) * GRP)
                    pool.sem_inc(sum_taken, 1)
                    nc.gpsimd.tensor_scalar(sq_mean[:, j, :], sq_sum[:, j, :], 1.0 / HD, RMS_EPS, ALU.mult, ALU.add).then_inc(mean_done, 1)
                    pool.wait_ge(mean_done, i * LASTG + f + 1)
                    if positive(i * LASTG + f - GRAN + 1):
                        pool.wait_ge(normed_done, i * LASTG + f - GRAN + 1)
                    nc.gpsimd.tensor_tensor(rms[:, j, :], sq_mean[:, j, :], half[:, 0:GRP], ALU.pow).then_inc(rms_done, 1)

                def cosines(i, f):
                    tt, j = granule(f)
                    pool.wait_ge(normed_done, i * LASTG + f + 1)
                    if positive(i * LASTG + f - GRAN + 1):
                        pool.wait_ge(roped_done, i * LASTG + f - GRAN + 1)
                    nc.gpsimd.tensor_tensor(by_cos[:, j, 0:CH * HD].rearrange("p (h d) -> p h d", h=CH),
                                            normed[:, j, 0:CH * HD].rearrange("p (h d) -> p h d", h=CH),
                                            table[:, 0 if j == 0 else 1, 0, tt, :].unsqueeze(1).to_broadcast([P, CH, HD]),
                                            ALU.mult).then_inc(cos_done, 1)

                pool.wait_ge(half_made, 1)
                for part in range(NORM_PARTS):
                    norm_rstd(nc, pool, mean_var, rstd, half, norm, part)
                for f in range(LEAD):
                    root(0, f)
                pool.wait_ge(table_ready, 5)
                cosines(0, 0)
                cosines(0, 1)

                def body(i, last):
                    for f in range(LASTG):
                        if exists(f + LEAD, last):
                            root(i, f + LEAD)
                        if exists(f + 2, last):
                            cosines(i, f + 2)

                body(0, False)
                with pool.Fori(1, LAST) as i:
                    body(i, False)
                body(LAST, True)

            @block.tensor
            def _(pe):
                def transpose_x(i, tt):
                    pe.wait_ge(xn_ready, i * 2 + tt + 1)
                    if positive(i * 2 + tt):
                        pe.wait_ge(xt_lo_done, i * 2 + tt)
                    for c in range(DC):
                        last = nc.tensor.transpose(ps_x[:, c * P:c * P + P], xn[:, tt % 2, c * P:c * P + P], ident[:, :])
                    last.then_inc(xt_ready, 1)

                def three(out, slot, cols):
                    for c in range(DC):
                        a_hi, a_lo = xt_hi[:, slot, c, :], xt_lo[:, slot, c, :]
                        nc.tensor.matmul(out, a_hi, w_hi[:, c, cols], start=c == 0, stop=False)
                        nc.tensor.matmul(out, a_hi, w_lo[:, c, cols], start=False, stop=False)
                        last = nc.tensor.matmul(out, a_lo, w_hi[:, c, cols], start=False, stop=c == DC - 1)
                    return last

                def project(i, f):
                    tt, j = granule(f)
                    if j == 0:
                        pe.wait_ge(xt_lo_done, i * 2 + f // GRAN + 1)
                    if positive(i * LASTG + f - GRAN + 1):
                        pe.wait_ge(normed_done, i * LASTG + f - GRAN + 1)
                        pe.wait_ge(square_done, (i * LASTG + f - GRAN + 1) * GRP)
                    if isinstance(i, int) and i == 0 and f < GRAN:
                        pe.wait_ge(w_lo_done, 2 + j)
                    if j == 0:
                        three(ps_p[:, j, :], tt, w_cols(j)).then_inc(proj_done, 1)
                        if positive(i * 2 + f // GRAN):
                            pe.wait_ge(v_copied, i * 2 + f // GRAN)
                        three(ps_v[:, :], tt, slice(NKV * HD, 2 * NKV * HD)).then_inc(v_done, 1)
                    else:
                        three(ps_p[:, j, :], tt, w_cols(j)).then_inc(proj_done, 1)

                def transposes(i, f):
                    j = f % GRAN
                    pe.wait_ge(roped_done, i * LASTG + f + 1)
                    if positive(i * LASTG + f):
                        pe.wait_ge(copied, i * LASTG + f)
                    for h in range(GRP):
                        last = nc.tensor.transpose(ps_t[:, h * P:h * P + P], roped[:, j, h * P:h * P + P], ident[:, :])
                    last.then_inc(t_done, 1)

                pe.wait_ge(ident_loaded, 16)
                transpose_x(0, 0)
                for f in range(LEAD):
                    project(0, f)

                def body(i, last):
                    for f in range(LASTG):
                        tt, j = granule(f)
                        if j == 0 and exists(f + GRAN, last):
                            transpose_x(i, tt + 1)
                        if exists(f + LEAD, last):
                            project(i, f + LEAD)
                        transposes(i, f)

                body(0, False)
                with pe.Fori(1, LAST) as i:
                    body(i, False)
                body(LAST, True)
def context_projections(nc, ctx_dram, wk_dram, wv_dram, kw_dram, q_dram, k_dram, v_dram, half, ident, operands):
    NTILE = B * CT
    TB = 4
    NB = NTILE // TB
    LAST = NB - 1
    END_BODIES = 3
    FIRST_BODIES = -(-CT // TB)
    LEAD = 2
    W = NKV * HD
    with ExitStack() as ctx:
        sb, psum, sem = scope(ctx, nc)
        w_raw = sb("w2_raw", [P, DC, 2 * W])
        w_hi = sb("w2_hi", [P, DC, 2 * W], F32R)
        w_lo = sb("w2_lo", [P, DC, 2 * W], F32R)
        kw_col = sb("kw_col", [P, 1])
        c_raw = sb("c_raw", [P, 2, 2, DC * P])
        c_hi = sb("c_hi", [P, 2, 2, DC, P], F32R)
        c_lo = sb("c_lo", [P, 2, 2, DC, P], F32R)
        squares = sb("squares2", [P, 2, W])
        sq_sum = sb("sq_sum2", [P, TB, NKV])
        sq_mean = sb("sq_mean2", [P, TB, NKV])
        rms = sb("rms2", [P, TB, NKV])
        normed = sb("normed2", [P, TB, W])
        k_out = sb("k_out2", [P, TB, NKV, P])
        v_out = sb("v_out2", [P, TB, W])
        ps_k = psum("ps_k2", [P, 4, 512])
        ps_v = psum("ps_v2", [P, 2, 512])
        ps_t = psum("ps_t2", [P, 2, 512])

        wk_loaded, wv_loaded, kw_loaded = sem("wk2_loaded"), sem("wv2_loaded"), sem("kw_loaded")
        c_loaded = [sem(f"c_loaded{j}") for j in range(2)]
        w_hi_done, w_lo_done = sem("w2_hi_done"), sem("w2_lo_done")
        c_hi_done, c_lo_done = sem("c_hi_done"), sem("c_lo_done")
        k_done, v_done = sem("k2_done"), sem("v2_done")
        square_done, sum_done, sum_taken = sem("square2"), sem("sum2"), sem("sum2_taken")
        mean_done, rms_done, normed_done = sem("mean2"), sem("rms2s"), sem("normed2s")
        t_done, k_copied, v_copied, store_begun = sem("t2_done"), sem("k2_copied"), sem("v2_copied"), sem("store2_begun")
        load_begun = sem("load2_begun")
        k_written = [sem(f"k2_written{j}") for j in range(TB)]
        v_written = [sem(f"v2_written{j}") for j in range(TB)]

        def exists(t, last):
            return not (last and t >= TB)

        with nc.Block() as block:
            @block.sync
            def _(sp):
                sp.dma_start(w_raw[:, :, 0:W], wk_dram.rearrange("(c p) n -> p c n", p=P)).then_inc(wk_loaded, 16)
                sp.dma_start(w_raw[:, :, W:2 * W], wv_dram.rearrange("(c p) n -> p c n", p=P)).then_inc(wv_loaded, 16)
                sp.dma_start(kw_col[:, :], kw_dram.rearrange("(p a) -> p a", a=1)).then_inc(kw_loaded, 16)

                for j in range(TB):
                    sp.sem_inc(k_written[j], 16)
                    sp.sem_inc(v_written[j], 16)

                def body(i):
                    for t in range(TB):
                        tile = i * TB + t
                        g0, at = (tile // CT) * NKV, (tile % CT)
                        sp.wait_ge(v_copied, tile + 1)
                        sp.sem_inc(store_begun, 1)
                        sp.dma_start(v_dram[bass.ds(g0, NKV), :, bass.ds(at + QT, 1), :].rearrange("g p a d -> p g (a d)"),
                                     v_out[:, t, :].rearrange("p (g d) -> p g d", g=NKV)).then_inc(v_written[t], 16)
                        sp.wait_ge(k_copied, tile + 1)
                        sp.sem_inc(store_begun, 1)
                        sp.dma_start(k_dram[bass.ds(g0, NKV), :, bass.ds(at * P + QT * P, P)].rearrange("g p n -> p g n"),
                                     k_out[:, t, :, :]).then_inc(k_written[t], 16)

                with sp.Fori(0, NB - END_BODIES) as i:
                    body(i)
                for j in range(TB):
                    sp.wait_ge(k_written[j], 16 * (FIRST_BODIES + 1))
                    sp.wait_ge(v_written[j], 16 * (FIRST_BODIES + 1))
                load_kq(sp, 0, q_dram, k_dram, operands)
                load_v(sp, 0, v_dram, operands)
                with sp.Fori(NB - END_BODIES, NB) as i:
                    body(i)
                for j in range(TB):
                    sp.wait_ge(k_written[j], 16 * (NB + 1))
                    sp.wait_ge(v_written[j], 16 * (NB + 1))

            def pair_place(i, p):
                return p % 2, i + p // 2

            @block.scalar
            def _(act):
                def load(i, p):
                    act.sem_inc(load_begun, 1)
                    act.dma_start(c_raw[:, p % 2, :, :], ctx_dram[bass.ds((i * 2 + p) * 2, 2)].rearrange("t p c n -> p t (c n)")).then_inc(c_loaded[p % 2], 16)

                load(0, 0)
                load(0, 1)

                def high_w(h):
                    cols = slice(h * 256, h * 256 + 256)
                    nc.scalar.activation(w_hi[:, :, cols], w_raw[:, :, cols], ACT.Copy).then_inc(w_hi_done, 1)

                def high(i, p):
                    j, before = pair_place(i, p)
                    act.wait_ge(c_loaded[j], 16 * (before + 1))
                    if positive((i * 2 + p - 1) * 2):
                        act.wait_ge(v_done, (i * 2 + p - 1) * 2)
                    nc.scalar.activation(c_hi[:, j, :, :, :], c_raw[:, j, :, :].rearrange("p t (c n) -> p t c n", c=DC), ACT.Copy).then_inc(c_hi_done, 1)

                def square_and_v(i, t):
                    act.wait_ge(k_done, i * TB + t + 1)
                    if positive(i * TB + t - 1):
                        act.wait_ge(sum_done, i * TB + t - 1)
                    nc.scalar.activation(squares[:, t % 2, :], ps_k[:, t % TB, :], ACT.Square).then_inc(square_done, 1)
                    act.wait_ge(v_done, i * TB + t + 1)
                    act.wait_ge(v_written[t % TB], 16 * (i + t // TB + 1))
                    nc.scalar.activation(v_out[:, t % TB, :], ps_v[:, t % 2, :], ACT.Copy).then_inc(v_copied, 1)

                def copy_k(i, t):
                    act.wait_ge(t_done, i * TB + t + 1)
                    act.wait_ge(k_written[t % TB], 16 * (i + 1))
                    nc.scalar.activation(k_out[:, t, :, :], ps_t[:, t % 2, :].rearrange("p (h n) -> p h n", h=NKV),
                                         ACT.Copy, scale=kw_col[:, :]).then_inc(k_copied, 1)

                for p, loaded in enumerate((wk_loaded, wv_loaded)):
                    act.wait_ge(loaded, 16)
                    high_w(2 * p)
                    high_w(2 * p + 1)
                    high(0, p)
                act.wait_ge(kw_loaded, 16)
                for p in range(2):
                    act.wait_ge(c_lo_done, p + 1)
                    load(0, p + 2)
                for t in range(LEAD):
                    square_and_v(0, t)

                def body(i, last, loads):
                    for t in range(TB):
                        if t % 2 == 0 and not last:
                            high(i, t // 2 + 2)
                        if t % 2 == 1 and loads:
                            act.wait_ge(c_lo_done, i * 2 + t // 2 + 3)
                            load(i, t // 2 + 4)
                        if exists(t + LEAD, last):
                            square_and_v(i, t + LEAD)
                        copy_k(i, t)

                body(0, False, True)
                with act.Fori(1, LAST - 1) as i:
                    body(i, False, True)
                body(LAST - 1, False, False)
                body(LAST, True, False)

            @block.vector
            def _(dve):
                def low(i, p):
                    j, _ = pair_place(i, p)
                    dve.wait_ge(c_hi_done, i * 2 + p + 1)
                    if positive((i * 2 + p - 1) * 2):
                        dve.wait_ge(v_done, (i * 2 + p - 1) * 2)
                    nc.vector.tensor_tensor(c_lo[:, j, :, :, :], c_raw[:, j, :, :].rearrange("p t (c n) -> p t c n", c=DC),
                                            c_hi[:, j, :, :, :].bitcast(F32), ALU.subtract).then_inc(c_lo_done, 1)

                def sum_squares(i, t):
                    dve.wait_ge(square_done, i * TB + t + 1)
                    if positive(i * TB + t - TB + 1):
                        dve.wait_ge(mean_done, i * TB + t - TB + 1)
                    nc.vector.tensor_reduce(sq_sum[:, t % TB, :], squares[:, t % 2, :].rearrange("p (h d) -> p h d", h=NKV),
                                            AX.X, ALU.add).then_inc(sum_done, 1)

                def normalise(i, t):
                    dve.wait_ge(rms_done, i * TB + t + 1)
                    if positive(i * TB + t - TB + 1):
                        dve.wait_ge(t_done, i * TB + t - TB + 1)
                    nc.vector.tensor_tensor(normed[:, t % TB, :].rearrange("p (h d) -> p h d", h=NKV),
                                            ps_k[:, t % TB, :].rearrange("p (h d) -> p h d", h=NKV),
                                            rms[:, t % TB, :].unsqueeze(2).to_broadcast([P, NKV, HD]), ALU.mult).then_inc(normed_done, 1)

                for p in range(2):
                    for h in range(2 * p, 2 * p + 2):
                        cols = slice(h * 256, h * 256 + 256)
                        dve.wait_ge(w_hi_done, h + 1)
                        nc.vector.tensor_tensor(w_lo[:, :, cols], w_raw[:, :, cols], w_hi[:, :, cols].bitcast(F32),
                                                ALU.subtract).then_inc(w_lo_done, 1)
                    low(0, p)
                for t in range(LEAD):
                    sum_squares(0, t)
                normalise(0, 0)

                def body(i, last):
                    for t in range(TB):
                        if t % 2 == 0 and not last:
                            low(i, t // 2 + 2)
                        if exists(t + 1, last):
                            normalise(i, t + 1)
                        if exists(t + LEAD, last):
                            sum_squares(i, t + LEAD)

                body(0, False)
                with dve.Fori(1, LAST) as i:
                    body(i, False)
                body(LAST, True)

            @block.gpsimd
            def _(pool):
                def root(i, t):
                    pool.wait_ge(sum_done, i * TB + t + 1)
                    pool.sem_inc(sum_taken, 1)
                    nc.gpsimd.tensor_scalar(sq_mean[:, t, :], sq_sum[:, t, :], 1.0 / HD, RMS_EPS, ALU.mult, ALU.add).then_inc(mean_done, 1)
                    pool.wait_ge(mean_done, i * TB + t + 1)
                    if positive(i * TB + t - TB + 1):
                        pool.wait_ge(normed_done, i * TB + t - TB + 1)
                    nc.gpsimd.tensor_tensor(rms[:, t, :], sq_mean[:, t, :], half[:, 0:NKV], ALU.pow).then_inc(rms_done, 1)

                for t in range(TB):
                    root(0, t)
                with pool.Fori(1, NB) as i:
                    for t in range(TB):
                        root(i, t)

            @block.tensor
            def _(pe):
                def three(out, j, tt, cols):
                    for c in range(DC):
                        a_hi, a_lo = c_hi[:, j, tt, c, :], c_lo[:, j, tt, c, :]
                        nc.tensor.matmul(out, a_hi, w_hi[:, c, cols], start=c == 0, stop=False)
                        nc.tensor.matmul(out, a_hi, w_lo[:, c, cols], start=False, stop=False)
                        last = nc.tensor.matmul(out, a_lo, w_hi[:, c, cols], start=False, stop=c == DC - 1)
                    return last

                def project(i, t):
                    j, tt = (t // 2) % 2, t % 2
                    if not positive(i * TB + t):
                        pe.wait_ge(w_lo_done, 2)
                    if tt == 0:
                        pe.wait_ge(c_lo_done, i * 2 + t // 2 + 1)
                    if positive(i * TB + t - TB + 1):
                        pe.wait_ge(normed_done, i * TB + t - TB + 1)
                    three(ps_k[:, t % TB, :], j, tt, slice(0, W)).then_inc(k_done, 1)
                    if positive(i * TB + t - 1):
                        pe.wait_ge(v_copied, i * TB + t - 1)
                    if not positive(i * TB + t):
                        pe.wait_ge(w_lo_done, 4)
                    three(ps_v[:, t % 2, :], j, tt, slice(W, 2 * W)).then_inc(v_done, 1)

                def transposes(i, t):
                    pe.wait_ge(normed_done, i * TB + t + 1)
                    if positive(i * TB + t - 1):
                        pe.wait_ge(k_copied, i * TB + t - 1)
                    for h in range(NKV):
                        last = nc.tensor.transpose(ps_t[:, t % 2, h * P:h * P + P], normed[:, t, h * HD:h * HD + HD], ident[:, :])
                    last.then_inc(t_done, 1)

                for t in range(LEAD):
                    project(0, t)

                def body(i, last):
                    for t in range(TB):
                        if exists(t + LEAD, last):
                            project(i, t + LEAD)
                        transposes(i, t)

                body(0, False)
                with pe.Fori(1, LAST) as i:
                    body(i, False)
                body(LAST, True)


UNITS = 2 * QT
BODY_IT = 2
BODY_U = BODY_IT * UNITS
SLOTS = 8
PC = 512
PB = 4
RING = 4
KQ_PIECES, V_PIECES = 6, 4
KPIECE = NK // 4


def blocks_of(qt, c):
    return [k for k in (2 * c, 2 * c + 1) if (0 if qt else 1) <= k < KB]


def attention_operands(ctx, nc):
    sb, _, sem = scope(ctx, nc)
    return sb("raw_q", [P, GRP, L]), sb("raw_k", [P, NK]), sb("raw_v", [P, KB * HD]), sem("kq_loaded"), sem("v_loaded")


def load_kq(sp, it, q_dram, k_dram, operands):
    raw_q, raw_k, _, kq_loaded, _ = operands
    sp.dma_start(raw_q[:, :, :], q_dram[bass.ds(it, 1)].rearrange("a p h q -> p (a h) q")).then_inc(kq_loaded, 16)
    sp.dma_start(raw_k[:, :], k_dram[bass.ds(it, 1)].rearrange("a p n -> p (a n)")).then_inc(kq_loaded, 16)


def load_v(sp, it, v_dram, operands):
    _, _, raw_v, _, v_loaded = operands
    sp.dma_start(raw_v[:, :], v_dram[bass.ds(it, 1)].rearrange("a p k n -> p (a k n)")).then_inc(v_loaded, 16)


def attention(nc, q_dram, k_dram, v_dram, wo_dram, x_sb, ident, ident_bf, mask_bf, operands):
    raw_q, raw_k, raw_v, kq_loaded, v_loaded = operands
    with ExitStack() as ctx:
        sb, psum, sem = scope(ctx, nc)
        q_hi = sb("q_hi", [P, BODY_IT, GRP, L], F32R)
        q_lo = sb("q_lo", [P, BODY_IT, GRP, L], F32R)
        k_hi = sb("k_hi", [P, BODY_IT, NK], F32R)
        k_lo = sb("k_lo", [P, BODY_IT, NK], F32R)
        v_hi = sb("v_hi", [P, BODY_IT, KB * HD], F32R)
        v_lo = sb("v_lo", [P, BODY_IT, KB * HD], F32R)
        prob = sb("prob", [P, PB, NK])
        pt_hi = sb("pt_hi", [P, RING, PC], F32R)
        pt_lo = sb("pt_lo", [P, RING, PC], F32R)
        wo = sb("wo", [P, NH, D])
        o_t = sb("o_t", [P, 2, GRP, P])
        piece_max = sb("piece_max", [P, 2, 4])
        neg_max = sb("neg_max", [P, PB])
        piece_sum = sb("piece_sum", [P, 2, 4])
        row_sum = sb("row_sum", [P, 2])
        inv_sum = sb("inv_sum", [P, PB])
        ps_s = psum("ps_s", [P, 4, PC])
        ps_t = psum("ps_t", [P, 2, PC])
        ps_o = psum("ps_o", [P, 2, PC])

        wo_loaded = sem("wo_loaded")
        kq_hi, kq_lo = sem("kq_hi_split"), sem("kq_lo_split")
        vv_hi, vv_lo = sem("v_hi_split"), sem("v_lo_split")
        scores_ready = sem("scores_ready")
        max_ready = sem("max_ready")
        neg_max_ready = sem("neg_max_ready")
        exp_done = sem("exp_done")
        sum_ready = sem("sum_ready")
        inv_ready = sem("inv_ready")
        norm_begun, norm_done = sem("norm_begun"), sem("norm_done")
        t_ready = sem("t_ready")
        hi_done, lo_done = sem("pt_hi_done"), sem("pt_lo_done")
        pv_done = sem("pv_done")
        o_copied = sem("o_copied")
        y_ready, y_added = sem("y_ready"), sem("y_added")
        prob_zeroed = sem("prob_zeroed")

        T_CREDIT, PV_CREDIT, O_CREDIT, YR_CREDIT, YA_CREDIT, N_CREDIT = 16, 8, 2, 2, 1, 8
        LAST = BG // BODY_IT - 1

        def head(i, n):
            return (n // 8) % BODY_IT, (n // 4) % QT, n % 4

        def score_cols(qt, p):
            return max(p * PC, 0 if qt else P), min((p + 1) * PC, NKV_USED + 1)

        with nc.Block() as block:
            @block.sync
            def _(sp):
                sp.dma_start(wo[:, :, :], wo_dram.rearrange("(h p) n -> p h n", p=P)).then_inc(wo_loaded, 16)
                with sp.Fori(1, BG) as it:
                    sp.wait_ge(kq_hi, it * KQ_PIECES)
                    sp.wait_ge(kq_lo, it * KQ_PIECES)
                    load_kq(sp, it, q_dram, k_dram, operands)
                    sp.wait_ge(vv_hi, it * V_PIECES)
                    sp.wait_ge(vv_lo, it * V_PIECES)
                    load_v(sp, it, v_dram, operands)

            def kq_piece(gi, x):
                if x < 2:
                    h = slice(2 * x, 2 * x + 2)
                    return raw_q[:, h, :], q_hi[:, gi, h, :], q_lo[:, gi, h, :]
                k = slice((x - 2) * KPIECE, (x - 1) * KPIECE)
                return raw_k[:, k], k_hi[:, gi, k], k_lo[:, gi, k]

            def v_piece(gi, x):
                k = slice(x * PC, min((x + 1) * PC, KB * HD))
                return raw_v[:, k], v_hi[:, gi, k], v_lo[:, gi, k]

            KQ_PLAN = {0: [(1, 4)], 1: [(1, 5)], 2: [(2, 0), (2, 1)], 3: [(2, 2), (2, 3)], 4: [(2, 4)],
                       5: [(2, 5)], 6: [(3, 0), (3, 1)], 7: [(3, 2), (3, 3)]}
            V_PLAN = {0: [(1, 0)], 1: [(1, 1)], 2: [(1, 2), (1, 3)], 3: [],
                      4: [(2, 0)], 5: [(2, 1)], 6: [(2, 2), (2, 3)], 7: []}

            @block.scalar
            def _(act):
                def exp(i, n, p):
                    _, qt, _ = head(i, n)
                    lo, hi = score_cols(qt, p)
                    hi = min(hi, NKV_USED)
                    if p == 0:
                        act.wait_ge(neg_max_ready, i * 16 + n + 1)
                    act.wait_ge(t_ready, T_CREDIT + i * 64 + 8 * (n // 2 - 2) + 2 * p + 2)
                    if p == 0:
                        act.wait_ge(sum_ready, i * 16 + n - 1 + 2)
                    nc.scalar.activation(prob[:, n % PB, lo:hi], ps_s[:, p, lo - p * PC:hi - p * PC], ACT.Exp,
                                         bias=neg_max[:, n % PB:n % PB + 1],
                                         accum_out=piece_sum[:, n % 2, p:p + 1]).then_inc(exp_done, 1)

                def high(i, u, c):
                    k = 8 * u + c
                    qt = (u // 2) % QT
                    bs = [x % 2 for x in blocks_of(qt, c)]
                    cols = slice(bs[0] * 256, bs[-1] * 256 + 256)
                    act.wait_ge(t_ready, T_CREDIT + i * 64 + k + 1)
                    act.wait_ge(pv_done, PV_CREDIT + i * 64 + k + 1 - RING)
                    nc.scalar.activation(pt_hi[:, k % RING, cols], ps_t[:, k % 2, cols], ACT.Copy).then_inc(hi_done, 1)

                def split_kq(i, it, x):
                    raw, hi, _ = kq_piece(it % BODY_IT, x)
                    act.wait_ge(kq_loaded, (i * BODY_IT + it + 1) * 32)
                    if it >= BODY_IT:
                        act.wait_ge(scores_ready, i * 64 + 32 * (it - 1))
                    nc.scalar.activation(hi, raw, ACT.Copy).then_inc(kq_hi, 1)

                def split_v(i, it, x):
                    raw, hi, _ = v_piece(it % BODY_IT, x)
                    act.wait_ge(v_loaded, (i * BODY_IT + it + 1) * 16)
                    if it >= 1:
                        act.wait_ge(pv_done, PV_CREDIT + i * 64 + 32 * (it - 1))
                    nc.scalar.activation(hi, raw, ACT.Copy).then_inc(vv_hi, 1)

                def copy_o(i, u):
                    act.wait_ge(pv_done, PV_CREDIT + i * 64 + 8 * u + 8)
                    if u % 2 == 0:
                        act.wait_ge(y_ready, YR_CREDIT + i * (BODY_U // 2) + u // 2 + 1 - 2)
                    pp = u % 2
                    nc.scalar.activation(o_t[:, (u // 2) % 2, 2 * pp:2 * pp + 2, :],
                                         ps_o[:, u % 2, 0:2 * P].rearrange("p (h q) -> p h q", h=2),
                                         ACT.Copy).then_inc(o_copied, 1)

                for x in range(KQ_PIECES):
                    split_kq(0, 0, x)
                for x in range(V_PIECES):
                    split_v(0, 0, x)
                act.wait_ge(prob_zeroed, 1)
                for n in range(3):
                    for p in range(4):
                        exp(0, n, p)
                for x in range(4):
                    split_kq(0, 1, x)
                high(0, 0, 0)

                def body(i, last):
                    for u in range(BODY_U):
                        more = not (last and u >= BODY_U - 2)
                        for s in range(SLOTS):
                            if s < 7 or not (last and u == BODY_U - 1):
                                high(i, u + (s + 1) // 8, (s + 1) % 8)
                            if s < 4 and not (last and u == BODY_U - 1):
                                exp(i, 2 * u + 3, s)
                            elif s >= 4 and more:
                                exp(i, 2 * u + 4, s - 4)
                            if s == 0 and u > 0:
                                copy_o(i, u - 1)
                            if s == 3:
                                for it, x in KQ_PLAN[u]:
                                    if not (last and it >= BODY_IT):
                                        split_kq(i, it, x)
                            if s == 7:
                                for it, x in V_PLAN[u]:
                                    if not (last and it >= BODY_IT):
                                        split_v(i, it, x)
                    copy_o(i, BODY_U - 1)

                with act.Fori(0, LAST) as i:
                    body(i, False)
                body(LAST, True)

            @block.vector
            def _(dve):
                def piece_maximum(i, n, p):
                    _, qt, _ = head(i, n)
                    lo, hi = score_cols(qt, p)
                    hi = min(hi, NKV_USED)
                    dve.wait_ge(scores_ready, i * 64 + 4 * n + p + 1)
                    nc.vector.tensor_reduce(piece_max[:, n % 2, p:p + 1], ps_s[:, p, lo - p * PC:hi - p * PC],
                                            AX.X, ALU.max).then_inc(max_ready, 1)

                def negative_maximum(i, n):
                    dve.wait_ge(max_ready, i * 64 + 4 * n + 4)
                    if not (isinstance(i, int) and 4 * n - 12 <= 0):
                        dve.wait_ge(exp_done, i * 64 + 4 * n - 12)
                    nc.vector.tensor_reduce(neg_max[:, n % PB:n % PB + 1], piece_max[:, n % 2, :], AX.X, ALU.max,
                                            negate=True).then_inc(neg_max_ready, 1)

                def inverse_sum(i, n):
                    dve.wait_ge(exp_done, i * 64 + 4 * n + 4)
                    nc.vector.tensor_reduce(row_sum[:, n % 2:n % 2 + 1], piece_sum[:, n % 2, :], AX.X, ALU.add).then_inc(sum_ready, 1)
                    dve.wait_ge(sum_ready, i * 16 + n + 1 + 2)
                    if not (isinstance(i, int) and 4 * n - 12 <= 0):
                        dve.wait_ge(norm_done, N_CREDIT + i * 64 + 4 * n - 12)
                    nc.vector.reciprocal(inv_sum[:, n % PB:n % PB + 1], row_sum[:, n % 2:n % 2 + 1]).then_inc(inv_ready, 1)

                def low(i, u, c):
                    k = 8 * u + c
                    qt = (u // 2) % QT
                    bs = [x % 2 for x in blocks_of(qt, c)]
                    cols = slice(bs[0] * 256, bs[-1] * 256 + 256)
                    dve.wait_ge(hi_done, i * 64 + k + 1)
                    dve.wait_ge(pv_done, PV_CREDIT + i * 64 + k + 1 - RING)
                    nc.vector.tensor_tensor(pt_lo[:, k % RING, cols], ps_t[:, k % 2, cols],
                                            pt_hi[:, k % RING, cols].bitcast(F32), ALU.subtract).then_inc(lo_done, 1)

                def add_y(i, u):
                    tile = bass.ds(2 * (i // 2) + (u // 2) % QT, 1)
                    dve.wait_ge(y_ready, YR_CREDIT + i * (BODY_U // 2) + u // 2 + 1)
                    x_t = x_sb[:, tile, :].rearrange("p a n -> p (a n)")
                    nc.vector.tensor_tensor(x_t, ps_o[:, u % 2, 256:512], x_t, ALU.add).then_inc(y_added, 1)

                nc.vector.memset(prob[:, :, NKV_USED:NK], 0.0).then_inc(prob_zeroed, 1)
                dve.sem_inc(sum_ready, 2)
                dve.sem_inc(y_added, YA_CREDIT)
                for x in range(2, KQ_PIECES):
                    raw, hi, lo = kq_piece(0, x)
                    dve.wait_ge(kq_hi, x + 1)
                    nc.vector.tensor_tensor(lo, raw, hi.bitcast(F32), ALU.subtract).then_inc(kq_lo, 1)
                for n in range(4):
                    for p in range(4):
                        piece_maximum(0, n, p)
                    negative_maximum(0, n)
                    if n >= 1:
                        inverse_sum(0, n - 1)
                low(0, 0, 0)
                low(0, 0, 1)

                def body(i, last):
                    for u in range(BODY_U):
                        more = not (last and u >= BODY_U - 2)
                        for s in range(SLOTS):
                            n, sp = 2 * u + 4 + s // 4, s % 4
                            ahead = not (last and u == BODY_U - 1 and s >= 6)
                            if ahead and sp < 3:
                                low(i, u + (s + 2) // 8, (s + 2) % 8)
                            if more:
                                piece_maximum(i, n, sp)
                                if sp == 3:
                                    negative_maximum(i, n)
                            if sp == 3 and not (last and n - 1 >= 2 * BODY_U):
                                inverse_sum(i, n - 1)
                            if ahead and sp == 3:
                                low(i, u + (s + 2) // 8, (s + 2) % 8)
                            if s == 5 and u % 2 == 0 and u > 0:
                                add_y(i, u - 1)
                    add_y(i, BODY_U - 1)

                with dve.Fori(0, LAST) as i:
                    body(i, False)
                body(LAST, True)

            @block.gpsimd
            def _(pool):
                def normalise(i, n):
                    _, qt, _ = head(i, n)
                    pool.wait_ge(inv_ready, i * 16 + n + 1)
                    pool.sem_inc(norm_begun, 1)
                    for p in range(4):
                        lo, hi = score_cols(qt, p)
                        hi = min(hi, NKV_USED)
                        nc.gpsimd.tensor_scalar(prob[:, n % PB, lo:hi], prob[:, n % PB, lo:hi],
                                                inv_sum[:, n % PB:n % PB + 1], 1.0, ALU.mult, ALU.mult).then_inc(norm_done, 1)

                def split_kq(i, it, x):
                    raw, hi, lo = kq_piece(it % BODY_IT, x)
                    pool.wait_ge(kq_hi, (i * BODY_IT + it) * KQ_PIECES + x + 1)
                    if it >= BODY_IT:
                        pool.wait_ge(scores_ready, i * 64 + 32 * (it - 1))
                    nc.gpsimd.tensor_tensor(lo, raw, hi.bitcast(F32), ALU.subtract).then_inc(kq_lo, 1)

                def split_v(i, it, x):
                    raw, hi, lo = v_piece(it % BODY_IT, x)
                    pool.wait_ge(vv_hi, (i * BODY_IT + it) * V_PIECES + x + 1)
                    if it >= 1:
                        pool.wait_ge(pv_done, PV_CREDIT + i * 64 + 32 * (it - 1))
                    nc.gpsimd.tensor_tensor(lo, raw, hi.bitcast(F32), ALU.subtract).then_inc(vv_lo, 1)

                pool.sem_inc(norm_done, N_CREDIT)
                for x in range(2):
                    split_kq(0, 0, x)
                for x in range(V_PIECES):
                    split_v(0, 0, x)
                for n in range(2):
                    normalise(0, n)
                for x in range(4):
                    split_kq(0, 1, x)

                def body(i, last):
                    for u in range(BODY_U):
                        if not (last and u == BODY_U - 1):
                            normalise(i, 2 * u + 2)
                        for it, x in KQ_PLAN[u]:
                            if not (last and it >= BODY_IT):
                                split_kq(i, it, x)
                        if not (last and u == BODY_U - 1):
                            normalise(i, 2 * u + 3)
                        for it, x in V_PLAN[u]:
                            if not (last and it >= BODY_IT):
                                split_v(i, it, x)

                with pool.Fori(0, LAST) as i:
                    body(i, False)
                body(LAST, True)

            @block.tensor
            def _(pe):
                def scores(i, n, p):
                    gi, qt, h = head(i, n)
                    lo, hi = score_cols(qt, p)
                    if n % 8 == 0 and p == 0:
                        pe.wait_ge(kq_hi, (i * BODY_IT + n // 8 + 1) * KQ_PIECES)
                        pe.wait_ge(kq_lo, (i * BODY_IT + n // 8 + 1) * KQ_PIECES)
                    if not (isinstance(i, int) and 4 * n + p - 3 <= 0):
                        pe.wait_ge(exp_done, i * 64 + 4 * n + p - 3)
                    out = ps_s[:, p, lo - p * PC:hi - p * PC]
                    qs = slice(qt * P, qt * P + P)
                    nc.tensor.matmul(out, q_hi[:, gi, h, qs], k_hi[:, gi, lo:hi], start=True, stop=False)
                    nc.tensor.matmul(out, q_hi[:, gi, h, qs], k_lo[:, gi, lo:hi], start=False, stop=False)
                    if p == 0:
                        nc.tensor.matmul(ps_s[:, 0, lo:lo + P], ident_bf[:, :], mask_bf[:, :], start=False, stop=False,
                                         skip_group_check=True)
                    nc.tensor.matmul(out, q_lo[:, gi, h, qs], k_hi[:, gi, lo:hi], start=False, stop=True).then_inc(scores_ready, 1)

                def transposes(i, u, c):
                    k = 8 * u + c
                    qt = (u // 2) % QT
                    if c % 2 == 0:
                        pe.wait_ge(norm_done, N_CREDIT + i * 64 + 4 * (2 * u + 1) + c // 2 + 1)
                    if not (isinstance(i, int) and k - 1 <= 0):
                        pe.wait_ge(lo_done, i * 64 + k - 1)
                    for blk in blocks_of(qt, c):
                        for j in range(2):
                            at = (blk % 2) * 256 + j * P
                            last = nc.tensor.transpose(ps_t[:, k % 2, at:at + P],
                                                       prob[:, (2 * u + j) % PB, blk * P:blk * P + P], ident[:, :])
                    last.then_inc(t_ready, 1)

                def products(i, u, c):
                    k = 8 * u + c
                    gi, qt = (u // 4) % BODY_IT, (u // 2) % QT
                    if u % 4 == 0 and c == 0:
                        pe.wait_ge(vv_hi, (i * BODY_IT + u // 4 + 1) * V_PIECES)
                        pe.wait_ge(vv_lo, (i * BODY_IT + u // 4 + 1) * V_PIECES)
                    if c == 0:
                        pe.wait_ge(o_copied, O_CREDIT + i * BODY_U + u - 1)
                        if u % 2 == 1:
                            pe.wait_ge(y_added, YA_CREDIT + i * (BODY_U // 2) + u // 2)
                    pe.wait_ge(lo_done, i * 64 + k + 1)
                    out = ps_o[:, u % 2, 0:256]
                    for blk in blocks_of(qt, c):
                        vs = slice(blk * HD, blk * HD + HD)
                        cols = slice((blk % 2) * 256, (blk % 2) * 256 + 256)
                        nc.tensor.matmul(out, v_hi[:, gi, vs], pt_hi[:, k % RING, cols], start=blk == (0 if qt else 1), stop=False)
                        nc.tensor.matmul(out, v_hi[:, gi, vs], pt_lo[:, k % RING, cols], start=False, stop=False)
                        last = nc.tensor.matmul(out, v_lo[:, gi, vs], pt_hi[:, k % RING, cols], start=False, stop=blk == KB - 1)
                    last.then_inc(pv_done, 1)

                def project(i, u):
                    gi = (u // 4) % BODY_IT
                    pe.wait_ge(o_copied, O_CREDIT + i * BODY_U + u + 1)
                    for h in range(GRP):
                        hh = (i % 2) * (BODY_IT * GRP) + gi * GRP + h
                        last = nc.tensor.matmul(ps_o[:, u % 2, 256:512], o_t[:, (u // 2) % 2, h, :],
                                                wo[:, bass.ds(hh, 1), :].rearrange("p a n -> p (a n)"),
                                                start=h == 0, stop=h == GRP - 1)
                    last.then_inc(y_ready, 1)

                pe.sem_inc(t_ready, T_CREDIT)
                pe.sem_inc(pv_done, PV_CREDIT)
                pe.sem_inc(o_copied, O_CREDIT)
                pe.sem_inc(y_ready, YR_CREDIT)
                for n in range(4):
                    for p in range(4):
                        scores(0, n, p)
                transposes(0, 0, 0)
                transposes(0, 0, 1)
                pe.wait_ge(wo_loaded, 16)

                def body(i, last):
                    for u in range(BODY_U):
                        for s in range(SLOTS):
                            n, sp = 2 * u + 4 + s // 4, s % 4
                            ahead = not (last and u == BODY_U - 1 and s >= 6)
                            more = not (last and u >= BODY_U - 2)
                            if s == 7 and more:
                                scores(i, n, sp)
                            if ahead:
                                transposes(i, u + (s + 2) // 8, (s + 2) % 8)
                            if s == 3 and more:
                                scores(i, n, sp)
                            products(i, u, s)
                            if sp < 3 and more:
                                scores(i, n, sp)
                            if s == 0 and u % 2 == 0 and u > 0:
                                project(i, u - 1)
                    project(i, BODY_U - 1)

                with pe.Fori(0, LAST) as i:
                    body(i, False)
                body(LAST, True)
GT = 4
NG = NT // GT


def moe_two_of_eight(nc, x_sb, gate_dram, bias_dram, w1_dram, w3_dram, w2_dram, sw1_dram, sw3_dram, sw2_dram,
                     mean_var, rstd, half, ident, ident_bf, iota, sorted_dram):
    with ExitStack() as ctx:
        sb, psum, sem = scope(ctx, nc)
        N = GT * P
        norm = norm_memory(sb, sem, "norm2")
        w_raw = sb("w4_raw", [P, 3, E0, D])
        w_bf = sb("w4_bf", [P, 3, E0, D], BF16)
        sw = sb("w4_shared", [P, 3, D])
        gate = sb("gate4", [P, DC, E0])
        bias = sb("bias4", [P, E0])
        xn = sb("xn4", [P, GT, D])
        xr = sb("xr4", [P, 4, D])
        xt = sb("xt4", [P, DC, TOK])
        score = sb("score4", [P, NT, E0])
        biased = sb("biased4", [P, NT, E0])
        best = sb("best4", [P, NT, 8])
        best_at = sb("best_at4", [P, NT, 8], U32)
        chosen_at = sb("chosen_at4", [P, NT, 2])
        first = sb("first4", [P, NT, E0])
        second = sb("second4", [P, NT, E0])
        chosen = sb("chosen4", [P, NT, E0])
        weight = sb("weight4", [P, GT, E0])
        xb = sb("xb4", [P, 2, GT, D], BF16)
        xbt = sb("xbt4", [P, 2, DC, N], BF16)
        h1_bf = sb("h1_4_bf", [P, 2, N], BF16)
        h3_bf = sb("h3_4_bf", [P, 2, N], BF16)
        exp_bf = sb("exp4_bf", [P, 2, N], BF16)
        den_bf = sb("den4_bf", [P, 2, N], BF16)
        inv_bf = sb("inv4_bf", [P, 2, N], BF16)
        silu_bf = sb("silu4_bf", [P, 2, N], BF16)
        exp_f = sb("exp4_f", [P, N])
        den_f = sb("den4_f", [P, N])
        inv_f = sb("inv4_f", [P, N])
        silu_f = sb("silu4_f", [P, N])
        y_bf = sb("y4_bf", [P, 2, 2 * D], BF16)
        score_exp = sb("score_exp4", [P, NT, E0])
        score_den = sb("score_den4", [P, NT, E0])
        zeros = sb("zeros4", [P, D])
        act_bf = sb("act4_bf", [P, 2, N], BF16)
        act_f = sb("act4_f", [P, N])
        ps_acc = psum("ps_acc4", [P, 2, 512])
        ps_h = psum("ps_h4", [P, 4, 512])
        ps_b = psum("ps_b4", [P, 1024], BF16)
        ps_y = psum("ps_y4", [P, 512])

        w_loaded = [sem(f"w4_loaded{e}") for e in range(E0)]
        sw_loaded, gate_loaded = sem("sw4_loaded"), sem("gate4_loaded")
        w_cast = sem("w4_cast")
        xr_ready, xn_ready, xt_ready, xt_copied = sem("xr4s"), sem("xn4s"), sem("xt4s"), sem("xt4_copied")
        logits, scored, added, maxed, indexed, idx_f = sem("logits4"), sem("scored4"), sem("biased4s"), sem("best4s"), sem("best4_at"), sem("chosen4_at")
        is_first, is_second, chosen_s, weighted = sem("first4s"), sem("second4s"), sem("chosen4s"), sem("weight4s")
        scale_begun = sem("scale4_begun")
        xb_ready, xbt_ready, xbt_copied = sem("xb4s"), sem("xbt4s"), sem("xbt4_copied")
        h1_ready, h3_ready, h1_copied, h3_copied = sem("h1_4"), sem("h3_4"), sem("h1_4_copied"), sem("h3_4_copied")
        exp_ready, den_ready, inv_ready, silu_ready, act_ready = sem("exp4s"), sem("den4s"), sem("inv4s"), sem("silu4s"), sem("act4s")
        score_exps, score_dens = sem("score_exp4s"), sem("score_den4s")
        y_done, y_copied, summed, x_added = sem("y4"), sem("y4_copied"), sem("summed4"), sem("x4_added")
        shared_done = sem("shared4")
        zeros_ready, zeroed = sem("zeros4s"), sem("zeroed4")
        STEPS = E0 + 1
        PAIRS = NT // 2

        with nc.Block() as block:
            @block.sync
            def _(sp):
                sp.dma_start(gate[:, :, :], gate_dram.rearrange("(c p) e -> p c e", p=P)).then_inc(gate_loaded, 16)
                sp.dma_start(bias[:, :], bias_dram.rearrange("(a e) -> a e", a=1).to_broadcast([P, E0])).then_inc(gate_loaded, 16)
                for n, w in enumerate((sw1_dram, sw3_dram)):
                    sp.dma_start(sw[:, n, :].rearrange("p (c h) -> p c h", c=DC), w.rearrange("(c p) h -> p c h", p=P)).then_inc(sw_loaded, 16)
                sp.dma_start(sw[:, 2, :], sw2_dram).then_inc(sw_loaded, 16)
                for e in range(E0):
                    for n, w in enumerate((w1_dram, w3_dram)):
                        sp.dma_start(w_raw[:, n, e, :].rearrange("p (c h) -> p c h", c=DC),
                                     w[e].rearrange("(c p) h -> p c h", p=P)).then_inc(w_loaded[e], 16)
                    sp.dma_start(w_raw[:, 2, e, :], w2_dram[e]).then_inc(w_loaded[e], 16)
                sp.wait_ge(zeros_ready, 1)
                sp.dma_start(sorted_dram.rearrange("(s p) d -> p s d", p=P), zeros[:, :].unsqueeze(1).to_broadcast([P, ESLOTS, D])).then_inc(zeroed, 16)
                sp.wait_ge(zeroed, 16)

            @block.gpsimd
            def _(pool):
                for part in range(NORM_PARTS):
                    norm_rstd(nc, pool, mean_var, rstd, half, norm, part)

                def cast(e):
                    pool.wait_ge(w_loaded[e], 16 * 3)
                    for n in range(3):
                        nc.gpsimd.tensor_copy(w_bf[:, n, e, :], w_raw[:, n, e, :]).then_inc(w_cast, 1)

                def scale(i, e):
                    if e == 0:
                        pool.wait_ge(xn_ready, (i + 1) * GT)
                        pool.wait_ge(weighted, i + 1)
                    if positive(i * E0 + e - 1):
                        pool.wait_ge(xbt_ready, i * E0 + e - 1)
                    pool.sem_inc(scale_begun, 1)
                    for t in range(GT):
                        nc.gpsimd.tensor_scalar(xb[:, e % 2, t, :], xn[:, t, :], weight[:, t, e:e + 1], 1.0, ALU.mult, ALU.mult).then_inc(xb_ready, 1)

                nc.gpsimd.memset(zeros[:, :], 0.0).then_inc(zeros_ready, 1)
                for e in range(E0):
                    cast(e)
                    scale(0, e)
                with pool.Fori(1, NG) as i:
                    for e in range(E0):
                        scale(i, e)

            @block.scalar
            def _(act):
                for g in range(PAIRS):
                    act.wait_ge(xt_ready, g + 1)
                    nc.scalar.activation(xt[:, :, g * 2 * P:(g + 1) * 2 * P].rearrange("p c (t n) -> p c t n", t=2),
                                         ps_h[:, g % 4, :].rearrange("p (t c n) -> p c t n", t=2, c=DC), ACT.Copy).then_inc(xt_copied, 1)
                act.wait_ge(logits, 1)
                nc.scalar.activation(score_exp[:, :, :], ps_y[:, 0:NT * E0].rearrange("p (t e) -> p t e", t=NT), ACT.Exp, scale=-1.0).then_inc(score_exps, 1)

                def group(i, last):
                    def inputs(e, i=i):
                        act.wait_ge(xbt_ready, i * E0 + e + 1)
                        if positive(i * E0 + e - 1):
                            act.wait_ge(h3_ready, (i * STEPS + e - 1 + 1) if e >= 2 else i * STEPS - (1 - e))
                        nc.scalar.activation(xbt[:, e % 2, :, :], ps_b[:, :].rearrange("p (c n) -> p c n", c=DC), ACT.Copy).then_inc(xbt_copied, 1)

                    def outputs(s, h):
                        k = (i * E0 + s - 1) * 2 + h
                        act.wait_ge(y_done, k + 1)
                        if positive(k - 1):
                            act.wait_ge(summed, k - 1)
                        nc.scalar.activation(y_bf[:, h, :], ps_y[:, :], ACT.Copy).then_inc(y_copied, 1)

                    def hidden(s, i=i):
                        j = s % 2
                        act.wait_ge(h1_ready, i * STEPS + s + 1)
                        if s == 0:
                            if positive(i):
                                act.wait_ge(den_ready, (i - 1) * STEPS + 1)
                            nc.scalar.activation(exp_f[:, :], ps_h[:, 0, :], ACT.Exp, scale=-1.0).then_inc(exp_ready, 1)
                            return
                        if positive(i * STEPS + s - 2):
                            act.wait_ge(act_ready, i * STEPS + s - 1)
                        nc.scalar.activation(h1_bf[:, j, :], ps_h[:, 2 * j, :], ACT.Copy).then_inc(h1_copied, 1)
                        act.wait_ge(h1_copied, i * E0 + s)
                        nc.scalar.activation(exp_bf[:, j, :], h1_bf[:, j, :], ACT.Exp, scale=-1.0).then_inc(exp_ready, 1)
                        act.wait_ge(h3_ready, i * STEPS + s + 1)
                        nc.scalar.activation(h3_bf[:, j, :], ps_h[:, 2 * j + 1, :], ACT.Copy).then_inc(h3_copied, 1)

                    if not positive(i):
                        hidden(0)
                        inputs(0)
                    for s in range(STEPS):
                        if s + 1 < STEPS:
                            hidden(s + 1)
                        elif not last:
                            hidden(0, i + 1)
                        if s + 1 < E0:
                            inputs(s + 1)
                        elif s + 1 == STEPS and not last:
                            inputs(0, i + 1)
                        if s > 0:
                            outputs(s, 0)
                            outputs(s, 1)

                group(0, False)
                with act.Fori(1, NG - 1) as i:
                    group(i, False)
                group(NG - 1, True)

            @block.vector
            def _(dve):
                def normalise(dst, tile):
                    return nc.vector.tensor_scalar(dst, x_sb[:, tile, :].rearrange("p a n -> p (a n)"),
                                                   mean_var[:, tile, 0], rstd[:, tile], ALU.subtract, ALU.mult)

                def choose():
                    dve.wait_ge(score_exps, 1)
                    nc.vector.tensor_scalar(score_den[:, :, :], score_exp[:, :, :], 1.0, None, ALU.add).then_inc(score_dens, 1)
                    dve.wait_ge(score_dens, 1)
                    nc.vector.reciprocal(score[:, :, :], score_den[:, :, :]).then_inc(scored, 1)
                    dve.wait_ge(scored, 1)
                    nc.vector.tensor_tensor(biased[:, :, :], score[:, :, :], bias[:, :].unsqueeze(1).to_broadcast([P, NT, E0]), ALU.add).then_inc(added, 1)
                    dve.wait_ge(added, 1)
                    for t in range(NT):
                        nc.vector.max(best[:, t, :], biased[:, t, :]).then_inc(maxed, 1)
                    dve.wait_ge(maxed, NT)
                    for t in range(NT):
                        nc.vector.max_index(best_at[:, t, :], best[:, t, :], biased[:, t, :]).then_inc(indexed, 1)
                    dve.wait_ge(indexed, NT)
                    nc.vector.tensor_copy(chosen_at[:, :, :], best_at[:, :, 0:2]).then_inc(idx_f, 1)
                    dve.wait_ge(idx_f, 1)
                    places = iota[:, 0:E0].unsqueeze(1).to_broadcast([P, NT, E0])
                    for n, (out, s) in enumerate(((first, is_first), (second, is_second))):
                        nc.vector.tensor_tensor(out[:, :, :], places, chosen_at[:, :, n:n + 1].to_broadcast([P, NT, E0]), ALU.is_equal).then_inc(s, 1)
                    dve.wait_ge(is_first, 1)
                    dve.wait_ge(is_second, 1)
                    nc.vector.tensor_tensor(chosen[:, :, :], first[:, :, :], second[:, :, :], ALU.add).then_inc(chosen_s, 1)
                    dve.wait_ge(chosen_s, 1)

                def add_x(i):
                    dve.wait_ge(summed, (i + 1) * E0 * 2)
                    for h in range(2):
                        x_t = x_sb[:, bass.ds(i * GT + 2 * h, 2), :].rearrange("p a n -> p (a n)")
                        nc.vector.tensor_tensor(x_t, ps_acc[:, h, :], x_t, ALU.add).then_inc(x_added, 1)

                def prepare(i):
                    if positive(i):
                        dve.wait_ge(xb_ready, i * E0 * GT)
                    for t in range(GT):
                        normalise(xn[:, t, :], bass.ds(i * GT + t, 1)).then_inc(xn_ready, 1)
                    tiles = bass.ds(i * GT, GT)
                    nc.vector.tensor_tensor(weight[:, :, :], chosen[:, tiles, :], score[:, tiles, :], ALU.mult).then_inc(weighted, 1)

                def places(s):
                    j = s % 2
                    if s == 0:
                        return exp_f[:, :], den_f[:, :], inv_f[:, :], silu_f[:, :], act_f[:, :], ps_h[:, 0, :], ps_h[:, 1, :]
                    return exp_bf[:, j, :], den_bf[:, j, :], inv_bf[:, j, :], silu_bf[:, j, :], act_bf[:, j, :], h1_bf[:, j, :], h3_bf[:, j, :]

                def denominator(i, s):
                    exp, den = places(s)[:2]
                    dve.wait_ge(exp_ready, i * STEPS + s + 1)
                    nc.vector.tensor_scalar(den, exp, 1.0, None, ALU.add).then_inc(den_ready, 1)

                def group(i, last):
                    if not positive(i):
                        denominator(i, 0)
                    for s in range(STEPS):
                        _, den, inv, silu, act, h1, h3 = places(s)
                        dve.wait_ge(den_ready, i * STEPS + s + 1)
                        with nc.allow_low_precision(reason="the reference divides in bfloat16"):
                            nc.vector.reciprocal(inv, den).then_inc(inv_ready, 1)
                        dve.wait_ge(inv_ready, i * STEPS + s + 1)
                        nc.vector.tensor_tensor(silu, h1, inv, ALU.mult).then_inc(silu_ready, 1)
                        if s + 1 < STEPS:
                            denominator(i, s + 1)
                        elif not last:
                            denominator(i + 1, 0)
                        if s == 0:
                            dve.wait_ge(h3_ready, i * STEPS + 1)
                        else:
                            dve.wait_ge(h3_copied, i * E0 + s)
                        dve.wait_ge(silu_ready, i * STEPS + s + 1)
                        if s == 0 and positive(i):
                            dve.wait_ge(shared_done, i)
                        if s > 0 and positive((i * E0 + s - 1) * 2 - 2):
                            dve.wait_ge(y_done, (i * E0 + s - 2) * 2)
                        nc.vector.tensor_tensor(act, h3, silu, ALU.mult).then_inc(act_ready, 1)
                        if s == 0 and positive(i):
                            add_x(i - 1)
                        if s == STEPS - 2 and not last:
                            prepare(i + 1)

                norm_mean_var(nc, dve, x_sb, mean_var, norm, 0)
                for part in range(NORM_PARTS):
                    if part + 1 < NORM_PARTS:
                        norm_mean_var(nc, dve, x_sb, mean_var, norm, part + 1)
                    dve.wait_ge(norm[-1], part + 1)
                    for t in range(part * NORM_TILES, (part + 1) * NORM_TILES):
                        if t >= 4:
                            dve.wait_ge(xt_ready, t // 2 - 1)
                        normalise(xr[:, t % 4, :], slice(t, t + 1)).then_inc(xr_ready, 1)
                dve.wait_ge(gate_loaded, 32)
                choose()
                prepare(0)
                group(0, False)
                with dve.Fori(1, NG - 1) as i:
                    group(i, False)
                group(NG - 1, True)
                add_x(NG - 1)

            @block.tensor
            def _(pe):
                def turn(g):
                    pe.wait_ge(xr_ready, 2 * g + 2)
                    if g >= 4:
                        pe.wait_ge(xt_copied, g - 3)
                    for t in range(2):
                        for c in range(DC):
                            last = nc.tensor.transpose(ps_h[:, g % 4, (t * DC + c) * P:(t * DC + c + 1) * P], xr[:, (2 * g + t) % 4, c * P:c * P + P], ident[:, :])
                    last.then_inc(xt_ready, 1)

                def route():
                    turn(0)
                    for g in range(PAIRS):
                        if g + 1 < PAIRS:
                            turn(g + 1)
                        pe.wait_ge(xt_copied, g + 1)
                        for t in range(2 * g, 2 * g + 2):
                            for c in range(DC):
                                last = nc.tensor.matmul(ps_y[:, t * E0:(t + 1) * E0], xt[:, c, t * P:t * P + P], gate[:, c, :],
                                                        start=c == 0, stop=c == DC - 1)
                    last.then_inc(logits, 1)

                def group(i, last):
                    def inputs(e, i=i):
                        pe.wait_ge(xb_ready, (i * E0 + e + 1) * GT)
                        if positive(i * E0 + e):
                            pe.wait_ge(xbt_copied, i * E0 + e)
                        for c in range(DC):
                            for t in range(GT):
                                last = nc.tensor.transpose(ps_b[:, c * N + t * P:c * N + t * P + P], xb[:, e % 2, t, c * P:c * P + P], ident_bf[:, :])
                        last.then_inc(xbt_ready, 1)

                    def hidden(s, i=i):
                        j = s % 2
                        if s > 0:
                            pe.wait_ge(xbt_copied, i * E0 + s)
                        if s == 2:
                            pe.wait_ge(act_ready, i * STEPS + 1)
                        elif positive(i * E0 + s - 2):
                            pe.wait_ge(h3_copied, i * E0 + (s - 2 if s > 2 else s - 1 if s else 0))
                        for n, done in ((0, h1_ready), (1, h3_ready)):
                            for c in range(DC):
                                if s == 0:
                                    a, b = sw[:, n, c * H0:c * H0 + H0], xt[:, c, bass.ds(i * N, N)]
                                else:
                                    a, b = w_bf[:, n, s - 1, c * H0:c * H0 + H0], xbt[:, (s - 1) % 2, c, :]
                                last = nc.tensor.matmul(ps_h[:, 2 * j + n, :], a, b, start=c == 0, stop=c == DC - 1)
                            last.then_inc(done, 1)

                    def add(t, a, b, first=False, last=False):
                        return nc.tensor.matmul(ps_acc[:, t // 2, (t % 2) * D:(t % 2) * D + D], a, b, start=first and t % 2 == 0,
                                                stop=last and t % 2 == 1, skip_group_check=True)

                    def shared_outputs():
                        pe.wait_ge(act_ready, i * STEPS + 1)
                        if positive(i):
                            pe.wait_ge(x_added, i * 2)
                        for t in range(GT):
                            last = add(t, act_f[:, t * P:t * P + P], sw[:, 2, :], first=True)
                        last.then_inc(shared_done, 1)

                    def outputs(s, h):
                        k = (i * E0 + s - 1) * 2 + h
                        if h == 0:
                            pe.wait_ge(act_ready, i * STEPS + s + 1)
                        if s == 1 and h == 0 and not positive(i):
                            pe.wait_ge(score_exps, 1)
                        if positive(k):
                            pe.wait_ge(y_copied, k)
                        for t in range(2):
                            last = nc.tensor.matmul(ps_y[:, t * D:t * D + D], act_bf[:, s % 2, (2 * h + t) * P:(2 * h + t + 1) * P], w_bf[:, 2, s - 1, :],
                                                    start=True, stop=True)
                        last.then_inc(y_done, 1)

                    def sums(s, h, i=i):
                        pe.wait_ge(y_copied, (i * E0 + s - 1) * 2 + h + 1)
                        for t in range(2):
                            last = add(2 * h + t, ident_bf[:, :], y_bf[:, h, t * D:t * D + D], last=s == STEPS - 1)
                        last.then_inc(summed, 1)

                    if not positive(i):
                        hidden(0)
                        inputs(0)
                    for s in range(STEPS):
                        if s + 1 < STEPS:
                            if not positive(i):
                                pe.wait_ge(w_cast, 3 * (s + 1))
                            hidden(s + 1)
                        elif not last:
                            hidden(0, i + 1)
                        if s > 1:
                            sums(s - 1, 1)
                        elif s == 1:
                            shared_outputs()
                        elif positive(i):
                            sums(STEPS - 1, 1, i - 1)
                        if s + 1 < E0:
                            inputs(s + 1)
                        elif s + 1 == STEPS and not last:
                            inputs(0, i + 1)
                        if s > 0:
                            outputs(s, 0)
                            outputs(s, 1)
                            sums(s, 0)
                    if last:
                        sums(STEPS - 1, 1)

                pe.wait_ge(gate_loaded, 32)
                route()
                pe.wait_ge(sw_loaded, 48)
                group(0, False)
                with pe.Fori(1, NG - 1) as i:
                    group(i, False)
                group(NG - 1, True)


def memory_attention(nc, x_sb, ctx_t_dram, ctx_dram, mask_dram, mean_var, rstd, half, ident):
    UB = 2 * QT
    NB = NT // UB
    LAST = NB - 1
    KP = CT * P
    SL = 4
    RINGC = 4
    PIECES = [(0, 4), (4, 8), (8, 12), (12, CT)]
    with ExitStack() as ctx:
        sb, psum, sem = scope(ctx, nc)
        raw_t = sb("raw_t5", [P, CT, DC * P])
        raw_r = sb("raw_r5", [P, CT, D])
        mask = sb("mask5", [1, 2, T], U8)
        pen = sb("pen5", [P, 2, KP], BF16)
        row0 = sb("row0_5", [P, P], BF16)
        t_hi = sb("t_hi5", [P, 2, CT, DC, P], F32R)
        t_lo = sb("t_lo5", [P, 2, CT, DC, P], F32R)
        r_hi = sb("r_hi5", [P, 2, CT, D], F32R)
        r_lo = sb("r_lo5", [P, 2, CT, D], F32R)
        rstd_scaled = sb("rstd5", [P, NT])
        xn = sb("xn5", [P, 2, D])
        xt_hi = sb("xt5_hi", [P, 2, DC, P], F32R)
        xt_lo = sb("xt5_lo", [P, 2, DC, P], F32R)
        prob = sb("prob5", [P, 2, KP])
        pt_hi = sb("pt5_hi", [P, RINGC, 512], F32R)
        pt_lo = sb("pt5_lo", [P, RINGC, 512], F32R)
        piece_max = sb("piece_max5", [P, 2, SL])
        neg_max = sb("neg_max5", [P, 4])
        piece_sum = sb("piece_sum5", [P, 2, SL])
        row_sum = sb("row_sum5", [P, 2])
        inv_row = sb("inv_row5", [P, 2])
        inv_sum = sb("inv_sum5", [P, 2])
        ps_s = psum("ps_s5", [P, SL, 512])
        ps_t = psum("ps_t5", [P, 2, 512])
        ps_o = psum("ps_o5", [P, 2, 512])

        norm = norm_memory(sb, sem, "norm3")
        t_loaded, r_loaded, m_loaded = [sem(f"t5_loaded{x}") for x in range(4)], [sem(f"r5_loaded{x}") for x in range(4)], [sem(f"m5_loaded{j}") for j in range(2)]
        th_done, tl_done, rh_done, rl_done = sem("t5_hi"), sem("t5_lo"), sem("r5_hi"), sem("r5_lo")
        mask_begun = sem("mask5_begun")
        zeroed, row0_ready, pen_ready, scaled = sem("zeroed5"), sem("row0_5s"), sem("pen5s"), sem("rstd5s")
        xn_ready, xt_ready, xt_hi_done, xt_lo_done = sem("xn5s"), sem("xt5s"), sem("xt5_his"), sem("xt5_los")
        scores_ready, max_ready, neg_max_ready, exp_done = sem("scores5"), sem("max5"), sem("neg_max5s"), sem("exp5")
        sum_ready, recip_ready, inv_ready = sem("sum5"), sem("recip5"), sem("inv5")
        pt_ready, hi_done, lo_done, pv_done, x_added = sem("pt5"), sem("pt5_his"), sem("pt5_los"), sem("pv5"), sem("x5_added")

        def exists(n, last):
            return not (last and n >= UB)

        def cols(p):
            return p * 512, min((p + 1) * 512, T)

        def blocks(c):
            return range(4 * c, min(4 * c + 4, CT))

        with nc.Block() as block:
            @block.sync
            def _(sp):
                def load_mask(b, j):
                    sp.dma_start(mask[:, j, :], mask_dram[bass.ds(b, 1), :]).then_inc(m_loaded[j], 16)

                def load_t(b, x):
                    lo, hi = PIECES[x]
                    sp.dma_start(raw_t[:, lo:hi, :], ctx_t_dram[bass.ds(b * CT + lo, hi - lo)].rearrange("t p c n -> p t (c n)")).then_inc(t_loaded[x], 16)

                def load_r(b, x):
                    lo, hi = PIECES[x]
                    sp.dma_start(raw_r[:, lo:hi, :], ctx_dram[bass.ds(b, 1), lo * P:hi * P, :].rearrange("a (t p) d -> p (a t) d", p=P)).then_inc(r_loaded[x], 16)

                for x in range(4):
                    load_t(0, x)
                for j in range(2):
                    load_mask(j, j)
                for x in range(4):
                    load_r(0, x)
                for x in range(4):
                    sp.wait_ge(th_done, x + 1)
                    sp.wait_ge(tl_done, x + 1)
                    load_t(1, x)

                def both(i, more):
                    for j in range(2):
                        for x in range(4):
                            if more:
                                sp.wait_ge(th_done, (i * 2 + j + 1) * 4 + x + 1)
                                sp.wait_ge(tl_done, (i * 2 + j + 1) * 4 + x + 1)
                                load_t(i * 2 + j + 2, x)
                            if more or j == 0:
                                sp.wait_ge(rh_done, (i * 2 + j) * 4 + x + 1)
                                sp.wait_ge(rl_done, (i * 2 + j) * 4 + x + 1)
                                load_r(i * 2 + j + 1, x)
                        if more:
                            sp.wait_ge(pen_ready, i * 2 + j + 1)
                            sp.sem_inc(mask_begun, 1)
                            load_mask(i * 2 + j + 2, j)

                with sp.Fori(0, LAST) as i:
                    both(i, True)
                both(LAST, False)

            @block.gpsimd
            def _(pool):
                norm_rstd(nc, pool, mean_var, rstd, half, norm, 0)
                nc.gpsimd.memset(row0[:, :], 0.0).then_inc(row0_ready, 1)
                pool.wait_ge(row0_ready, 1)
                nc.gpsimd.memset(row0[0:1, :], 1.0).then_inc(row0_ready, 1)
                nc.gpsimd.memset(prob[:, :, T:KP], 0.0).then_inc(zeroed, 1)
                nc.gpsimd.memset(pen[:, :, :], 0.0).then_inc(zeroed, 1)
                for part in range(1, NORM_PARTS):
                    norm_rstd(nc, pool, mean_var, rstd, half, norm, part)

                def split_t(i, b, x):
                    lo, hi = PIECES[x]
                    pool.wait_ge(th_done, (i * 2 + b) * 4 + x + 1)
                    if positive((i * 2 + b - 2) * 2 * SL + 2 * SL):
                        pool.wait_ge(scores_ready, (i * 2 + b - 1) * 2 * SL)
                    nc.gpsimd.tensor_tensor(t_lo[:, b % 2, lo:hi, :, :], raw_t[:, lo:hi, :].rearrange("p t (c n) -> p t c n", c=DC),
                                            t_hi[:, b % 2, lo:hi, :, :].bitcast(F32), ALU.subtract).then_inc(tl_done, 1)

                def split_r(i, b, x):
                    lo, hi = PIECES[x]
                    pool.wait_ge(rh_done, (i * 2 + b) * 4 + x + 1)
                    if positive((i * 2 + b - 1) * 2 * SL):
                        pool.wait_ge(pv_done, (i * 2 + b - 1) * 2 * SL)
                    nc.gpsimd.tensor_tensor(r_lo[:, b % 2, lo:hi, :], raw_r[:, lo:hi, :], r_hi[:, b % 2, lo:hi, :].bitcast(F32),
                                            ALU.subtract).then_inc(rl_done, 1)

                for x in range(4):
                    split_t(0, 1, x)
                for x in range(4):
                    split_r(0, 0, x)

                def body(i, last):
                    for u in range(UB):
                        for x in (2 * (u % 2), 2 * (u % 2) + 1):
                            if not last:
                                split_t(i, u // 2 + 2, x)
                            if not (last and u >= 2):
                                split_r(i, u // 2 + 1, x)

                body(0, False)
                with pool.Fori(1, LAST) as i:
                    body(i, False)
                body(LAST, True)

            @block.scalar
            def _(act):
                def split_t(i, b, x):
                    lo, hi = PIECES[x]
                    act.wait_ge(t_loaded[x], (i * 2 + b + 1) * 16)
                    if positive((i * 2 + b - 1) * 2 * SL):
                        act.wait_ge(scores_ready, (i * 2 + b - 1) * 2 * SL)
                    nc.scalar.activation(t_hi[:, b % 2, lo:hi, :, :], raw_t[:, lo:hi, :].rearrange("p t (c n) -> p t c n", c=DC), ACT.Copy).then_inc(th_done, 1)

                def split_r(i, b, x):
                    lo, hi = PIECES[x]
                    act.wait_ge(r_loaded[x], (i * 2 + b + 1) * 16)
                    if positive((i * 2 + b - 1) * 2 * SL):
                        act.wait_ge(pv_done, (i * 2 + b - 1) * 2 * SL)
                    nc.scalar.activation(r_hi[:, b % 2, lo:hi, :], raw_r[:, lo:hi, :], ACT.Copy).then_inc(rh_done, 1)

                def exp(i, n, p):
                    lo, hi = cols(p)
                    if p == 0:
                        act.wait_ge(neg_max_ready, i * UB + n + 1)
                        if positive(i * UB + n - 1):
                            act.wait_ge(sum_ready, i * UB + n - 1)
                    if positive((i * UB + n - 2) * SL + p + 1):
                        act.wait_ge(pt_ready, (i * UB + n - 2) * SL + p + 1)
                    nc.scalar.activation(prob[:, n % 2, lo:hi], ps_s[:, p, 0:hi - lo], ACT.Exp, bias=neg_max[:, n % 4:n % 4 + 1],
                                         accum_out=piece_sum[:, n % 2, p:p + 1]).then_inc(exp_done, 1)

                def high(i, u, c):
                    k = u * SL + c
                    w = len(blocks(c)) * P
                    act.wait_ge(pt_ready, i * UB * SL + k + 1)
                    if positive(i * UB * SL + k + 1 - RINGC):
                        act.wait_ge(pv_done, i * UB * SL + k + 1 - RINGC)
                    nc.scalar.activation(pt_hi[:, k % RINGC, 0:w], ps_t[:, k % 2, 0:w], ACT.Copy).then_inc(hi_done, 1)

                def high_x(i, v):
                    act.wait_ge(xt_ready, i * UB + v + 1)
                    if positive((i * UB + v - 1) * SL):
                        act.wait_ge(scores_ready, (i * UB + v - 1) * SL)
                    nc.scalar.activation(xt_hi[:, v % 2, :, :], ps_o[:, v % 2, D:2 * D].rearrange("p (c n) -> p c n", c=DC), ACT.Copy).then_inc(xt_hi_done, 1)

                for x in range(4):
                    split_t(0, 0, x)
                for v in range(2):
                    high_x(0, v)
                for x in range(4):
                    split_t(0, 1, x)
                for x in range(4):
                    split_r(0, 0, x)
                act.wait_ge(zeroed, 2)
                for p in range(SL):
                    exp(0, 0, p)
                high_x(0, 2)
                high(0, 0, 0)

                def body(i, last):
                    for u in range(UB):
                        for s in range(SL):
                            if exists(u + (s + 1) // SL, last):
                                high(i, u + (s + 1) // SL, (s + 1) % SL)
                            if exists(u + 1, last):
                                exp(i, u + 1, s)
                            x = 2 * (u % 2) + s // 2
                            if s % 2 == 0 and not last:
                                split_t(i, u // 2 + 2, x)
                            if s % 2 == 1 and not (last and u >= 2):
                                split_r(i, u // 2 + 1, x)
                            if s == 2 and exists(u + 3, last):
                                high_x(i, u + 3)

                body(0, False)
                with act.Fori(1, LAST) as i:
                    body(i, False)
                body(LAST, True)

            @block.vector
            def _(dve):
                def normalise(i, v):
                    tile = bass.ds(i * UB + v, 1)
                    if positive(i * UB + v - 1):
                        dve.wait_ge(xt_ready, i * UB + v - 1)
                    nc.vector.tensor_scalar(xn[:, v % 2, :], x_sb[:, tile, :].rearrange("p a n -> p (a n)"),
                                            mean_var[:, tile, 0], rstd_scaled[:, tile], ALU.subtract, ALU.mult).then_inc(xn_ready, 1)

                def low_x(i, v):
                    dve.wait_ge(xt_hi_done, i * UB + v + 1)
                    if positive((i * UB + v - 1) * SL):
                        dve.wait_ge(scores_ready, (i * UB + v - 1) * SL)
                    nc.vector.tensor_tensor(xt_lo[:, v % 2, :, :], ps_o[:, v % 2, D:2 * D].rearrange("p (c n) -> p c n", c=DC),
                                            xt_hi[:, v % 2, :, :].bitcast(F32), ALU.subtract).then_inc(xt_lo_done, 1)

                def penalty(i, b):
                    dve.wait_ge(m_loaded[b % 2], 16 * (i + b // 2 + 1))
                    if positive((i * 2 + b - 1) * 2 * SL):
                        dve.wait_ge(scores_ready, (i * 2 + b - 1) * 2 * SL)
                    nc.vector.tensor_scalar(pen[0:1, b % 2, 0:T], mask[0:1, b % 2, :], -NEG, NEG, ALU.mult, ALU.add).then_inc(pen_ready, 1)

                def piece_maximum(i, n, p):
                    lo, hi = cols(p)
                    dve.wait_ge(scores_ready, (i * UB + n) * SL + p + 1)
                    nc.vector.tensor_reduce(piece_max[:, n % 2, p:p + 1], ps_s[:, p, 0:hi - lo], AX.X, ALU.max).then_inc(max_ready, 1)

                def negative_maximum(i, n):
                    dve.wait_ge(max_ready, (i * UB + n + 1) * SL)
                    if positive((i * UB + n - 3) * SL):
                        dve.wait_ge(exp_done, (i * UB + n - 3) * SL)
                    nc.vector.tensor_reduce(neg_max[:, n % 4:n % 4 + 1], piece_max[:, n % 2, :], AX.X, ALU.max, negate=True).then_inc(neg_max_ready, 1)

                def inverse_sum(i, n):
                    dve.wait_ge(exp_done, (i * UB + n + 1) * SL)
                    nc.vector.tensor_reduce(row_sum[:, n % 2:n % 2 + 1], piece_sum[:, n % 2, :], AX.X, ALU.add).then_inc(sum_ready, 1)
                    dve.wait_ge(sum_ready, i * UB + n + 1)
                    nc.vector.reciprocal(inv_row[:, n % 2:n % 2 + 1], row_sum[:, n % 2:n % 2 + 1]).then_inc(recip_ready, 1)
                    dve.wait_ge(recip_ready, i * UB + n + 1)
                    nc.vector.scalar_tensor_tensor(inv_sum[:, n % 2:n % 2 + 1], neg_max[:, n % 4:n % 4 + 1], -NEG / 2,
                                                   inv_row[:, n % 2:n % 2 + 1], ALU.is_lt, ALU.mult).then_inc(inv_ready, 1)

                def low(i, u, c):
                    k = u * SL + c
                    w = len(blocks(c)) * P
                    dve.wait_ge(hi_done, i * UB * SL + k + 1)
                    if positive(i * UB * SL + k + 1 - RINGC):
                        dve.wait_ge(pv_done, i * UB * SL + k + 1 - RINGC)
                    nc.vector.tensor_tensor(pt_lo[:, k % RINGC, 0:w], ps_t[:, k % 2, 0:w], pt_hi[:, k % RINGC, 0:w].bitcast(F32),
                                            ALU.subtract).then_inc(lo_done, 1)

                def add_x(i, u):
                    tile = bass.ds(i * UB + u, 1)
                    dve.wait_ge(inv_ready, i * UB + u + 1)
                    dve.wait_ge(pv_done, (i * UB + u + 1) * SL)
                    x_t = x_sb[:, tile, :].rearrange("p a n -> p (a n)")
                    nc.vector.scalar_tensor_tensor(x_t, ps_o[:, u % 2, 0:D], inv_sum[:, u % 2:u % 2 + 1], x_t, ALU.mult, ALU.add).then_inc(x_added, 1)

                def scale_rstd(first, end):
                    dve.wait_ge(norm[-1], end)
                    tiles = slice(first * NORM_TILES, end * NORM_TILES)
                    nc.vector.tensor_scalar(rstd_scaled[:, tiles], rstd[:, tiles], float(D) ** -0.5, None, ALU.mult).then_inc(scaled, 1)

                norm_mean_var(nc, dve, x_sb, mean_var, norm, 0)
                scale_rstd(0, 1)
                dve.wait_ge(scaled, 1)
                normalise(0, 0)
                normalise(0, 1)
                for x, (lo, hi) in enumerate(PIECES):
                    dve.wait_ge(th_done, x + 1)
                    nc.vector.tensor_tensor(t_lo[:, 0, lo:hi, :, :], raw_t[:, lo:hi, :].rearrange("p t (c n) -> p t c n", c=DC),
                                            t_hi[:, 0, lo:hi, :, :].bitcast(F32), ALU.subtract).then_inc(tl_done, 1)
                dve.wait_ge(zeroed, 2)
                penalty(0, 0)
                penalty(0, 1)
                low_x(0, 0)
                low_x(0, 1)
                normalise(0, 2)
                for part in range(1, NORM_PARTS):
                    norm_mean_var(nc, dve, x_sb, mean_var, norm, part)
                scale_rstd(1, NORM_PARTS)
                dve.wait_ge(scaled, 2)
                for n in range(2):
                    for p in range(SL):
                        piece_maximum(0, n, p)
                    negative_maximum(0, n)
                low_x(0, 2)
                normalise(0, 3)
                low(0, 0, 0)
                low(0, 0, 1)

                def body(i, last):
                    for u in range(UB):
                        for s in range(SL):
                            if s < SL - 1 and exists(u + (s + 2) // SL, last):
                                low(i, u + (s + 2) // SL, (s + 2) % SL)
                            if exists(u + 2, last):
                                piece_maximum(i, u + 2, s)
                            if s == 0:
                                inverse_sum(i, u)
                            if s == 1:
                                if positive(i * UB + u):
                                    add_x(i, u - 1) if u else add_x(i - 1, UB - 1)
                                if exists(u + 4, last):
                                    normalise(i, u + 4)
                                if u % 2 == 0 and not last:
                                    penalty(i, u // 2 + 2)
                            if s == 2 and exists(u + 3, last):
                                low_x(i, u + 3)
                        if exists(u + 2, last):
                            negative_maximum(i, u + 2)
                        if exists(u + 1, last):
                            low(i, u + 1, 1)

                body(0, False)
                with dve.Fori(1, LAST) as i:
                    body(i, False)
                body(LAST, True)
                add_x(LAST, UB - 1)

            @block.tensor
            def _(pe):
                def transpose_x(i, v):
                    pe.wait_ge(xn_ready, i * UB + v + 1)
                    if positive(i * UB + v - 3):
                        pe.wait_ge(x_added, i * UB + v - 3)
                    if positive(i * UB + v - 1):
                        pe.wait_ge(xt_lo_done, i * UB + v - 1)
                    for c in range(DC):
                        last = nc.tensor.transpose(ps_o[:, v % 2, D + c * P:D + c * P + P], xn[:, v % 2, c * P:c * P + P], ident[:, :])
                    last.then_inc(xt_ready, 1)

                def scores(i, n, p):
                    b = (n // 2) % 2
                    t0, t1 = 4 * p, min(4 * p + 4, CT)
                    if p == 0:
                        pe.wait_ge(xt_lo_done, i * UB + n + 1)
                        if n % 2 == 0:
                            pe.wait_ge(tl_done, (i * 2 + n // 2 + 1) * 4)
                            pe.wait_ge(pen_ready, i * 2 + n // 2 + 1)
                    if positive((i * UB + n - 1) * SL + p + 1):
                        pe.wait_ge(exp_done, (i * UB + n - 1) * SL + p + 1)
                    out = ps_s[:, p, 0:(t1 - t0) * P]
                    for c in range(DC):
                        a_hi, a_lo = xt_hi[:, n % 2, c, :], xt_lo[:, n % 2, c, :]
                        k_hi, k_lo = t_hi[:, b, t0:t1, c, :], t_lo[:, b, t0:t1, c, :]
                        nc.tensor.matmul(out, a_hi, k_hi, start=c == 0, stop=False)
                        nc.tensor.matmul(out, a_hi, k_lo, start=False, stop=False)
                        if c == 0:
                            nc.tensor.matmul(out, row0[:, :], pen[:, b, t0 * P:t1 * P], start=False, stop=False)
                        last = nc.tensor.matmul(out, a_lo, k_hi, start=False, stop=c == DC - 1)
                    last.then_inc(scores_ready, 1)

                def transposes(i, u, c):
                    k = u * SL + c
                    pe.wait_ge(exp_done, (i * UB + u) * SL + c + 1)
                    if positive(i * UB * SL + k - 1):
                        pe.wait_ge(lo_done, i * UB * SL + k - 1)
                    for n, blk in enumerate(blocks(c)):
                        last = nc.tensor.transpose(ps_t[:, k % 2, n * P:n * P + P], prob[:, u % 2, blk * P:blk * P + P], ident[:, :])
                    last.then_inc(pt_ready, 1)

                def products(i, u, c):
                    k = u * SL + c
                    b = (u // 2) % 2
                    if c == 0:
                        if u % 2 == 0:
                            pe.wait_ge(rl_done, (i * 2 + u // 2 + 1) * 4)
                        if not (isinstance(i, int) and i * UB + u + 3 > NT):
                            pe.wait_ge(xt_lo_done, i * UB + u + 3)
                        if positive(i * UB + u - 1):
                            pe.wait_ge(x_added, i * UB + u - 1)
                    pe.wait_ge(lo_done, i * UB * SL + k + 1)
                    out = ps_o[:, u % 2, 0:D]
                    for n, blk in enumerate(blocks(c)):
                        p_hi, p_lo = pt_hi[:, k % RINGC, n * P:n * P + P], pt_lo[:, k % RINGC, n * P:n * P + P]
                        nc.tensor.matmul(out, p_hi, r_hi[:, b, blk, :], start=blk == 0, stop=False)
                        nc.tensor.matmul(out, p_hi, r_lo[:, b, blk, :], start=False, stop=False)
                        last = nc.tensor.matmul(out, p_lo, r_hi[:, b, blk, :], start=False, stop=blk == CT - 1)
                    last.then_inc(pv_done, 1)

                for v in range(2):
                    transpose_x(0, v)
                pe.wait_ge(row0_ready, 2)
                for p in range(SL):
                    scores(0, 0, p)
                for p in range(SL):
                    scores(0, 1, p)
                transpose_x(0, 2)
                transposes(0, 0, 0)
                transposes(0, 0, 1)

                def body(i, last):
                    for u in range(UB):
                        for s in range(SL):
                            if exists(u + (s + 2) // SL, last):
                                transposes(i, u + (s + 2) // SL, (s + 2) % SL)
                            products(i, u, s)
                            if s == 2 and exists(u + 3, last):
                                transpose_x(i, u + 3)
                            if exists(u + 2, last):
                                scores(i, u + 2, s)

                body(0, False)
                with pe.Fori(1, LAST) as i:
                    body(i, False)
                body(LAST, True)


TO_INT = 1.5 * 2.0 ** 23


def route_to_slots(nc, x_sb, router_dram, weights_dram, weights, w_loaded, sorted_dram, mean_var, rstd, half, ident, upper_bf, ones_bf, iota,
                   place, expert_of, max_prob):
    with ExitStack() as ctx:
        sb, psum, sem = scope(ctx, nc)
        norm = norm_memory(sb, sem, "norm4")
        router = sb("router6", [P, DC, E1])
        xn = sb("xn6", [P, NT, D])
        xt = sb("xt6", [P, 2, 2 * DC * P])
        score = sb("score6", [P, NT, E1])
        best = sb("best6", [P, NT, 8])
        best_at = sb("best_at6", [P, NT, 8], U32)
        best_f = sb("best_f6", [P, NT])
        onehot = sb("onehot6", [P, NT, E1])
        onehot_bf = sb("onehot6_bf", [P, NT, E1], BF16)
        upto = sb("upto6", [P, E1, E1])
        share = sb("share6", [P, E1])
        share_int = sb("share6_int", [P, E1])
        slots = sb("slots6", [P, E1])
        slots_upto = sb("slots_upto6", [P, E1, E1])
        end = sb("end6", [P, E1])
        first_slot = sb("first_slot6", [P, E1])
        first_row = sb("first_row6", [P, E1])
        row = sb("row6", [P, NT, E1])
        own_row = sb("own_row6", [P, NT, E1])
        place_f = sb("place_f6", [P, NT])
        passed = sb("passed6", [P, ESLOTS, E1])
        passed_n = sb("passed_n6", [P, ESLOTS])
        passed_min = sb("passed_min6", [P, ESLOTS])
        ps_t = psum("ps_t6", [P, 2, 512])
        ps_l = psum("ps_l6", [P, NT * E1])
        ps_n = psum("ps_n6", [P, (NT + 1) * E1])

        router_loaded, upto_ready = sem("router6_loaded"), sem("upto6s")
        xn_ready, xt_ready, xt_copied, logits, scored = sem("xn6s"), sem("xt6s"), sem("xt6_copied"), sem("logits6"), sem("scored6")
        choice_begun, maxed, indexed, idx_f = sem("choice6_begun"), sem("best6s"), sem("best6_at"), sem("best6_f")
        prob_copied, is_own, is_own_bf, counted = sem("prob6"), sem("onehot6s"), sem("onehot6_bfs"), sem("counted6")
        shared, share_rounded, slots_ready, upto_slots, ends = sem("share6s"), sem("share6_ints"), sem("slots6s"), sem("slots_upto6s"), sem("end6s")
        first_slots, first_rows, rows, own_rows, places = sem("first_slot6s"), sem("first_row6s"), sem("row6s"), sem("own_row6s"), sem("place_f6s")
        place_ready, compared, passed_s, passed_max, table_ready = sem("place6"), sem("passed6s"), sem("passed_n6s"), sem("passed_min6s"), sem("expert_of6")
        scattered = sem("scattered6")

        with nc.Block() as block:
            @block.sync
            def _(sp):
                sp.dma_start(router[:, :, :], router_dram.rearrange("(c p) e -> p c e", p=P)).then_inc(router_loaded, 16)
                for dst, src in zip(weights, weights_dram):
                    sp.dma_start(dst[:, :, :, :], src.rearrange("e (c p) n -> p e c n", p=P)).then_inc(w_loaded, 16)

            @block.vector
            def _(dve):
                by_row = iota[:, 0:E1].unsqueeze(2).to_broadcast([P, E1, E1])
                by_col = iota[:, 0:E1].unsqueeze(1).to_broadcast([P, E1, E1])
                nc.vector.tensor_tensor(upto[:, :, :], by_col, by_row, ALU.is_le).then_inc(upto_ready, 1)
                norm_mean_var(nc, dve, x_sb, mean_var, norm, 0)
                for t in range(NT):
                    if t % NORM_TILES == 0:
                        part = t // NORM_TILES
                        if part + 1 < NORM_PARTS:
                            norm_mean_var(nc, dve, x_sb, mean_var, norm, part + 1)
                        dve.wait_ge(norm[-1], part + 1)
                    nc.vector.tensor_scalar(xn[:, t, :], x_sb[:, t, :], mean_var[:, t, 0:1], rstd[:, t:t + 1], ALU.subtract, ALU.mult).then_inc(xn_ready, 1)
                dve.wait_ge(scored, 1)
                dve.sem_inc(choice_begun, 1)
                for t in range(NT):
                    nc.vector.max(best[:, t, :], score[:, t, :]).then_inc(maxed, 1)
                dve.wait_ge(maxed, NT)
                dve.sem_inc(choice_begun, 1)
                for t in range(NT):
                    nc.vector.max_index(best_at[:, t, :], best[:, t, :], score[:, t, :]).then_inc(indexed, 1)
                nc.vector.tensor_copy(max_prob[:, :], best[:, :, 0]).then_inc(prob_copied, 1)
                dve.wait_ge(indexed, NT)
                nc.vector.tensor_copy(best_f[:, :], best_at[:, :, 0]).then_inc(idx_f, 1)
                dve.wait_ge(idx_f, 1)
                nc.vector.tensor_tensor(onehot[:, :, :], iota[:, 0:E1].unsqueeze(1).to_broadcast([P, NT, E1]),
                                        best_f[:, :].unsqueeze(2).to_broadcast([P, NT, E1]), ALU.is_equal).then_inc(is_own, 1)
                dve.wait_ge(is_own, 1)
                nc.vector.tensor_copy(onehot_bf[:, :, :], onehot[:, :, :]).then_inc(is_own_bf, 1)

                dve.wait_ge(counted, 1)
                nc.vector.tensor_scalar(share[:, :], ps_n[:, NT * E1:], 1.0 / P, (P - 1) / (2 * P), ALU.mult, ALU.add).then_inc(shared, 1)
                dve.wait_ge(shared, 1)
                nc.vector.tensor_scalar(share_int[:, :], share[:, :], TO_INT, None, ALU.add).then_inc(share_rounded, 1)
                dve.wait_ge(share_rounded, 1)
                nc.vector.tensor_scalar(slots[:, :], share_int[:, :], TO_INT, None, ALU.subtract).then_inc(slots_ready, 1)
                dve.wait_ge(slots_ready, 1)
                dve.wait_ge(upto_ready, 1)
                nc.vector.tensor_tensor(slots_upto[:, :, :], upto[:, :, :], slots[:, :].unsqueeze(1).to_broadcast([P, E1, E1]), ALU.mult).then_inc(upto_slots, 1)
                dve.wait_ge(upto_slots, 1)
                nc.vector.tensor_reduce(end[:, :], slots_upto[:, :, :], AX.X, ALU.add).then_inc(ends, 1)
                dve.wait_ge(ends, 1)
                nc.vector.tensor_tensor(first_slot[:, :], end[:, :], slots[:, :], ALU.subtract).then_inc(first_slots, 1)
                dve.wait_ge(first_slots, 1)
                nc.vector.tensor_scalar(first_row[:, :], first_slot[:, :], float(P), None, ALU.mult).then_inc(first_rows, 1)
                dve.wait_ge(first_rows, 1)
                nc.vector.tensor_tensor(row[:, :, :], ps_n[:, 0:NT * E1].rearrange("p (t e) -> p t e", t=NT),
                                        first_row[:, :].unsqueeze(1).to_broadcast([P, NT, E1]), ALU.add).then_inc(rows, 1)
                dve.wait_ge(rows, 1)
                nc.vector.tensor_tensor(own_row[:, :, :], row[:, :, :], onehot[:, :, :], ALU.mult).then_inc(own_rows, 1)
                dve.wait_ge(own_rows, 1)
                nc.vector.tensor_reduce(place_f[:, :], own_row[:, :, :], AX.X, ALU.add).then_inc(places, 1)
                dve.wait_ge(places, 1)
                nc.vector.tensor_copy(place[:, :], place_f[:, :]).then_inc(place_ready, 1)
                nc.vector.tensor_tensor(passed[:, :, :], iota[:, 0:ESLOTS].unsqueeze(2).to_broadcast([P, ESLOTS, E1]),
                                        end[:, :].unsqueeze(1).to_broadcast([P, ESLOTS, E1]), ALU.is_ge).then_inc(compared, 1)
                dve.wait_ge(compared, 1)
                nc.vector.tensor_reduce(passed_n[:, :], passed[:, :, :], AX.X, ALU.add).then_inc(passed_s, 1)
                dve.wait_ge(passed_s, 1)
                nc.vector.tensor_scalar(passed_min[:, :], passed_n[:, :], float(E1 - 1), None, ALU.min).then_inc(passed_max, 1)
                dve.wait_ge(passed_max, 1)
                nc.vector.tensor_copy(expert_of[:, :], passed_min[:, :]).then_inc(table_ready, 1)
                dve.wait_ge(table_ready, 1)
                dve.wait_ge(prob_copied, 1)

            @block.tensor
            def _(pe):
                pe.wait_ge(router_loaded, 16)

                def turn(g):
                    pe.wait_ge(xn_ready, 2 * g + 2)
                    if g >= 2:
                        pe.wait_ge(xt_copied, g - 1)
                    for t in range(2):
                        for c in range(DC):
                            last = nc.tensor.transpose(ps_t[:, g % 2, (t * DC + c) * P:(t * DC + c + 1) * P], xn[:, 2 * g + t, c * P:c * P + P], ident[:, :])
                    last.then_inc(xt_ready, 1)

                turn(0)
                for g in range(NT // 2):
                    if g + 1 < NT // 2:
                        turn(g + 1)
                    pe.wait_ge(xt_copied, g + 1)
                    for t in range(2):
                        for c in range(DC):
                            last = nc.tensor.matmul(ps_l[:, (2 * g + t) * E1:(2 * g + t + 1) * E1], xt[:, g % 2, (t * DC + c) * P:(t * DC + c + 1) * P],
                                                    router[:, c, :], start=c == 0, stop=c == DC - 1)
                    last.then_inc(logits, 1)
                pe.wait_ge(is_own_bf, 1)
                nc.tensor.matmul(ps_n[:, 0:NT * E1], upper_bf[:, :], onehot_bf[:, :, :].rearrange("p t e -> p (t e)"), start=True, stop=False, skip_group_check=True)
                for t in range(NT):
                    last = nc.tensor.matmul(ps_n[:, (t + 1) * E1:].rearrange("p (n e) -> p n e", e=E1), ones_bf[:, :],
                                            onehot_bf[:, t:t + 1, :].to_broadcast([P, NT - t, E1]), start=False, stop=t == NT - 1, skip_group_check=True)
                last.then_inc(counted, 1)

            @block.scalar
            def _(act):
                for g in range(NT // 2):
                    act.wait_ge(xt_ready, g + 1)
                    if g >= 2:
                        act.wait_ge(logits, g - 1)
                    nc.scalar.activation(xt[:, g % 2, :], ps_t[:, g % 2, :], ACT.Copy).then_inc(xt_copied, 1)
                act.wait_ge(logits, NT // 2)
                nc.scalar.activation(score[:, :, :], ps_l[:, :].rearrange("p (t e) -> p t e", t=NT), ACT.Sigmoid).then_inc(scored, 1)

            @block.gpsimd
            def _(pool):
                for part in range(NORM_PARTS):
                    norm_rstd(nc, pool, mean_var, rstd, half, norm, part)
                pool.wait_ge(xn_ready, NT)
                pool.wait_ge(place_ready, 1)
                for t in range(NT):
                    nc.gpsimd.indirect_dma_start(sorted_dram, bass.IndirectOffsetOnAxis(ap=place[:, t:t + 1], axis=0), xn[:, t, :], None).then_inc(scattered, 16)
                pool.wait_ge(scattered, 16 * NT)


def moe_slots(nc, x_sb, weights, sorted_dram, y_dram, out_dram, ident, place, expert_of, max_prob, w_loaded):
    gate_w, up_w, down_w = weights
    with ExitStack() as ctx:
        sb, psum, sem = scope(ctx, nc)
        xs = sb("xs7", [P, 2, D])
        xt = sb("xt7", [P, 2, DC, P])
        sig = sb("sig7", [P, H1])
        silu = sb("silu7", [P, H1])
        hid = sb("hid7", [P, H1])
        ht = sb("ht7", [P, HC1, P])
        y = sb("y7", [P, 2, D])
        back = sb("back7", [P, NT, D])
        ps_x = psum("ps_x7", [P, 512])
        ps_g = psum("ps_g7", [P, 512])
        ps_u = psum("ps_u7", [P, 512])
        ps_h = psum("ps_h7", [P, 512])
        ps_y = psum("ps_y7", [P, 2, 512])

        xs_loaded = [sem(f"xs7_loaded{j}") for j in range(2)]
        y_written = [sem(f"y7_written{j}") for j in range(2)]
        io_begun = sem("io7_begun")
        xt_ready, xt_copied, gate_done, up_done = sem("xt7s"), sem("xt7_copied"), sem("gate7"), sem("up7")
        sig_ready, silu_ready, hid_ready, ht_ready, ht_copied = sem("sig7s"), sem("silu7s"), sem("hid7s"), sem("ht7s"), sem("ht7_copied")
        y_done, y_copied = sem("y7s"), sem("y7_copied")
        returned = [sem(f"returned7_{q}") for q in range(4)]
        x_added, out_written = sem("x7_added"), sem("out_written")
        Q = NT // 4
        PAIRS = (ESLOTS - 3) // 2

        def all_slots(engine, step):
            for s in range(2):
                step(s, s)
            with engine.Fori(1, PAIRS) as i:
                for j in range(2):
                    step(i * 2 + j, j)
            for s in range(2 * PAIRS, ESLOTS):
                step(s, s % 2)

        def exists(s):
            return not isinstance(s, int) or s < ESLOTS

        with nc.Block() as block:
            @block.sync
            def _(sp):
                def load(s, j, n):
                    if positive(n):
                        sp.wait_ge(xt_ready, s - 1)
                        sp.sem_inc(io_begun, 1)
                    sp.dma_start(xs[:, j, :], sorted_dram[bass.ds(s * P, P), :]).then_inc(xs_loaded[j], 16)

                def step(s, j):
                    if exists(s + 3):
                        load(s + 3, 1 - j, 1)
                    sp.wait_ge(y_copied, s + 1)
                    sp.sem_inc(io_begun, 1)
                    sp.dma_start(y_dram[bass.ds(s * P, P), :], y[:, j, :]).then_inc(y_written[j], 16)

                load(0, 0, 0)
                load(1, 1, 0)
                load(2, 0, 1)
                all_slots(sp, step)
                for q in range(4):
                    sp.wait_ge(x_added, (q + 1) * Q)
                    sp.dma_start(out_dram[:, q * Q:(q + 1) * Q, :], x_sb[:, q * Q:(q + 1) * Q, :]).then_inc(out_written, 16)
                sp.wait_ge(out_written, 16 * 4)

            @block.tensor
            def _(pe):
                def turn_x(s, j):
                    pe.wait_ge(xs_loaded[j], 16 * (s // 2 + 1))
                    if positive(s):
                        pe.wait_ge(xt_copied, s)
                    for c in range(DC):
                        last = nc.tensor.transpose(ps_x[:, c * P:c * P + P], xs[:, j, c * P:c * P + P], ident[:, :])
                    last.then_inc(xt_ready, 1)

                def expert(s):
                    return pe.value_load(expert_of[0:1, bass.ds(s, 1)], min_val=0, max_val=E1 - 1)

                def hidden(s, j, e):
                    pe.wait_ge(xt_copied, s + 1)
                    if positive(s):
                        pe.wait_ge(hid_ready, s)
                    for ps, w, done in ((ps_g, gate_w, gate_done), (ps_u, up_w, up_done)):
                        for c in range(DC):
                            last = nc.tensor.matmul(ps[:, :], xt[:, j, c, :], w[:, bass.ds(e, 1), c, :].rearrange("p a n -> p (a n)"),
                                                    start=c == 0, stop=c == DC - 1)
                        last.then_inc(done, 1)

                def turn_h(s):
                    pe.wait_ge(hid_ready, s + 1)
                    if positive(s):
                        pe.wait_ge(ht_copied, s)
                    for c in range(HC1):
                        last = nc.tensor.transpose(ps_h[:, c * P:c * P + P], hid[:, c * P:c * P + P], ident[:, :])
                    last.then_inc(ht_ready, 1)

                def output(s, j, e):
                    pe.wait_ge(ht_copied, s + 1)
                    if positive(s - 1):
                        pe.wait_ge(y_copied, s - 1)
                    for c in range(HC1):
                        last = nc.tensor.matmul(ps_y[:, j, 0:D], ht[:, c, :], down_w[:, bass.ds(e, 1), c, :].rearrange("p a n -> p (a n)"),
                                                start=c == 0, stop=c == HC1 - 1)
                    last.then_inc(y_done, 1)

                def step(s, j):
                    e = expert(s)
                    if exists(s + 2):
                        e_ahead = expert(s + 2)
                        turn_x(s + 2, j)
                    output(s, j, e)
                    if exists(s + 1):
                        turn_h(s + 1)
                    if exists(s + 2):
                        hidden(s + 2, j, e_ahead)

                turn_x(0, 0)
                turn_x(1, 1)
                pe.wait_ge(w_loaded[0], w_loaded[1])
                hidden(0, 0, expert(0))
                turn_h(0)
                hidden(1, 1, expert(1))
                all_slots(pe, step)

            @block.scalar
            def _(act):
                def copy_x(s, j):
                    act.wait_ge(xt_ready, s + 1)
                    if positive(s - 1):
                        act.wait_ge(up_done, s - 1)
                    nc.scalar.activation(xt[:, j, :, :], ps_x[:, 0:D].rearrange("p (c n) -> p c n", c=DC), ACT.Copy).then_inc(xt_copied, 1)

                def squash(s):
                    act.wait_ge(gate_done, s + 1)
                    if positive(s):
                        act.wait_ge(silu_ready, s)
                    nc.scalar.activation(sig[:, :], ps_g[:, :], ACT.Sigmoid).then_inc(sig_ready, 1)

                def step(s, j):
                    if exists(s + 1):
                        squash(s + 1)
                    if exists(s + 2):
                        copy_x(s + 2, j)
                    act.wait_ge(y_done, s + 1)
                    if positive(s - 1):
                        act.wait_ge(y_written[j], 16 * (s // 2))
                        act.sem_inc(io_begun, 1)
                    nc.scalar.activation(y[:, j, :], ps_y[:, j, 0:D], ACT.Copy).then_inc(y_copied, 1)

                copy_x(0, 0)
                copy_x(1, 1)
                squash(0)
                all_slots(act, step)

            @block.vector
            def _(dve):
                def step(s, j):
                    dve.wait_ge(sig_ready, s + 1)
                    nc.vector.tensor_tensor(silu[:, :], ps_g[:, :], sig[:, :], ALU.mult).then_inc(silu_ready, 1)
                    dve.wait_ge(silu_ready, s + 1)
                    dve.wait_ge(up_done, s + 1)
                    if positive(s):
                        dve.wait_ge(ht_ready, s)
                    nc.vector.tensor_tensor(hid[:, :], ps_u[:, :], silu[:, :], ALU.mult).then_inc(hid_ready, 1)
                    dve.wait_ge(ht_ready, s + 1)
                    if positive(s):
                        dve.wait_ge(y_done, s)
                    nc.vector.tensor_copy(ht[:, :, :], ps_h[:, :].rearrange("p (c n) -> p c n", c=HC1)).then_inc(ht_copied, 1)

                all_slots(dve, step)
                for t in range(NT):
                    dve.wait_ge(returned[t // Q], 16 * Q)
                    nc.vector.scalar_tensor_tensor(x_sb[:, t, :], back[:, t, :], max_prob[:, t:t + 1], x_sb[:, t, :], ALU.mult, ALU.add).then_inc(x_added, 1)

            @block.gpsimd
            def _(pool):
                for j in range(2):
                    pool.wait_ge(y_written[j], 16 * ((ESLOTS + 1 - j) // 2))
                for t in range(NT):
                    nc.gpsimd.indirect_dma_start(back[:, t, :], None, y_dram, bass.IndirectOffsetOnAxis(ap=place[:, t:t + 1], axis=0)).then_inc(returned[t // Q], 16)
def program(nc, x_dram, ctx_dram, ctx_t_dram, mask_dram, wq, wk, wv, wo, wk_ctx, wv_ctx, q_norm_w, k_norm_w,
            gate, expert_bias, w1, w3, w2, sw1, sw3, sw2, router_w, gate_w, up_w, down_w,
            ident_dram, iota_dram, upper_dram, causal_dram, rope_dram, out_dram):
    q_dram = nc.dram_tensor("q_scratch", (BG, P, GRP, L), F32).ap()
    k_dram = nc.dram_tensor("k_scratch", (BG, P, NK), F32).ap()
    v_dram = nc.dram_tensor("v_scratch", (BG, P, KB, HD), F32).ap()
    sorted_dram = nc.dram_tensor("sorted_scratch", (ESLOTS * P, D), F32).ap()
    y_dram = nc.dram_tensor("y_scratch", (ESLOTS * P, D), F32).ap()
    with ExitStack() as ctx:
        sb, _, sem = scope(ctx, nc)
        x_sb = sb("x_sb", [P, NT, D])
        ident = sb("ident", [P, P])
        ident_bf = sb("ident_bf", [P, P], BF16)
        iota = sb("iota", [P, P])
        upper_bf = sb("upper_bf", [P, P], BF16)
        ones_bf = sb("ones_bf", [P, P], BF16)
        causal_bf = sb("causal_bf", [P, P], BF16)
        half = sb("half", [P, 64])
        mean_var = sb("mean_var", [P, NT, 2])
        rstd = sb("rstd", [P, NT])
        upper = sb("upper", [P, P])
        causal = sb("causal", [P, P])
        ident_loaded, x_loaded, consts_loaded, half_made, made = sem("ident_loaded"), sem("x_loaded"), sem("consts_loaded"), sem("half_made"), sem("consts_made")
        with nc.Block() as block:
            @block.sync
            def _(sp):
                sp.dma_start(ident[:, :], ident_dram).then_inc(ident_loaded, 16)
                sp.dma_start(x_sb[:, :, :], x_dram.rearrange("b (t p) d -> p (b t) d", p=P)).then_inc(x_loaded, 16)
                for dst, src in ((iota, iota_dram), (upper, upper_dram), (causal, causal_dram)):
                    sp.dma_start(dst[:, :], src).then_inc(consts_loaded, 16)

            @block.vector
            def _(dve):
                nc.vector.memset(half[:, :], -0.5).then_inc(half_made, 1)

        self_projections(nc, x_sb, x_loaded, ident_loaded, half_made, (wq, wk, wv), rope_dram, q_norm_w, k_norm_w, q_dram, k_dram, v_dram, mean_var, rstd, half, ident)
        with nc.Block() as block:
            @block.vector
            def _(dve):
                nc.vector.memset(ones_bf[:, :], 1.0).then_inc(made, 1)
                dve.wait_ge(consts_loaded, 48)
                dve.wait_ge(ident_loaded, 16)
                for dst, src in ((ident_bf, ident), (upper_bf, upper), (causal_bf, causal)):
                    nc.vector.tensor_copy(dst[:, :], src[:, :]).then_inc(made, 1)
                dve.wait_ge(made, 4)

        with ExitStack() as attention_ctx:
            operands = attention_operands(attention_ctx, nc)
            context_projections(nc, ctx_t_dram, wk_ctx, wv_ctx, k_norm_w, q_dram, k_dram, v_dram, half, ident, operands)
            attention(nc, q_dram, k_dram, v_dram, wo, x_sb, ident, ident_bf, causal_bf, operands)

        moe_two_of_eight(nc, x_sb, gate, expert_bias, w1, w3, w2, sw1, sw3, sw2, mean_var, rstd, half, ident, ident_bf, iota, sorted_dram)

        memory_attention(nc, x_sb, ctx_t_dram, ctx_dram, mask_dram, mean_var, rstd, half, ident)

        gate_sb = sb("gate_w", [P, E1, DC, H1])
        up_sb = sb("up_w", [P, E1, DC, H1])
        down_sb = sb("down_w", [P, E1, HC1, D])
        place = sb("place", [P, NT], U32)
        expert_of = sb("expert_of", [P, ESLOTS], U32)
        max_prob = sb("max_prob", [P, NT])
        w_loaded = sem("w6_loaded")
        route_to_slots(nc, x_sb, router_w, (gate_w, up_w, down_w), (gate_sb, up_sb, down_sb), w_loaded, sorted_dram, mean_var, rstd, half, ident, upper_bf, ones_bf, iota, place, expert_of, max_prob)
        moe_slots(nc, x_sb, (gate_sb, up_sb, down_sb), sorted_dram, y_dram, out_dram.rearrange("b (t p) d -> p (b t) d", p=P),
                  ident, place, expert_of, max_prob, (w_loaded, 3 * 16))


def kernel(x, ctx_2048, mask_BxS2_bk0, L0_xattn_wq, L0_xattn_wk, L0_xattn_wv, L0_xattn_wo, L0_xattn_wk_ctx, L0_xattn_wv_ctx,
           L0_xattn_q_norm_w, L0_xattn_k_norm_w, L0_ffn_gate, L0_ffn_expert_bias, L0_ffn_w1, L0_ffn_w2, L0_ffn_w3,
           L0_ffn_shared_w1, L0_ffn_shared_w2, L0_ffn_shared_w3, L1_ffn_router_w, L1_ffn_gate_w, L1_ffn_up_w, L1_ffn_down_w):
    import numpy as np
    import concourse.bacc as bacc
    from concourse.bass_utils import run_bass_kernel_spmd

    context = np.zeros((B, TP, D), np.float32)
    context[:, :T] = np.asarray(ctx_2048)
    context_t = context.reshape(B * CT, P, DC, P).transpose(0, 3, 2, 1)
    inv_freq = np.float32(1) / np.float32(10000) ** (np.arange(0, HD, 2, dtype=np.float32) / np.float32(HD))
    angle = np.outer(np.arange(L, dtype=np.float32), inv_freq)
    rope = np.stack([np.concatenate([np.cos(angle), np.cos(angle)], 1), np.concatenate([-np.sin(angle), np.sin(angle)], 1)])
    arrays = [
        ("x", x), ("ctx", context), ("ctx_t", context_t), ("mask", mask_BxS2_bk0),
        ("wq", L0_xattn_wq), ("wk", L0_xattn_wk), ("wv", L0_xattn_wv), ("wo", L0_xattn_wo),
        ("wk_ctx", L0_xattn_wk_ctx), ("wv_ctx", L0_xattn_wv_ctx), ("q_norm_w", L0_xattn_q_norm_w), ("k_norm_w", L0_xattn_k_norm_w),
        ("gate", np.asarray(L0_ffn_gate).T), ("expert_bias", L0_ffn_expert_bias),
        ("w1", np.asarray(L0_ffn_w1).transpose(0, 2, 1)), ("w3", np.asarray(L0_ffn_w3).transpose(0, 2, 1)),
        ("w2", np.asarray(L0_ffn_w2).transpose(0, 2, 1)), ("sw1", np.asarray(L0_ffn_shared_w1).T),
        ("sw3", np.asarray(L0_ffn_shared_w3).T), ("sw2", np.asarray(L0_ffn_shared_w2).T),
        ("router_w", L1_ffn_router_w), ("gate_w", L1_ffn_gate_w), ("up_w", L1_ffn_up_w), ("down_w", L1_ffn_down_w),
        ("ident", np.eye(P, dtype=np.float32)), ("iota", np.tile(np.arange(P, dtype=np.float32), (P, 1))),
        ("upper", np.triu(np.ones((P, P), np.float32), 1)), ("causal", np.triu(np.full((P, P), NEG, np.float32), 1)),
        ("rope", rope.astype(np.float32))]
    nc = bacc.Bacc("TRN2", target_bir_lowering=False, num_devices=1)
    inputs, aps = {}, []
    for name, a in arrays:
        a = np.ascontiguousarray(a)
        inputs["in_" + name] = a
        aps.append(nc.dram_tensor("in_" + name, a.shape, mybir.dt.from_np(a.dtype), kind="ExternalInput").ap())
    out = nc.dram_tensor("out", (B, L, D), F32, kind="ExternalOutput").ap()
    program(nc, *aps, out)
    return run_bass_kernel_spmd(nc, [inputs], core_ids=[0]).results[0]["out"]
```
